# Optimizing a Trainium2 kernel written in Bass

```python
import numpy as np
import jax
import jax.numpy as jnp

def _softmax(x, axis=-1):
    return jax.nn.softmax(x, axis=axis)

def _gelu(x):
    return jax.nn.gelu(x, approximate=True)

def _silu(x):
    return jax.nn.silu(x)

def _sigmoid(x):
    return jax.nn.sigmoid(x)

def _layernorm(x, axis=-1, eps=1e-05):
    m = jnp.mean(x, axis=axis, keepdims=True)
    v = jnp.var(x, axis=axis, keepdims=True)
    return (x - m) / jnp.sqrt(v + eps)

def _scatter_add(tgt, idx, src, axis=0):
    return tgt.at[idx].add(src)

def _segment_sum(src, seg, n):
    return jax.ops.segment_sum(src, seg, n)
kernel_name = 'mk_adaln_d2_jaxref_r8_f47d68'

def setup_inputs(seed: int=0):
    np.random.seed(seed)
    _w = jnp.asarray

    def _L0_attn_setup():
        import jax, jax.numpy as jnp
        import numpy as np
        D_MODEL = 128
        D_STATE = 16
        D_CONV = 4
        EXPAND = 2
        D_INNER = EXPAND * D_MODEL
        DT_RANK = D_MODEL // 16
        BATCH = 2
        SEQ = 256

        def _mamba_block(u, m_in_w, conv_w, conv_b, xproj_w, dt_w, dt_b, A_log, Dp, m_out_w):
            xz = u @ m_in_w.T
            xc, z = jnp.split(xz, 2, axis=-1)
            xt = jax.lax.conv_general_dilated(xc.transpose(0, 2, 1), conv_w, (1,), [(D_CONV - 1, 0)], dimension_numbers=('NCH', 'OIH', 'NCH'), feature_group_count=D_INNER)
            xc = jax.nn.silu(xt.transpose(0, 2, 1) + conv_b)
            x_dbl = xc @ xproj_w.T
            dt = jax.nn.softplus(x_dbl[..., :DT_RANK] @ dt_w.T + dt_b)
            Bm = x_dbl[..., DT_RANK:DT_RANK + D_STATE]
            Cm = x_dbl[..., DT_RANK + D_STATE:]
            A = -jnp.exp(A_log)

            def step(h, inp):
                dt_i, B_i, C_i, u_i = inp
                dA = jnp.exp(dt_i[:, :, None] * A)
                h = dA * h + dt_i[:, :, None] * B_i[:, None, :] * u_i[:, :, None]
                y = jnp.einsum('bds,bs->bd', h, C_i)
                return (h, y)
            h0 = jnp.zeros((u.shape[0], D_INNER, D_STATE), u.dtype)
            xs = (dt.transpose(1, 0, 2), Bm.transpose(1, 0, 2), Cm.transpose(1, 0, 2), xc.transpose(1, 0, 2))
            _, ys = jax.lax.scan(step, h0, xs)
            y = ys.transpose(1, 0, 2) + xc * Dp
            y = y * jax.nn.silu(z)
            return y @ m_out_w.T
        key = jax.random.key(seed)
        ks = jax.random.split(key, 12)
        s = 0.02
        x = jax.random.normal(ks[0], (BATCH, SEQ, D_MODEL), jnp.float32)
        w_in = jax.random.normal(ks[1], (2 * D_MODEL, D_MODEL), jnp.float32) * s
        b_in = jnp.zeros((2 * D_MODEL,), jnp.float32)
        w_out = jax.random.normal(ks[2], (D_MODEL, D_MODEL), jnp.float32) * s
        b_out = jnp.zeros((D_MODEL,), jnp.float32)
        m_in_w = jax.random.normal(ks[3], (2 * D_INNER, D_MODEL), jnp.float32) * s
        conv_w = jax.random.normal(ks[4], (D_INNER, 1, D_CONV), jnp.float32) * s
        conv_b = jnp.zeros((D_INNER,), jnp.float32)
        xproj_w = jax.random.normal(ks[5], (DT_RANK + 2 * D_STATE, D_INNER), jnp.float32) * s
        dt_w = jax.random.normal(ks[6], (D_INNER, DT_RANK), jnp.float32) * s
        dt_b = jax.random.normal(ks[7], (D_INNER,), jnp.float32) * s
        A_log = jnp.log(jnp.tile(jnp.arange(1, D_STATE + 1, dtype=jnp.float32), (D_INNER, 1)))
        Dp = jnp.ones((D_INNER,), jnp.float32)
        m_out_w = jax.random.normal(ks[8], (D_MODEL, D_INNER), jnp.float32) * s
        return {'x': x, 'w_in': w_in, 'b_in': b_in, 'w_out': w_out, 'b_out': b_out, 'm_in_w': m_in_w, 'conv_w': conv_w, 'conv_b': conv_b, 'xproj_w': xproj_w, 'dt_w': dt_w, 'dt_b': dt_b, 'A_log': A_log, 'Dp': Dp, 'm_out_w': m_out_w}
    _L0_attn_in = _L0_attn_setup()

    def _L0_ffn_setup():
        import jax, jax.numpy as jnp
        import numpy as np
        CAPACITY_FACTOR = 1.25
        key = jax.random.key(seed)
        k1, k2, k3, k4 = jax.random.split(key, 4)
        B, T, D, F, E = (4, 512, 128, 512, 8)
        s = 0.02
        return {'x': jax.random.normal(k1, (B, T, D), dtype=jnp.float32), 'wg': jax.random.normal(k2, (D, E), dtype=jnp.float32) * s, 'W1': jax.random.normal(k3, (E, D, F), dtype=jnp.float32) * s, 'b1': jnp.zeros((E, F), dtype=jnp.float32), 'W2': jax.random.normal(k4, (E, F, D), dtype=jnp.float32) * s, 'b2': jnp.zeros((E, D), dtype=jnp.float32)}
    _L0_ffn_in = _L0_ffn_setup()
    _L0_c = _w((lambda *s: np.random.randn(*s).astype(np.float32) * 0.05)(8, 128))
    _L0_wmod = _w((lambda *s: np.random.randn(*s).astype(np.float32) * 0.05)(128, 6 * 128) * 128 ** (-0.5))

    def _L1_attn_setup():
        import jax, jax.numpy as jnp
        import numpy as np
        D_MODEL = 128
        NUM_HEADS = 16
        D_K = D_MODEL // NUM_HEADS
        THETA = 10000.0

        def _rope(x, positions):
            d = x.shape[-1]
            inv_freq = THETA ** (-jnp.arange(0, d, 2, dtype=jnp.float32) / d)
            ang = positions[:, :, None].astype(jnp.float32) * inv_freq[None, None, :]
            cos = jnp.cos(ang)[:, None, :, :]
            sin = jnp.sin(ang)[:, None, :, :]
            x1 = x[..., 0::2]
            x2 = x[..., 1::2]
            r1 = x1 * cos - x2 * sin
            r2 = x1 * sin + x2 * cos
            out = jnp.stack([r1, r2], axis=-1).reshape(x.shape)
            return out
        key = jax.random.key(seed)
        k1, k2, k3 = jax.random.split(key, 3)
        B, S = (4, 256)
        x = jax.random.normal(k1, (B, S, D_MODEL), dtype=jnp.float32)
        W_qkv = jax.random.normal(k2, (3 * D_MODEL, D_MODEL), dtype=jnp.float32) * (1.0 / np.sqrt(D_MODEL))
        W_o = jax.random.normal(k3, (D_MODEL, D_MODEL), dtype=jnp.float32) * (1.0 / np.sqrt(D_MODEL))
        return {'x': x, 'W_qkv': W_qkv, 'W_o': W_o}
    _L1_attn_in = _L1_attn_setup()

    def _L1_ffn_setup():
        import jax, jax.numpy as jnp
        import numpy as np
        B, S, H = (1, 256, 128)
        E, K = (16, 4)
        G, TG = (4, 2)
        I_MOE = 64
        N_SH = 2
        SCALE = 2.5

        def _mlp(x, gw, uw, dw):
            return jax.nn.silu(x @ gw.T) * (x @ uw.T) @ dw.T

        def _route(x2d, router_weight, e_bias):
            T = x2d.shape[0]
            scores = jax.nn.sigmoid(x2d @ router_weight.T)
            sc = scores + e_bias[None, :]
            group_scores = jnp.sum(jax.lax.top_k(sc.reshape(T, G, E // G), 2)[0], axis=-1)
            _, gidx = jax.lax.top_k(group_scores, TG)
            gmask = jnp.zeros((T, G), sc.dtype).at[jnp.arange(T)[:, None], gidx].set(1.0)
            smask = jnp.repeat(gmask, E // G, axis=1)
            masked = jnp.where(smask > 0, sc, 0.0)
            _, tidx = jax.lax.top_k(masked, K)
            tw = jnp.take_along_axis(scores, tidx, axis=1)
            tw = tw / (jnp.sum(tw, axis=-1, keepdims=True) + 1e-20)
            tw = tw * SCALE
            return (tidx, tw)

        def _moe_forward(hidden_states, router_weight, e_bias, gate_w, up_w, down_w, sh_gate_w, sh_up_w, sh_down_w):
            orig_shape = hidden_states.shape
            x = hidden_states.reshape(-1, H)
            T = x.shape[0]
            tidx, tw = _route(x, router_weight, e_bias)
            g = jnp.einsum('th,eih->tei', x, gate_w)
            u = jnp.einsum('th,eih->tei', x, up_w)
            h = jax.nn.silu(g) * u
            yo = jnp.einsum('tei,ehi->teh', h, down_w)
            combine = jnp.zeros((T, E), tw.dtype).at[jnp.arange(T)[:, None], tidx].add(tw)
            routed = jnp.einsum('te,teh->th', combine, yo)
            shared = _mlp(hidden_states.reshape(-1, H), sh_gate_w, sh_up_w, sh_down_w)
            return (routed + shared).reshape(orig_shape)
        key = jax.random.key(seed)
        ks = jax.random.split(key, 9)
        s = 0.02
        return {'hidden_states': jax.random.normal(ks[0], (B, S, H), jnp.float32), 'router_weight': jax.random.normal(ks[1], (E, H), jnp.float32) * s, 'e_bias': jnp.zeros((E,), jnp.float32), 'gate_w': jax.random.normal(ks[2], (E, I_MOE, H), jnp.float32) * s, 'up_w': jax.random.normal(ks[3], (E, I_MOE, H), jnp.float32) * s, 'down_w': jax.random.normal(ks[4], (E, H, I_MOE), jnp.float32) * s, 'sh_gate_w': jax.random.normal(ks[5], (N_SH * I_MOE, H), jnp.float32) * s, 'sh_up_w': jax.random.normal(ks[6], (N_SH * I_MOE, H), jnp.float32) * s, 'sh_down_w': jax.random.normal(ks[7], (H, N_SH * I_MOE), jnp.float32) * s}
    _L1_ffn_in = _L1_ffn_setup()
    _L1_c = _w((lambda *s: np.random.randn(*s).astype(np.float32) * 0.05)(8, 128))
    _L1_wmod = _w((lambda *s: np.random.randn(*s).astype(np.float32) * 0.05)(128, 6 * 128) * 128 ** (-0.5))
    _d = {'L0_attn_x': _L0_attn_in['x'], 'L0_attn_w_in': _L0_attn_in['w_in'], 'L0_attn_b_in': _L0_attn_in['b_in'], 'L0_attn_w_out': _L0_attn_in['w_out'], 'L0_attn_b_out': _L0_attn_in['b_out'], 'L0_attn_m_in_w': _L0_attn_in['m_in_w'], 'L0_attn_conv_w': _L0_attn_in['conv_w'], 'L0_attn_conv_b': _L0_attn_in['conv_b'], 'L0_attn_xproj_w': _L0_attn_in['xproj_w'], 'L0_attn_dt_w': _L0_attn_in['dt_w'], 'L0_attn_dt_b': _L0_attn_in['dt_b'], 'L0_attn_A_log': _L0_attn_in['A_log'], 'L0_attn_Dp': _L0_attn_in['Dp'], 'L0_attn_m_out_w': _L0_attn_in['m_out_w'], 'L0_ffn_wg': _L0_ffn_in['wg'], 'L0_ffn_W1': _L0_ffn_in['W1'], 'L0_ffn_b1': _L0_ffn_in['b1'], 'L0_ffn_W2': _L0_ffn_in['W2'], 'L0_ffn_b2': _L0_ffn_in['b2'], 'L0_c': _L0_c, 'L0_wmod': _L0_wmod, 'L1_attn_W_qkv': _L1_attn_in['W_qkv'], 'L1_attn_W_o': _L1_attn_in['W_o'], 'L1_ffn_router_weight': _L1_ffn_in['router_weight'], 'L1_ffn_e_bias': _L1_ffn_in['e_bias'], 'L1_ffn_gate_w': _L1_ffn_in['gate_w'], 'L1_ffn_up_w': _L1_ffn_in['up_w'], 'L1_ffn_down_w': _L1_ffn_in['down_w'], 'L1_ffn_sh_gate_w': _L1_ffn_in['sh_gate_w'], 'L1_ffn_sh_up_w': _L1_ffn_in['sh_up_w'], 'L1_ffn_sh_down_w': _L1_ffn_in['sh_down_w'], 'L1_c': _L1_c, 'L1_wmod': _L1_wmod}
    _x0 = _d['L0_attn_x']
    _d['L0_attn_x'] = jax.random.normal(jax.random.fold_in(jax.random.key(seed), 1), (8, 512, 128), dtype=_x0.dtype)
    del _x0
    return _d

def reference(L0_attn_x, L0_attn_w_in, L0_attn_b_in, L0_attn_w_out, L0_attn_b_out, L0_attn_m_in_w, L0_attn_conv_w, L0_attn_conv_b, L0_attn_xproj_w, L0_attn_dt_w, L0_attn_dt_b, L0_attn_A_log, L0_attn_Dp, L0_attn_m_out_w, L0_ffn_wg, L0_ffn_W1, L0_ffn_b1, L0_ffn_W2, L0_ffn_b2, L0_c, L0_wmod, L1_attn_W_qkv, L1_attn_W_o, L1_ffn_router_weight, L1_ffn_e_bias, L1_ffn_gate_w, L1_ffn_up_w, L1_ffn_down_w, L1_ffn_sh_gate_w, L1_ffn_sh_up_w, L1_ffn_sh_down_w, L1_c, L1_wmod):

    def _L0_attn_ref(x, w_in, b_in, w_out, b_out, m_in_w, conv_w, conv_b, xproj_w, dt_w, dt_b, A_log, Dp, m_out_w):
        import jax, jax.numpy as jnp
        import numpy as np
        D_MODEL = 128
        D_STATE = 16
        D_CONV = 4
        EXPAND = 2
        D_INNER = EXPAND * D_MODEL
        DT_RANK = D_MODEL // 16
        BATCH = 2
        SEQ = 256

        def _mamba_block(u, m_in_w, conv_w, conv_b, xproj_w, dt_w, dt_b, A_log, Dp, m_out_w):
            xz = u @ m_in_w.T
            xc, z = jnp.split(xz, 2, axis=-1)
            xt = jax.lax.conv_general_dilated(xc.transpose(0, 2, 1), conv_w, (1,), [(D_CONV - 1, 0)], dimension_numbers=('NCH', 'OIH', 'NCH'), feature_group_count=D_INNER)
            xc = jax.nn.silu(xt.transpose(0, 2, 1) + conv_b)
            x_dbl = xc @ xproj_w.T
            dt = jax.nn.softplus(x_dbl[..., :DT_RANK] @ dt_w.T + dt_b)
            Bm = x_dbl[..., DT_RANK:DT_RANK + D_STATE]
            Cm = x_dbl[..., DT_RANK + D_STATE:]
            A = -jnp.exp(A_log)

            def step(h, inp):
                dt_i, B_i, C_i, u_i = inp
                dA = jnp.exp(dt_i[:, :, None] * A)
                h = dA * h + dt_i[:, :, None] * B_i[:, None, :] * u_i[:, :, None]
                y = jnp.einsum('bds,bs->bd', h, C_i)
                return (h, y)
            h0 = jnp.zeros((u.shape[0], D_INNER, D_STATE), u.dtype)
            xs = (dt.transpose(1, 0, 2), Bm.transpose(1, 0, 2), Cm.transpose(1, 0, 2), xc.transpose(1, 0, 2))
            _, ys = jax.lax.scan(step, h0, xs)
            y = ys.transpose(1, 0, 2) + xc * Dp
            y = y * jax.nn.silu(z)
            return y @ m_out_w.T
        xp = x @ w_in.T + b_in
        x_f, x_b = jnp.split(xp, 2, axis=-1)
        mb = lambda u: _mamba_block(u, m_in_w, conv_w, conv_b, xproj_w, dt_w, dt_b, A_log, Dp, m_out_w)
        out_f = mb(x_f)
        out_b = jnp.flip(mb(jnp.flip(x_b, axis=1)), axis=1)
        return (out_f + out_b) @ w_out.T + b_out

    def _L0_ffn_ref(x, wg, W1, b1, W2, b2):
        import jax, jax.numpy as jnp
        import numpy as np
        CAPACITY_FACTOR = 1.25
        B, T, D = x.shape
        E = wg.shape[1]
        N = B * T
        capacity = int(N / E * CAPACITY_FACTOR) + 1
        xf = x.reshape(N, D)
        logits = xf @ wg
        scores = jax.nn.softmax(logits, axis=-1)
        top1 = jnp.argmax(scores, axis=-1)
        combine_w = jnp.take_along_axis(scores, top1[:, None], axis=1)[:, 0]
        oh = jax.nn.one_hot(top1, E, dtype=jnp.int32)
        rank = jnp.take_along_axis(jnp.cumsum(oh, axis=0), top1[:, None], axis=1)[:, 0] - 1
        valid = rank < capacity
        trash = E * capacity
        slot = jnp.where(valid, top1 * capacity + rank, trash)
        buf = jnp.zeros((E * capacity + 1, D), dtype=x.dtype).at[slot].set(xf)
        eb = buf[:E * capacity].reshape(E, capacity, D)
        h = jax.nn.gelu(jnp.einsum('ecd,edf->ecf', eb, W1) + b1[:, None, :], approximate=False)
        y = jnp.einsum('ecf,efd->ecd', h, W2) + b2[:, None, :]
        yf = y.reshape(E * capacity, D)
        gathered = yf[jnp.minimum(slot, E * capacity - 1)]
        out_flat = jnp.where(valid[:, None], gathered, 0.0) * combine_w[:, None]
        return out_flat.reshape(B, T, D)

    def _L1_attn_ref(x, W_qkv, W_o):
        import jax, jax.numpy as jnp
        import numpy as np
        D_MODEL = 128
        NUM_HEADS = 16
        D_K = D_MODEL // NUM_HEADS
        THETA = 10000.0

        def _rope(x, positions):
            d = x.shape[-1]
            inv_freq = THETA ** (-jnp.arange(0, d, 2, dtype=jnp.float32) / d)
            ang = positions[:, :, None].astype(jnp.float32) * inv_freq[None, None, :]
            cos = jnp.cos(ang)[:, None, :, :]
            sin = jnp.sin(ang)[:, None, :, :]
            x1 = x[..., 0::2]
            x2 = x[..., 1::2]
            r1 = x1 * cos - x2 * sin
            r2 = x1 * sin + x2 * cos
            out = jnp.stack([r1, r2], axis=-1).reshape(x.shape)
            return out
        B, S, _ = x.shape
        H, dk = (NUM_HEADS, D_K)
        qkv = jnp.einsum('bsd,ed->bse', x, W_qkv)
        qkv = qkv.reshape(B, S, 3, H, dk).transpose(2, 0, 3, 1, 4)
        q, k, v = (qkv[0], qkv[1], qkv[2])
        positions = jnp.broadcast_to(jnp.arange(S)[None, :], (B, S))
        q = _rope(q, positions)
        k = _rope(k, positions)
        scores = jnp.einsum('bhqd,bhkd->bhqk', q, k) / jnp.sqrt(jnp.float32(dk))
        causal = jnp.tril(jnp.ones((S, S), dtype=bool))
        scores = jnp.where(causal[None, None, :, :], scores, -jnp.inf)
        attn = jax.nn.softmax(scores, axis=-1)
        out = jnp.einsum('bhqk,bhkd->bhqd', attn, v)
        out = out.transpose(0, 2, 1, 3).reshape(B, S, H * dk)
        return jnp.einsum('bsd,ed->bse', out, W_o)

    def _L1_ffn_ref(hidden_states, router_weight, e_bias, gate_w, up_w, down_w, sh_gate_w, sh_up_w, sh_down_w):
        import jax, jax.numpy as jnp
        import numpy as np
        B, S, H = (1, 256, 128)
        E, K = (16, 4)
        G, TG = (4, 2)
        I_MOE = 64
        N_SH = 2
        SCALE = 2.5

        def _mlp(x, gw, uw, dw):
            return jax.nn.silu(x @ gw.T) * (x @ uw.T) @ dw.T

        def _route(x2d, router_weight, e_bias):
            T = x2d.shape[0]
            scores = jax.nn.sigmoid(x2d @ router_weight.T)
            sc = scores + e_bias[None, :]
            group_scores = jnp.sum(jax.lax.top_k(sc.reshape(T, G, E // G), 2)[0], axis=-1)
            _, gidx = jax.lax.top_k(group_scores, TG)
            gmask = jnp.zeros((T, G), sc.dtype).at[jnp.arange(T)[:, None], gidx].set(1.0)
            smask = jnp.repeat(gmask, E // G, axis=1)
            masked = jnp.where(smask > 0, sc, 0.0)
            _, tidx = jax.lax.top_k(masked, K)
            tw = jnp.take_along_axis(scores, tidx, axis=1)
            tw = tw / (jnp.sum(tw, axis=-1, keepdims=True) + 1e-20)
            tw = tw * SCALE
            return (tidx, tw)

        def _moe_forward(hidden_states, router_weight, e_bias, gate_w, up_w, down_w, sh_gate_w, sh_up_w, sh_down_w):
            orig_shape = hidden_states.shape
            x = hidden_states.reshape(-1, H)
            T = x.shape[0]
            tidx, tw = _route(x, router_weight, e_bias)
            g = jnp.einsum('th,eih->tei', x, gate_w)
            u = jnp.einsum('th,eih->tei', x, up_w)
            h = jax.nn.silu(g) * u
            yo = jnp.einsum('tei,ehi->teh', h, down_w)
            combine = jnp.zeros((T, E), tw.dtype).at[jnp.arange(T)[:, None], tidx].add(tw)
            routed = jnp.einsum('te,teh->th', combine, yo)
            shared = _mlp(hidden_states.reshape(-1, H), sh_gate_w, sh_up_w, sh_down_w)
            return (routed + shared).reshape(orig_shape)
        return _moe_forward(hidden_states, router_weight, e_bias, gate_w, up_w, down_w, sh_gate_w, sh_up_w, sh_down_w)
    x = L0_attn_x
    mod = (_silu(L0_c) @ L0_wmod).reshape(L0_c.shape[0], 6, 1, -1)
    sa, ca, ga, sb, cb, gb = (mod[:, 0], mod[:, 1], mod[:, 2], mod[:, 3], mod[:, 4], mod[:, 5])
    ga = (2 * (ga >= 0) - 1) * jnp.maximum(jnp.abs(ga), 0.25)
    gb = (2 * (gb >= 0) - 1) * jnp.maximum(jnp.abs(gb), 0.25)
    h = _layernorm(x, axis=-1) * (1 + ca) + sa
    x = x + ga * _L0_attn_ref(h, L0_attn_w_in, L0_attn_b_in, L0_attn_w_out, L0_attn_b_out, L0_attn_m_in_w, L0_attn_conv_w, L0_attn_conv_b, L0_attn_xproj_w, L0_attn_dt_w, L0_attn_dt_b, L0_attn_A_log, L0_attn_Dp, L0_attn_m_out_w)
    h = _layernorm(x, axis=-1) * (1 + cb) + sb
    x = x + gb * _L0_ffn_ref(h, L0_ffn_wg, L0_ffn_W1, L0_ffn_b1, L0_ffn_W2, L0_ffn_b2)
    mod = (_silu(L1_c) @ L1_wmod).reshape(L1_c.shape[0], 6, 1, -1)
    sa, ca, ga, sb, cb, gb = (mod[:, 0], mod[:, 1], mod[:, 2], mod[:, 3], mod[:, 4], mod[:, 5])
    ga = (2 * (ga >= 0) - 1) * jnp.maximum(jnp.abs(ga), 0.25)
    gb = (2 * (gb >= 0) - 1) * jnp.maximum(jnp.abs(gb), 0.25)
    h = _layernorm(x, axis=-1) * (1 + ca) + sa
    x = x + ga * _L1_attn_ref(h, L1_attn_W_qkv, L1_attn_W_o)
    h = _layernorm(x, axis=-1) * (1 + cb) + sb
    x = x + gb * _L1_ffn_ref(h, L1_ffn_router_weight, L1_ffn_e_bias, L1_ffn_gate_w, L1_ffn_up_w, L1_ffn_down_w, L1_ffn_sh_gate_w, L1_ffn_sh_up_w, L1_ffn_sh_down_w)
    return x

_drawn_inputs = setup_inputs


def setup_inputs(seed=0):
    import zlib

    import numpy as np

    out = dict(_drawn_inputs(seed))
    spreads = {'L0_attn_b_in': (0.0, 0.8),
     'L0_attn_b_out': (0.0, 2.0),
     'L0_attn_conv_b': (0.0, 0.8),
     'L0_attn_Dp': (1.0, 0.6),
     'L0_ffn_b1': (0.0, 2.0),
     'L0_ffn_b2': (0.0, 2.0),
     'L1_ffn_e_bias': (0.0, 2.0)}
    factors = {'L0_attn_w_in': 8.0,
     'L0_attn_w_out': 8.0,
     'L0_attn_m_in_w': 8.0,
     'L0_attn_conv_w': 8.0,
     'L0_attn_xproj_w': 8.0,
     'L0_attn_dt_w': 8.0,
     'L0_attn_dt_b': 8.0,
     'L0_attn_A_log': 8.0,
     'L0_attn_m_out_w': 8.0,
     'L0_ffn_wg': 58.365,
     'L0_ffn_W1': 64.0,
     'L0_ffn_W2': 56.626,
     'L1_ffn_router_weight': 62.128,
     'L1_ffn_gate_w': 47.969,
     'L1_ffn_up_w': 43.024,
     'L1_ffn_down_w': 43.366,
     'L1_ffn_sh_gate_w': 46.461,
     'L1_ffn_sh_up_w': 41.623,
     'L1_ffn_sh_down_w': 41.243,
     'L1_attn_W_qkv': 8.0,
     'L1_attn_W_o': 8.0,
     'L1_c': 3.667,
     'L1_wmod': 3.735}
    for name, (base, spread) in spreads.items():
        noise = np.random.default_rng([zlib.crc32(name.encode()), seed]).standard_normal(out[name].shape)
        drawn = base * np.exp(spread * noise) if base else spread * noise
        out[name] = jnp.asarray(drawn.astype(out[name].dtype))
    for name, factor in factors.items():
        out[name] = (out[name] * factor).astype(out[name].dtype)
    return out
```

```python
from contextlib import ExitStack

import concourse.bass as bass
from concourse import mybir

F32 = mybir.dt.float32
BF16 = mybir.dt.bfloat16
U32 = mybir.dt.uint32
ALU = mybir.AluOpType
ACT = mybir.ActivationFunctionType
AX = mybir.AxisListType
ds = bass.ds

P = 128
B = 8
T = 512
N = B * T
NT = N // P
NCH = 2
NS = 16
KC = 4
PAD = KC - 1
RANK = 8
UNITS = 2 * B
XW = T + PAD
EPS = 1e-5

PACK1 = dict(ident=P, center=P, mean=P, eps=1, pick=32, c0=B, c1=B, wmod0=6 * P, wmod1=6 * P,
             w_in=2 * P, b_in=2, conv_b=NCH, m_in=2 * NCH * P, conv_w=KC * NCH * P, xproj=NCH * 104,
             dt_w=NCH * P, dt_b=NCH, a_log=NCH * NS, d_skip=NCH, m_out=NCH * P, w_out=P, b_out=1)


def offsets(widths):
    at, out = 0, {}
    for name, w in widths.items():
        out[name] = (at, at + w)
        at += w
    return out, at


OFF1, WIDTH1 = offsets(PACK1)

E0, F0 = 8, 512
CAP = int(N / E0 * 1.25) + 1
SLOTS = E0 * CAP
SLOT_TILES = -(-SLOTS // P)
ROWS = 107
RT = -(-CAP // ROWS)
HALF = -(-CAP // 2)
PACK2 = dict(wg=E0, ramp=E0, not_first=E0 * NT, overflow=NT, tri=P, ones=P, b2=E0 * P)
OFF2, WIDTH2 = offsets(PACK2)

HEADS, DK = 16, 8
QT = T // P
PACK3 = dict(wq=P, wq_swap=P, wk=P, wk_swap=P, wv=P, wo=P, cos=T, sin=T, mask_qk=P, mask_kq=P)
OFF3, WIDTH3 = offsets(PACK3)

E1, I1 = 16, 64
GROUPS, TOP_GROUPS, TOP_K = 4, 2, 4
RC = E1 * I1 // P
FC = RC + 1
ROUTED_SCALE = 2.5
PACK4 = dict(router=E1, e_bias=E1, ramp16=E1, before=GROUPS * GROUPS, spread=RC * P, gate_w=FC * P, up_w=FC * P, down_w=FC * P)
OFF4, WIDTH4 = offsets(PACK4)


def setup_stage(nc, x, slots, pack1, W, xT, mod, convW, negA, sel, identb):
    w = lambda name: W[:, OFF1[name][0]:OFF1[name][1]]
    with ExitStack() as ctx:
        sb = lambda name, shape, dt=F32: ctx.enter_context(nc.sbuf_tensor(name, shape, dt))
        sem = lambda name: ctx.enter_context(nc.semaphore(name))
        xtok = sb("xtok", [P, NT, P])
        zeros = sb("zeros", [P, SLOT_TILES * P])
        silu_c = sb("silu_c", [P, 2 * B])
        gsign = sb("gsign", [P, 2, 2, B])
        gabs = sb("gabs", [P, 2, 2, B])
        xps = [ctx.enter_context(nc.psum_tensor(f"xps{i}", [P, 4 * P], F32)) for i in range(2)]
        mps = ctx.enter_context(nc.psum_tensor("mps", [P, 2 * 6 * B], F32))
        w_loaded, x_loaded = sem("w_loaded"), sem("x_loaded")
        xps_ready, xT_ready, silu_ready = sem("xps_ready"), sem("xT_ready"), sem("silu_ready")
        mps_ready, mod_step, conv_step, prepared = sem("mps_ready"), sem("mod_step"), sem("conv_step"), sem("prepared")
        zeroed = sem("zeroed")
        with nc.Block() as block:
            @block.sync
            def _(sp):
                sp.dma_start(W[:, :], pack1).then_inc(w_loaded, 16)
                sp.dma_start(xtok[:, :, :], x.rearrange("(n p) d -> p n d", p=P)).then_inc(x_loaded, 16)

            @block.tensor
            def _(pe):
                pe.wait_ge(w_loaded, 16)
                pe.wait_ge(x_loaded, 16)
                for i in range(NT // 4):
                    if i >= 2:
                        pe.wait_ge(xT_ready, i - 1)
                    for k in range(4):
                        last = nc.tensor.transpose(xps[i % 2][:, k * P:(k + 1) * P], xtok[:, 4 * i + k, :], w("ident"))
                    last.then_inc(xps_ready, 1)
                pe.wait_ge(silu_ready, 1)
                for layer in range(2):
                    wm = w(f"wmod{layer}")
                    for j in range(6):
                        col = (layer * 6 + j) * B
                        last = nc.tensor.matmul(mps[:, col:col + B], wm[:, j * P:(j + 1) * P],
                                                silu_c[:, layer * B:(layer + 1) * B], start=True, stop=True)
                last.then_inc(mps_ready, 1)

            @block.scalar
            def _(act):
                act.wait_ge(w_loaded, 16)
                nc.scalar.activation(silu_c[:, :], W[:, OFF1["c0"][0]:OFF1["c1"][1]], ACT.Silu).then_inc(silu_ready, 1)
                nc.scalar.activation(negA[:, :], w("a_log"), ACT.Exp).then_inc(prepared, 1)
                act.wait_ge(prepared, 1)
                nc.scalar.mul(negA[:, :], negA[:, :], -1.0).then_inc(prepared, 1)
                nc.scalar.copy(identb[:, :], w("ident")).then_inc(prepared, 1)

            @block.vector
            def _(dve):
                for i in range(NT // 4):
                    dve.wait_ge(xps_ready, i + 1)
                    nc.vector.tensor_copy(xT[:, i * 4 * P:(i + 1) * 4 * P], xps[i % 2][:, :]).then_inc(xT_ready, 1)
                dve.wait_ge(mps_ready, 1)
                nc.vector.tensor_copy(mod[:, :, :, :], mps[:, :].rearrange("p (l j b) -> p l j b", l=2, j=6)).then_inc(mod_step, 1)
                dve.wait_ge(mod_step, 1)
                scales = mod[:, :, :, :].rearrange("p l (h j) b -> p l h j b", h=2)
                for layer in range(2):
                    nc.vector.tensor_scalar(scales[:, layer, :, 1, :], scales[:, layer, :, 1, :], 1.0, None, ALU.add).then_inc(mod_step, 1)
                    gate = scales[:, layer, :, 2, :]
                    nc.vector.tensor_scalar(gsign[:, layer], gate, 0.0, 2.0, ALU.is_ge, ALU.mult).then_inc(mod_step, 1)
                    nc.vector.scalar_tensor_tensor(gabs[:, layer], gate, -1.0, gate, ALU.mult, ALU.max).then_inc(mod_step, 1)
                    dve.wait_ge(mod_step, 5 * layer + 4)
                    nc.vector.tensor_scalar(gabs[:, layer], gabs[:, layer], 0.25, None, ALU.max).then_inc(mod_step, 1)
                    dve.wait_ge(mod_step, 5 * layer + 5)
                    nc.vector.scalar_tensor_tensor(gate, gsign[:, layer], -1.0, gabs[:, layer], ALU.add, ALU.mult).then_inc(mod_step, 1)

            @block.gpsimd
            def _(pool):
                nc.gpsimd.memset(zeros[:, :], 0.0).then_inc(conv_step, 1)
                pool.wait_ge(conv_step, 1)
                pool.dma_start(slots[0:SLOT_TILES * P, :].rearrange("(p n) d -> p (n d)", p=P), zeros[:, :]).then_inc(zeroed, 16)
                pool.wait_ge(w_loaded, 16)
                for k in range(KC):
                    nc.gpsimd.tensor_tensor(convW[:, k, :], W[:, OFF1["m_in"][0]:OFF1["m_in"][0] + NCH * P],
                                            w("conv_w")[:, k * NCH * P:(k + 1) * NCH * P], ALU.mult).then_inc(conv_step, 1)
                nc.gpsimd.tensor_copy(sel[:, :, :], w("pick")[0:96, :].unsqueeze(2).to_broadcast([96, 32, P])).then_inc(conv_step, 1)
                pool.wait_ge(zeroed, 16)


def layernorm_stage(nc, tag, W, xT, hT, scale, shift):
    center = W[:, OFF1["center"][0]:OFF1["center"][1]]
    mean = W[:, OFF1["mean"][0]:OFF1["mean"][0] + 1]
    eps = W[:, OFF1["eps"][0]:OFF1["eps"][1]]
    ident = W[:, OFF1["ident"][0]:OFF1["ident"][1]]
    with ExitStack() as ctx:
        sem = lambda name: ctx.enter_context(nc.semaphore(f"{tag}_{name}"))
        sq = [ctx.enter_context(nc.sbuf_tensor(f"{tag}_sq{i}", [P, T], F32)) for i in range(2)]
        sd, rs = (ctx.enter_context(nc.sbuf_tensor(f"{tag}_{name}", [P, NT], F32)) for name in ("sd", "rs"))
        xc = [ctx.enter_context(nc.psum_tensor(f"{tag}_xc{i}", [P, T], F32)) for i in range(4)]
        rb = [ctx.enter_context(nc.psum_tensor(f"{tag}_rb{i}", [P, T], F32)) for i in range(2)]
        var = ctx.enter_context(nc.psum_tensor(f"{tag}_var", [P, NT], F32))
        xc_ready, sq_ready, copied, var_ready, sd_ready = (
            sem("xc_ready"), sem("sq_ready"), sem("copied"), sem("var_ready"), sem("sd_ready"))
        rs_ready, rb_ready, scaled, h_ready = sem("rs_ready"), sem("rb_ready"), sem("scaled"), sem("h_ready")
        tile = lambda t, b: t[:, b * T:(b + 1) * T]
        with nc.Block() as block:
            @block.tensor
            def _(pe):
                for b in range(B + 2):
                    if b < B:
                        if b >= 4:
                            pe.wait_ge(copied, b - 3)
                        nc.tensor.matmul(xc[b % 4][:, :], center, tile(xT, b), start=True, stop=True).then_inc(xc_ready, 1)
                    if b >= 2:
                        pe.wait_ge(sq_ready, b - 1)
                        for k in range(4):
                            t = 4 * (b - 2) + k
                            last = nc.tensor.matmul(var[:, t:t + 1], sq[b % 2][:, k * P:(k + 1) * P], mean, start=True, stop=True)
                        last.then_inc(var_ready, 1)
                pe.wait_ge(rs_ready, 1)
                for b in range(B):
                    if b >= 2:
                        pe.wait_ge(scaled, b - 1)
                    for k in range(4):
                        t = 4 * b + k
                        last = nc.tensor.matmul(rb[b % 2][:, k * P:(k + 1) * P], rs[:, t:t + 1].to_broadcast([P, P]), ident,
                                                start=True, stop=True)
                    last.then_inc(rb_ready, 1)

            @block.scalar
            def _(act):
                for b in range(B):
                    act.wait_ge(copied, b + 1)
                    if b >= 2:
                        act.wait_ge(var_ready, b - 1)
                    nc.scalar.activation(sq[b % 2][:, :], tile(hT, b), ACT.Square).then_inc(sq_ready, 1)
                act.wait_ge(var_ready, B)
                nc.scalar.activation(sd[:, :], var[:, :], ACT.Sqrt, bias=eps).then_inc(sd_ready, 1)
                for b in range(B):
                    act.wait_ge(scaled, b + 1)
                    nc.scalar.activation(tile(hT, b), tile(hT, b), ACT.Identity, bias=shift(b)).then_inc(h_ready, 1)

            @block.vector
            def _(dve):
                for b in range(B):
                    dve.wait_ge(xc_ready, b + 1)
                    nc.vector.tensor_copy(tile(hT, b), xc[b % 4][:, :]).then_inc(copied, 1)
                dve.wait_ge(sd_ready, 1)
                nc.vector.reciprocal(rs[:, :], sd[:, :]).then_inc(rs_ready, 1)
                dve.wait_ge(copied, B)
                dve.wait_ge(sq_ready, B)
                for b in range(B):
                    dve.wait_ge(rb_ready, b + 1)
                    nc.vector.scalar_tensor_tensor(tile(hT, b), tile(hT, b), scale(b), rb[b % 2][:, :], ALU.mult, ALU.mult).then_inc(scaled, 1)


def mamba_inputs_stage(nc, W, hT, XP):
    w = lambda name: W[:, OFF1[name][0]:OFF1[name][1]]
    with ExitStack() as ctx:
        ps = [ctx.enter_context(nc.psum_tensor(f"xp_ps{i}", [P, T], F32)) for i in range(4)]
        sem = lambda name: ctx.enter_context(nc.semaphore(name))
        xp_ps_ready, xp_done, pad_done = sem("xp_ps_ready"), sem("xp_done"), sem("pad_done")
        with nc.Block() as block:
            @block.tensor
            def _(pe):
                with pe.Fori(0, B // 2) as i:
                    for k in range(4):
                        pe.wait_ge(xp_done, 4 * i + k + 1)
                        nc.tensor.matmul(ps[k][:, :], w("w_in")[:, (k % 2) * P:(k % 2 + 1) * P],
                                         hT[:, ds((2 * i + k // 2) * T, T)], start=True, stop=True).then_inc(xp_ps_ready, 1)

            @block.scalar
            def _(act):
                act.sem_inc(xp_done, 4)
                with act.Fori(0, B // 2) as i:
                    for k in range(4):
                        act.wait_ge(xp_ps_ready, 4 * i + k + 1)
                        src = ps[k][:, :] if k % 2 == 0 else ps[k][:, ::-1]
                        nc.scalar.activation(XP[:, ds((4 * i + k + 1) * XW + PAD, T)], src, ACT.Identity,
                                             bias=w("b_in")[:, k % 2:k % 2 + 1]).then_inc(xp_done, 1)

            @block.gpsimd
            def _(pool):
                nc.gpsimd.memset(XP[:, :].rearrange("p (u t) -> p u t", t=XW)[:, :, 0:PAD], 0.0).then_inc(pad_done, 1)


def mamba_stage(nc, W, XP, convW, negA, sel):
    w = lambda name: W[:, OFF1[name][0]:OFF1[name][1]]
    with ExitStack() as ctx:
        sb = lambda name, shape, dt=F32: ctx.enter_context(nc.sbuf_tensor(name, shape, dt))
        ps = lambda name: ctx.enter_context(nc.psum_tensor(name, [P, T], F32))
        sem = lambda name: ctx.enter_context(nc.semaphore(name))
        pre = sb("pre", [P, 4 * T])
        UZ = [sb(f"UZ{i}", [P, 4 * T]) for i in range(2)]
        xd = sb("xd", [P, T])
        ST = [sb(f"ST{i}", [96, T], BF16) for i in range(2)]
        r1 = sb("r1", [96, T])
        m1 = sb("m1", [96, T], BF16)
        xdt = sb("xdt", [P, NCH * T])
        ab = sb("ab", [P, NCH * T])
        DT = [sb(f"DT{i}", [P, NCH * T]) for i in range(2)]
        DU = [sb(f"DU{i}", [P, NCH * T]) for i in range(2)]
        CS = [sb(f"CS{i}", [P, T]) for i in range(4)]
        DA = [sb(f"DA{i}", [P, NCH * T]) for i in range(4)]
        DB = [sb(f"DB{i}", [P, NCH * T]) for i in range(2)]
        H = [sb(f"H{i}", [P, T]) for i in range(8)]
        PR = [sb(f"PR{i}", [P, T]) for i in range(8)]
        YZ = sb("YZ", [P, NCH * T])
        psB = [ps("psB0"), ps("psB1")]
        psC = [ps("psC0"), ps("psC1")]
        psY = [ps("psY0"), ps("psY1")]
        banks = [ps("pp0"), ps("pp1")]
        B_ready, C_ready, Y_done, pp_ready = sem("B_ready"), sem("C_ready"), sem("Y_done"), sem("pp_ready")
        pp_copied, silu_done, softplus_step, cs_ready, dA_ready = (
            sem("pp_copied"), sem("silu_done"), sem("softplus_step"), sem("cs_ready"), sem("dA_ready"))
        mult_done, scan_done, dt_ready, du_ready, fin_step, fin_done = (
            sem("mult_done"), sem("scan_done"), sem("dt_ready"), sem("du_ready"), sem("fin_step"), sem("fin_done"))
        prod_ready, rest_ready, split_step = sem("prod_ready"), sem("rest_ready"), sem("split_step")
        chunk = lambda t, c: t[:, c * T:(c + 1) * T]

        ORDER = (1, 2, 0, 3, 4, 5, 6, 7)
        place = lambda u, k: 0 if isinstance(u, int) and u == UNITS - 1 else ORDER.index(k)
        used = lambda u, k: 8 * u + 7 + place(u, k)
        bank = lambda u, k: banks[(k - 1 if u is None else 7 + place(u, k)) % 2]
        STEPS = {3: (1, 2), 5: (0,), 6: (3,), 7: (4,), 10: (5,), 11: (6,), 12: (7,)}

        def pe_step(pe, k, u, v, pv):
            pp = bank(u, k)
            if u is not None or k > 2:
                pe.wait_ge(pp_copied, (used(u, k) if u is not None else k - 1) - 1)
            if k == 0:
                pe.wait_ge(fin_done, u + 1)
                for c in range(NCH):
                    last = nc.tensor.matmul(pp[:, :], w("m_out")[:, c * P:(c + 1) * P], chunk(YZ, c), start=c == 0, stop=c == NCH - 1)
            elif k in (1, 2):
                for tap in range(KC):
                    last = nc.tensor.matmul(pp[:, :], convW[:, tap, (k - 1) * P:k * P], XP[:, ds((v + 1) * XW + tap, T)],
                                            start=tap == 0, stop=tap == KC - 1)
            elif k in (3, 4):
                last = nc.tensor.matmul(pp[:, :], w("m_in")[:, (k - 1) * P:k * P], XP[:, ds((v + 1) * XW + PAD, T)], start=True, stop=True)
            elif k == 5:
                pe.wait_ge(silu_done, v + 1)
                for c in range(NCH):
                    last = nc.tensor.matmul(pp[0:104, :], w("xproj")[:, c * 104:(c + 1) * 104], chunk(UZ[pv], c), start=c == 0, stop=c == NCH - 1)
            else:
                if k == 6:
                    pe.wait_ge(pp_copied, used(u, 5) + 1 if u is not None else 5)
                last = nc.tensor.matmul(pp[:, :], w("dt_w")[96:104, (k - 6) * P:(k - 5) * P], xd[96:104, :], start=True, stop=True)
            last.then_inc(pp_ready, 1)

        def pe_spread(pe, g, s, p, first):
            if not first or s >= 2:
                pe.wait_ge(mult_done, g - 1)
            nc.tensor.matmul(psB[s % 2][:, :], sel[:, s, :], ST[p][:, :], start=True, stop=True).then_inc(B_ready, 1)
            if not first or s >= 2:
                pe.wait_ge(cs_ready, g - 1)
            nc.tensor.matmul(psC[s % 2][:, :], sel[:, NS + s, :], ST[p][:, :], start=True, stop=True).then_inc(C_ready, 1)

        def pe_turn(pe, u, p, more):
            for j in range(3, NS + 3):
                if j < NS:
                    pe_spread(pe, 16 * u + j, j, p, False)
                elif more:
                    if j == NS:
                        pe.wait_ge(split_step, 3 * u + 6)
                    pe_spread(pe, 16 * u + j, j - NS, 1 - p, False)
                for k in STEPS.get(j, ()):
                    if more or k == 0:
                        pe_step(pe, k, u, u + 1, 1 - p)
                for c in range(NCH):
                    n = 2 * (j - 3) + c
                    pe.wait_ge(prod_ready, 32 * u + n + 9)
                    if j == 3:
                        pe.wait_ge(fin_step, 2 * u + c + 1)
                    nc.tensor.matmul(psY[c][:, :], w("ident"), PR[n % 8][:, :],
                                     start=j == 3, stop=j == NS + 2).then_inc(Y_done, 1)

        def act_step(act, k, u, v, pv):
            pp = bank(u, k)
            act.wait_ge(pp_ready, used(u, k) + 1 if u is not None else k)
            if k == 0:
                nc.scalar.copy(XP[:, ds(u * XW + PAD, T)], pp[:, ::-1] if pv else pp[:, :]).then_inc(pp_copied, 1)
            elif k <= 4:
                if u is not None:
                    act.wait_ge(silu_done, v)
                if k <= 2:
                    nc.scalar.activation(chunk(pre, k - 1), pp[:, :], ACT.Identity, bias=w("conv_b")[:, k - 1:k]).then_inc(pp_copied, 1)
                else:
                    nc.scalar.activation(chunk(pre, k - 1), pp[:, :], ACT.Identity).then_inc(pp_copied, 1)
            elif k == 5:
                if u is not None:
                    act.wait_ge(split_step, 3 * v)
                nc.scalar.copy(ST[pv][:, :], pp[0:96, :])
                nc.scalar.copy(xd[0:104, :], pp[0:104, :]).then_inc(pp_copied, 1)
            else:
                if u is not None:
                    act.wait_ge(dt_ready, v)
                nc.scalar.activation(chunk(xdt, k - 6), pp[:, :], ACT.Identity, bias=w("dt_b")[:, k - 6:k - 5]).then_inc(pp_copied, 1)
            if k == 4:
                act.wait_ge(pp_copied, used(u, 4) + 1 if u is not None else 4)
                if u is not None:
                    act.wait_ge(fin_done, u + 1)
                nc.scalar.activation(UZ[pv][:, :], pre[:, :], ACT.Silu).then_inc(silu_done, 1)
            if k == 7:
                act.wait_ge(pp_copied, used(u, 7) + 1 if u is not None else 7)
                nc.scalar.activation(ab[:, :], xdt[:, :], ACT.Abs).then_inc(softplus_step, 1)
                act.wait_ge(softplus_step, 3 * v + 1)
                nc.scalar.activation(ab[:, :], ab[:, :], ACT.Exp, scale=-1.0).then_inc(softplus_step, 1)
                act.wait_ge(softplus_step, 3 * v + 2)
                nc.scalar.activation(ab[:, :], ab[:, :], ACT.Ln, bias=1.0).then_inc(softplus_step, 1)

        def act_turn(act, u, p, more):
            for j in range(3, NS + 3):
                for k in STEPS.get(j - 1, ()):
                    if more or k == 0:
                        act_step(act, k, u, u + 1, 1 - p)
                if j < NS or more:
                    act_c(act, 16 * u + j, j % NS, False)
                if j + 1 < NS:
                    act_da(act, 16 * u + j + 1, j + 1, p, False)
                elif more:
                    if j + 1 == NS:
                        act.wait_ge(dt_ready, u + 2)
                    act_da(act, 16 * u + j + 1, j + 1 - NS, 1 - p, False)

        def act_c(act, g, s, first):
            act.wait_ge(C_ready, g + 1)
            if not first:
                act.wait_ge(prod_ready, 2 * g + 2)
            nc.scalar.copy(CS[s % 4][:, :], psC[s % 2][:, :]).then_inc(cs_ready, 1)

        def act_da(act, g, s, p, first):
            for c in range(NCH):
                if not first:
                    act.wait_ge(scan_done, 2 * g + c - 7)
                nc.scalar.activation(chunk(DA[s % 4], c), chunk(DT[p], c), ACT.Exp, scale=negA[:, c * NS + s:c * NS + s + 1]).then_inc(dA_ready, 1)

        def dve_state(dve, g, s, p, first):
            dve.wait_ge(B_ready, g + 1)
            if not first or s >= 2:
                dve.wait_ge(scan_done, 2 * g - 2)
            nc.vector.tensor_tensor(DB[s % 2][:, :].rearrange("p (c t) -> p c t", c=NCH),
                                    DU[p][:, :].rearrange("p (c t) -> p c t", c=NCH),
                                    psB[s % 2][:, :].unsqueeze(1).to_broadcast([P, NCH, T]), ALU.mult).then_inc(mult_done, 1)
            for c in range(NCH):
                dve.wait_ge(dA_ready, 2 * g + c + 1)
                if c == 0:
                    dve.wait_ge(mult_done, g + 1)
                dve.wait_ge(prod_ready, 2 * g + c + 1)
                nc.vector.tensor_tensor_scan(H[(2 * s + c) % 8][:, :], chunk(DA[s % 4], c), chunk(DB[s % 2], c), 0.0,
                                             ALU.mult, ALU.add).then_inc(scan_done, 1)

        def dve_dt(dve, v, pv):
            dve.wait_ge(softplus_step, 3 * v + 3)
            nc.vector.scalar_tensor_tensor(DT[pv][:, :], xdt[:, :], 0.0, ab[:, :], ALU.max, ALU.add).then_inc(dt_ready, 1)
            dve.wait_ge(dt_ready, v + 1)
            nc.vector.tensor_tensor(DU[pv][:, :], DT[pv][:, :], UZ[pv][:, 0:NCH * T], ALU.mult).then_inc(du_ready, 1)

        def dve_turn(dve, u, p, more):
            for j in range(3, NS + 3):
                if j < NS:
                    dve_state(dve, 16 * u + j, j, p, False)
                elif more:
                    if j == NS:
                        dve.wait_ge(du_ready, u + 2)
                    dve_state(dve, 16 * u + j, j - NS, 1 - p, False)
                if j == 12 and more:
                    dve_split(dve, u + 1, 1 - p)
                if j == 13 and more:
                    dve_dt(dve, u + 1, 1 - p)
            dve.wait_ge(Y_done, 32 * u + 40)
            dve.wait_ge(pp_ready, used(u, 0) + 1)
            for c in range(NCH):
                nc.vector.scalar_tensor_tensor(chunk(YZ, c), chunk(UZ[p], c), w("d_skip")[:, c:c + 1], psY[c][:, :],
                                               ALU.mult, ALU.add).then_inc(fin_step, 1)
            dve.wait_ge(fin_step, 2 * u + 4)
            nc.vector.tensor_tensor(YZ[:, :], YZ[:, :], UZ[p][:, NCH * T:], ALU.mult).then_inc(fin_done, 1)

        def pool_state(pool, g, s):
            for c in range(NCH):
                n = 2 * g + c
                pool.wait_ge(scan_done, n + 1)
                if c == 0:
                    pool.wait_ge(cs_ready, g + 1)
                pool.wait_ge(Y_done, n + 1)
                nc.gpsimd.tensor_tensor(PR[(2 * s + c) % 8][:, :], H[(2 * s + c) % 8][:, :], CS[s % 4][:, :], ALU.mult).then_inc(prod_ready, 1)

        def pool_split_rest(pool, v, pv, copied):
            pool.wait_ge(pp_copied, copied)
            nc.gpsimd.tensor_tensor(r1[:, :], xd[0:96, :], ST[pv][:, :], ALU.subtract).then_inc(rest_ready, 1)

        def dve_split(dve, v, pv):
            dve.wait_ge(rest_ready, v + 1)
            nc.vector.tensor_copy(m1[:, :], r1[:, :]).then_inc(split_step, 1)
            dve.wait_ge(split_step, 3 * v + 1)
            nc.vector.tensor_copy(ST[pv][32:64, :], m1[32:64, :]).then_inc(split_step, 1)
            nc.vector.tensor_tensor(ST[pv][64:96, :], r1[64:96, :], m1[64:96, :], ALU.subtract).then_inc(split_step, 1)

        def pool_turn(pool, u, p, more):
            for j in range(3, NS + 3):
                if j < NS:
                    pool_state(pool, 16 * u + j, j)
                elif more:
                    pool_state(pool, 16 * u + j, j - NS)
                if j == 11 and more:
                    pool_split_rest(pool, u + 1, 1 - p, used(u, 5) + 1)

        with nc.Block() as block:
            @block.tensor
            def _(pe):
                pe.sem_inc(Y_done, 8)
                for k in range(1, 8):
                    pe_step(pe, k, None, 0, 0)
                pe.wait_ge(split_step, 3)
                for s in range(3):
                    pe_spread(pe, s, s, 0, True)
                with pe.Fori(0, B - 1) as i:
                    for p in range(2):
                        pe_turn(pe, 2 * i + p, p, True)
                pe_turn(pe, UNITS - 2, 0, True)
                pe_turn(pe, UNITS - 1, 1, False)
                pe.wait_ge(pp_copied, used(UNITS - 1, 0))
                pe.wait_ge(fin_done, UNITS + 1)
                for c in range(NCH):
                    last = nc.tensor.matmul(banks[0][:, :], w("m_out")[:, c * P:(c + 1) * P], chunk(YZ, c), start=c == 0, stop=c == NCH - 1)
                last.then_inc(pp_ready, 1)

            @block.scalar
            def _(act):
                for k in range(1, 8):
                    act_step(act, k, None, 0, 0)
                act.wait_ge(dt_ready, 1)
                for s in range(4):
                    act_da(act, s, s, 0, True)
                    if s < 3:
                        act_c(act, s, s, True)
                with act.Fori(0, B - 1) as i:
                    for p in range(2):
                        act_turn(act, 2 * i + p, p, True)
                act_turn(act, UNITS - 2, 0, True)
                act_turn(act, UNITS - 1, 1, False)
                act.wait_ge(pp_ready, used(UNITS - 1, 0) + 2)
                nc.scalar.copy(XP[:, UNITS * XW + PAD:UNITS * XW + PAD + T], banks[0][:, ::-1]).then_inc(pp_copied, 1)

            @block.vector
            def _(dve):
                dve.sem_inc(fin_step, 2)
                nc.vector.memset(YZ[:, :], 0.0).then_inc(fin_done, 1)
                dve_split(dve, 0, 0)
                dve_dt(dve, 0, 0)
                dve.wait_ge(du_ready, 1)
                for s in range(3):
                    dve_state(dve, s, s, 0, True)
                with dve.Fori(0, B - 1) as i:
                    for p in range(2):
                        dve_turn(dve, 2 * i + p, p, True)
                dve_turn(dve, UNITS - 2, 0, True)
                dve_turn(dve, UNITS - 1, 1, False)

            @block.gpsimd
            def _(pool):
                pool.sem_inc(prod_ready, 8)
                pool_split_rest(pool, 0, 0, 5)
                for s in range(3):
                    pool_state(pool, s, s)
                with pool.Fori(0, B - 1) as i:
                    for p in range(2):
                        pool_turn(pool, 2 * i + p, p, True)
                pool_turn(pool, UNITS - 2, 0, True)
                pool_turn(pool, UNITS - 1, 1, False)


def mamba_outputs_stage(nc, W, XP, xT, gate):
    w = lambda name: W[:, OFF1[name][0]:OFF1[name][1]]
    with ExitStack() as ctx:
        ps = [ctx.enter_context(nc.psum_tensor(f"wo_ps{i}", [P, T], F32)) for i in range(2)]
        gated = [ctx.enter_context(nc.sbuf_tensor(f"wo_gated{i}", [P, T], F32)) for i in range(2)]
        sem = lambda name: ctx.enter_context(nc.semaphore(name))
        wo_ready, gated_ready, res_done = sem("wo_ready"), sem("gated_ready"), sem("res_done")
        with nc.Block() as block:
            @block.tensor
            def _(pe):
                with pe.Fori(0, B // 2) as i:
                    for u in range(2):
                        b = 2 * i + u
                        pe.wait_ge(gated_ready, b + 1)
                        nc.tensor.matmul(ps[u][:, :], w("w_out"), XP[:, ds((2 * b + 1) * XW + PAD, T)], start=True, stop=False)
                        nc.tensor.matmul(ps[u][:, :], w("w_out"), XP[:, ds((2 * b + 2) * XW + PAD, T)], start=False, stop=True).then_inc(wo_ready, 1)

            @block.vector
            def _(dve):
                dve.sem_inc(gated_ready, 2)
                with dve.Fori(0, B // 2) as i:
                    for u in range(2):
                        b = 2 * i + u
                        dve.wait_ge(wo_ready, b + 1)
                        dve.wait_ge(res_done, b + 1)
                        nc.vector.tensor_scalar(gated[u][:, :], ps[u][:, :], w("b_out"), gate(b), ALU.add, ALU.mult).then_inc(gated_ready, 1)

            @block.gpsimd
            def _(pool):
                pool.sem_inc(res_done, 2)
                with pool.Fori(0, B // 2) as i:
                    for u in range(2):
                        b = 2 * i + u
                        pool.wait_ge(gated_ready, b + 3)
                        nc.gpsimd.tensor_tensor(xT[:, ds(b * T, T)], xT[:, ds(b * T, T)], gated[u][:, :], ALU.add).then_inc(res_done, 1)


def route_stage(nc, W, W2, pack2, hT, slots, cw, gather_at):
    w = lambda name: W2[:, OFF2[name][0]:OFF2[name][1]]
    with ExitStack() as ctx:
        sb = lambda name, shape, dt=F32: ctx.enter_context(nc.sbuf_tensor(name, shape, dt))
        sem = lambda name: ctx.enter_context(nc.semaphore(name))
        htok = sb("htok", [P, NT, P])
        big = lambda name: sb(name, [P, NT, E0])
        col = lambda name: sb(name, [P, NT])
        lm, ex, sc, key, oh, pos = big("lm"), big("ex"), big("scs"), big("key"), big("oh"), big("pos")
        tot, incl = sb("tot", [P, E0, NT]), sb("incl", [P, E0, NT])
        mx, sm, top, m8, rank, ok, slot, send = (col(n) for n in ("mx", "sm", "top", "m8", "rank", "ok", "slot", "send"))
        scatter_at = sb("scatter_at", [P, NT], U32)
        psL = ctx.enter_context(nc.psum_tensor("psL", [P, NT, E0], F32))
        psP = ctx.enter_context(nc.psum_tensor("psP", [P, NT, E0], F32))
        psN = ctx.enter_context(nc.psum_tensor("psN", [P, NT, E0], F32))
        tps = [ctx.enter_context(nc.psum_tensor(f"tps{i}", [P, 4, P], F32)) for i in range(2)]
        loaded, logits_ready, tps_ready, htok_ready = sem("r_loaded"), sem("logits_ready"), sem("tps_ready"), sem("htok_ready")
        lm_ready, ex_ready, oh_ready, count_ready, step, scattered = (
            sem("lm_ready"), sem("ex_ready"), sem("oh_ready"), sem("count_ready"), sem("route_step"), sem("scattered"))
        wide = lambda t: t[:, :].unsqueeze(2).to_broadcast([P, NT, E0])
        with nc.Block() as block:
            @block.sync
            def _(sp):
                sp.dma_start(W2[:, :], pack2).then_inc(loaded, 16)

            @block.tensor
            def _(pe):
                pe.wait_ge(loaded, 16)
                for t in range(NT):
                    last = nc.tensor.matmul(psL[:, t, :], hT[:, t * P:(t + 1) * P], w("wg"), start=True, stop=True)
                last.then_inc(logits_ready, 1)
                for i in range(NT // 4):
                    if i >= 2:
                        pe.wait_ge(htok_ready, i - 1)
                    for k in range(4):
                        t = 4 * i + k
                        last = nc.tensor.transpose(tps[i % 2][:, k, :], hT[:, t * P:(t + 1) * P], W[:, 0:P])
                    last.then_inc(tps_ready, 1)
                pe.wait_ge(oh_ready, 1)
                flat = oh[:, :, :].rearrange("p t e -> p (t e)")
                nc.tensor.matmul(psP[:, :, :].rearrange("p t e -> p (t e)"), w("tri"), flat, start=True, stop=True)
                nc.tensor.matmul(psN[:, :, :].rearrange("p t e -> p (t e)"), w("ones"), flat, start=True, stop=True).then_inc(count_ready, 1)

            @block.scalar
            def _(act):
                for i in range(NT // 4):
                    act.wait_ge(tps_ready, i + 1)
                    nc.scalar.copy(htok[:, 4 * i:4 * i + 4, :], tps[i % 2][:, :, :]).then_inc(htok_ready, 1)
                act.wait_ge(lm_ready, 1)
                nc.scalar.activation(ex[:, :, :], lm[:, :, :], ACT.Exp).then_inc(ex_ready, 1)

            @block.vector
            def _(dve):
                done = [0]

                def then(ins):
                    done[0] += 1
                    ins.then_inc(step, 1)
                    dve.wait_ge(step, done[0])

                v = nc.vector
                dve.wait_ge(logits_ready, 1)
                then(v.tensor_reduce(mx[:, :], psL[:, :, :], AX.X, ALU.max))
                v.tensor_tensor(lm[:, :, :], psL[:, :, :], wide(mx), ALU.subtract).then_inc(lm_ready, 1)
                dve.wait_ge(ex_ready, 1)
                then(v.tensor_reduce(sm[:, :], ex[:, :, :], AX.X, ALU.add))
                then(v.reciprocal(sm[:, :], sm[:, :]))
                then(v.tensor_tensor(sc[:, :, :], ex[:, :, :], wide(sm), ALU.mult))
                then(v.tensor_reduce(top[:, :], sc[:, :, :], AX.X, ALU.max))
                then(v.tensor_tensor(key[:, :, :], sc[:, :, :], wide(top), ALU.is_ge))
                then(v.tensor_tensor(key[:, :, :], key[:, :, :], w("ramp").unsqueeze(1).to_broadcast([P, NT, E0]), ALU.mult))
                then(v.tensor_reduce(m8[:, :], key[:, :, :], AX.X, ALU.max))
                v.tensor_tensor(oh[:, :, :], key[:, :, :], wide(m8), ALU.is_equal).then_inc(oh_ready, 1)
                dve.wait_ge(count_ready, 1)
                then(v.tensor_copy(tot[:, :, :], psN[:, :, :].rearrange("p t e -> p e t")))
                then(v.tensor_tensor_scan(incl[:, :, :].rearrange("p e t -> p (e t)"), w("not_first"),
                                          tot[:, :, :].rearrange("p e t -> p (e t)"), 0.0, ALU.mult, ALU.add))
                then(v.tensor_tensor(incl[:, :, :], incl[:, :, :], tot[:, :, :], ALU.subtract))
                then(v.tensor_tensor(pos[:, :, :], psP[:, :, :], incl[:, :, :].rearrange("p e t -> p t e"), ALU.add))
                then(v.tensor_tensor(pos[:, :, :], pos[:, :, :], oh[:, :, :], ALU.mult))
                then(v.tensor_reduce(rank[:, :], pos[:, :, :], AX.X, ALU.add))
                then(v.tensor_scalar(ok[:, :], rank[:, :], float(CAP), None, ALU.is_le))
                then(v.tensor_tensor(cw[:, :], top[:, :], ok[:, :], ALU.mult))
                then(v.tensor_scalar(slot[:, :], m8[:, :], float(-CAP), float(E0 * CAP - 1), ALU.mult, ALU.add))
                then(v.tensor_tensor(slot[:, :], slot[:, :], rank[:, :], ALU.add))
                then(v.tensor_tensor(send[:, :], slot[:, :], w("overflow"), ALU.subtract))
                then(v.tensor_tensor(send[:, :], send[:, :], ok[:, :], ALU.mult))
                then(v.tensor_tensor(send[:, :], send[:, :], w("overflow"), ALU.add))
                then(v.tensor_copy(scatter_at[:, :], send[:, :]))
                then(v.tensor_scalar(slot[:, :], slot[:, :], float(SLOTS - 1), None, ALU.min))
                then(v.tensor_copy(gather_at[:, :], slot[:, :]))

            @block.gpsimd
            def _(pool):
                pool.wait_ge(htok_ready, NT // 4)
                pool.wait_ge(step, 23)
                for t in range(NT):
                    nc.gpsimd.indirect_dma_start(slots, bass.IndirectOffsetOnAxis(ap=scatter_at[:, t:t + 1], axis=0),
                                                 htok[:, t, :], None).then_inc(scattered, 16)
                pool.wait_ge(scattered, 16 * NT)


def experts_stage(nc, W, W2, slots, results, w1, b1, w2):
    w = lambda name: W2[:, OFF2[name][0]:OFF2[name][1]]
    NF = F0 // P
    parts = [(0, HALF), (HALF, CAP - HALF)]
    with ExitStack() as ctx:
        sb = lambda name, shape, dt=F32: ctx.enter_context(nc.sbuf_tensor(name, shape, dt))
        sem = lambda name: ctx.enter_context(nc.semaphore(name))
        stok = sb("stok", [P, SLOT_TILES, P])
        sT = sb("sT", [P, SLOT_TILES * P])
        W1R = [sb(f"W1R{i}", [P, F0]) for i in range(2)]
        B1R = [sb(f"B1R{i}", [P, NF]) for i in range(2)]
        W2R = [sb(f"W2R{i}", [P, NF, P]) for i in range(2)]
        hs = [sb(f"hs{i}", [P, NF, CAP]) for i in range(2)]
        yt = sb("yt", [P, E0 * RT * P])
        tps = [ctx.enter_context(nc.psum_tensor(f"stp{i}", [P, 4, P], F32)) for i in range(2)]
        psH = [ctx.enter_context(nc.psum_tensor(f"psH{i}", [P, HALF], F32)) for i in range(4)]
        psO = [ctx.enter_context(nc.psum_tensor(f"psO{i}", [P, P], F32)) for i in range(2)]
        s_loaded = [sem(f"s_loaded{i}") for i in range(4)]
        w_loaded = [sem(f"ew_loaded{i}") for i in range(2)]
        tps_ready, sT_ready, H_ready, hs_ready, O_ready, yt_ready = (
            sem("stp_ready"), sem("sT_ready"), sem("H_ready"), sem("hs_ready"), sem("O_ready"), sem("yt_ready"))
        stored = sem("y_stored")
        groups = [range(i, min(i + 4, SLOT_TILES)) for i in range(0, SLOT_TILES, 4)]
        cuts = [0, 12, 24, 36, SLOT_TILES]
        src = slots[0:SLOT_TILES * P, :].rearrange("(n p) d -> p n d", p=P)
        with nc.Block() as block:
            @block.sync
            def _(sp):
                for i in range(4):
                    sp.dma_start(stok[:, cuts[i]:cuts[i + 1], :], src[:, cuts[i]:cuts[i + 1], :]).then_inc(s_loaded[i], 16)
                with sp.Fori(0, E0 // 2) as i:
                    for q in range(2):
                        e = 2 * i + q
                        sp.wait_ge(O_ready, RT * e + RT)
                        sp.dma_start(W1R[q][:, :], w1[ds(e * P, P), :]).then_inc(w_loaded[q], 16)
                        sp.dma_start(B1R[q][:, :], b1[ds(e * P, P), :]).then_inc(w_loaded[q], 16)
                        sp.dma_start(W2R[q][:, :, :], w2[ds(e * F0, F0), :].rearrange("(c p) d -> p c d", p=P)).then_inc(w_loaded[q], 16)

            @block.tensor
            def _(pe):
                pe.sem_inc(O_ready, 2 * RT)
                pe.sem_inc(H_ready, 8)
                for g, tiles in enumerate(groups):
                    if tiles[0] in cuts:
                        pe.wait_ge(s_loaded[cuts.index(tiles[0])], 16)
                    if g >= 2:
                        pe.wait_ge(sT_ready, g - 1)
                    for k, t in enumerate(tiles):
                        if t in cuts:
                            pe.wait_ge(s_loaded[cuts.index(t)], 16)
                        last = nc.tensor.transpose(tps[g % 2][:, k, :], stok[:, t, :], W[:, 0:P])
                    last.then_inc(tps_ready, 1)
                pe.wait_ge(sT_ready, len(groups))
                with pe.Fori(0, E0 // 2) as i:
                    for q in range(2):
                        pe.wait_ge(w_loaded[q], 48 * i + 48)
                        for n, (at, wide) in enumerate(parts):
                            for f in range(NF):
                                k = 16 * i + 8 * q + 4 * n + f
                                pe.wait_ge(hs_ready, k + 1)
                                nc.tensor.matmul(psH[f][:, 0:wide], W1R[q][:, f * P:(f + 1) * P],
                                                 sT[:, ds((2 * i + q) * CAP + at, wide)], start=True, stop=True).then_inc(H_ready, 1)
                    for q in range(2):
                        pe.wait_ge(hs_ready, 16 * i + 8 * q + 12)
                        for r in range(RT):
                            rows = min(ROWS, CAP - r * ROWS)
                            pe.wait_ge(yt_ready, RT * (2 * i + q) + r + 1)
                            for f in range(NF):
                                last = nc.tensor.matmul(psO[r % 2][0:rows, :], hs[q][:, f, r * ROWS:r * ROWS + rows],
                                                        W2R[q][:, f, :], start=f == 0, stop=f == NF - 1)
                            last.then_inc(O_ready, 1)

            @block.scalar
            def _(act):
                act.sem_inc(hs_ready, 4)
                with act.Fori(0, E0 // 2) as i:
                    for q in range(2):
                        act.wait_ge(O_ready, RT * (2 * i + q) + RT)
                        for n, (at, wide) in enumerate(parts):
                            for f in range(NF):
                                act.wait_ge(H_ready, 16 * i + 8 * q + 4 * n + f + 9)
                                nc.scalar.activation(hs[q][:, f, at:at + wide], psH[f][:, 0:wide], ACT.Gelu,
                                                     bias=B1R[q][:, f:f + 1]).then_inc(hs_ready, 1)

            @block.vector
            def _(dve):
                for g, tiles in enumerate(groups):
                    dve.wait_ge(tps_ready, g + 1)
                    nc.vector.tensor_copy(sT[:, tiles[0] * P:(tiles[-1] + 1) * P],
                                          tps[g % 2][:, 0:len(tiles), :].rearrange("p k t -> p (k t)")).then_inc(sT_ready, 1)
                dve.sem_inc(yt_ready, 2)
                with dve.Fori(0, E0 // 2) as i:
                    for q in range(2):
                        for r in range(RT):
                            rows = min(ROWS, CAP - r * ROWS)
                            dve.wait_ge(O_ready, RT * (2 * i + q) + r + 1 + 2 * RT)
                            nc.vector.tensor_tensor(yt[0:rows, ds(((2 * i + q) * RT + r) * P, P)], psO[r % 2][0:rows, :],
                                                    w("b2")[0:rows, ds((2 * i + q) * P, P)], ALU.add).then_inc(yt_ready, 1)

            @block.gpsimd
            def _(pool):
                with pool.Fori(0, E0 // 2) as i:
                    for q in range(2):
                        pool.wait_ge(yt_ready, RT * (2 * i + q + 1) + 2)
                        full = (RT - 1) * ROWS
                        pool.dma_start(results[ds((2 * i + q) * CAP, full), :].rearrange("(r p) d -> p r d", p=ROWS),
                                       yt[0:ROWS, ds((2 * i + q) * RT * P, (RT - 1) * P)].rearrange("p (r d) -> p r d", d=P)).then_inc(stored, 16)
                        pool.dma_start(results[ds((2 * i + q) * CAP + full, CAP - full), :],
                                       yt[0:CAP - full, ds(((2 * i + q) * RT + RT - 1) * P, P)]).then_inc(stored, 16)
                pool.wait_ge(stored, 32 * E0)


def combine_stage(nc, W, results, cw, gather_at, xT, gate):
    with ExitStack() as ctx:
        sb = lambda name, shape, dt=F32: ctx.enter_context(nc.sbuf_tensor(name, shape, dt))
        sem = lambda name: ctx.enter_context(nc.semaphore(name))
        gtok, scaled = sb("gtok", [P, NT, P]), sb("scaled", [P, NT, P])
        ps = [ctx.enter_context(nc.psum_tensor(f"gps{i}", [P, 4 * P], F32)) for i in range(2)]
        gathered = [sem(f"gathered{i}") for i in range(NT // 4)]
        scaled_ready, ps_ready, res_done = sem("scaled_ready"), sem("gps_ready"), sem("g_res_done")
        with nc.Block() as block:
            @block.gpsimd
            def _(pool):
                for t in range(NT):
                    nc.gpsimd.indirect_dma_start(gtok[:, t, :], None, results,
                                                 bass.IndirectOffsetOnAxis(ap=gather_at[:, t:t + 1], axis=0)).then_inc(gathered[t // 4], 16)

            @block.scalar
            def _(act):
                for t in range(NT):
                    if t % 4 == 0:
                        act.wait_ge(gathered[t // 4], 64)
                    nc.scalar.activation(scaled[:, t, :], gtok[:, t, :], ACT.Copy, scale=cw[:, t:t + 1]).then_inc(scaled_ready, 1)

            @block.tensor
            def _(pe):
                for i in range(NT // 4):
                    pe.wait_ge(scaled_ready, 4 * i + 4)
                    if i >= 2:
                        pe.wait_ge(res_done, i - 1)
                    for k in range(4):
                        last = nc.tensor.transpose(ps[i % 2][:, k * P:(k + 1) * P], scaled[:, 4 * i + k, :], W[:, 0:P])
                    last.then_inc(ps_ready, 1)

            @block.vector
            def _(dve):
                for i in range(NT // 4):
                    dve.wait_ge(ps_ready, i + 1)
                    x = xT[:, i * T:(i + 1) * T]
                    nc.vector.scalar_tensor_tensor(x, ps[i % 2][:, :], gate(i), x, ALU.mult, ALU.add).then_inc(res_done, 1)


def attention_stage(nc, W, pack3, scratch, m_scratch, hT, xT, identb, gate):
    w = lambda name: W3[:, OFF3[name][0]:OFF3[name][1]]
    ident = W[:, 0:P]
    MROW = 72
    KR = MROW + 3
    PAIRS = HEADS // 2
    UNITS_T = 5 * PAIRS
    BEFORE, EACH = 11, 13
    with ExitStack() as ctx:
        sb = lambda name, shape, dt=F32: ctx.enter_context(nc.sbuf_tensor("a_" + name, shape, dt))
        ps = lambda name: ctx.enter_context(nc.psum_tensor("a_" + name, [P, T], F32))
        sem = lambda name: ctx.enter_context(nc.semaphore("a_" + name))
        W3 = sb("W3", [P, WIDTH3])
        mqk, mkq = sb("mqk", [P, P], BF16), sb("mkq", [P, P], BF16)
        qst = [sb(f"qst{i}", [KR, HEADS * T], BF16) for i in range(2)]
        kst = [sb(f"kst{i}", [KR, HEADS * T], BF16) for i in range(2)]
        parts = [[sb(f"parts{x}{i}", [P, 3, T], BF16) for i in range(2)] for x in "qk"]
        TA, TB, QR, R = sb("TA", [P, T]), sb("TB", [P, T]), sb("QR", [P, T]), sb("R", [P, T])
        HB = sb("HB", [P, T])
        VA = [sb(f"VA{i}", [P, QT, HEADS, 32]) for i in range(2)]
        PT = [[sb(f"PT{i}{u}", [P, T]) for u in range(5)] for i in range(2)]
        OT = [sb(f"OT{i}", [P, T]) for i in range(2)]
        OTK, OF = sb("OTK", [P, QT, P]), sb("OF", [P, T])
        rec = sb("rec", [P, QT, 4])
        MX, NR = sb("MX", [P, QT, HEADS]), sb("NR", [P, QT, HEADS // 2])
        NMB = sb("NMB", [P, QT, 3, HEADS // 2], BF16)
        MTS = [sb(f"MTS{i}", [24, T], BF16) for i in range(2)]
        psM = [ps("psM0"), ps("psM1")]
        psS = [ps(f"psS{i}") for i in range(4)]
        psO, mb = ps("psO"), ps("mb")
        loaded = sem("loaded")
        mb_ready, S_ready, M_ready, PV_done = sem("mb_ready"), sem("S_ready"), sem("M_ready"), sem("PV_done")
        mb_used, M_used, m_step, x_done = sem("mb_used"), sem("M_used"), sem("m_step"), sem("x_done")
        E_done, O_copied, part_step, hb_ready, act_init = sem("E_done"), sem("O_copied"), sem("part_step"), sem("hb_ready"), sem("act_init")
        rope_step, pool_init = sem("rope_step"), sem("pool_init")
        ones_ready, ones_loaded = sem("ones_ready"), sem("ones_loaded")
        ones3 = sb("ones3", [3, 2 * T], BF16)
        st_loaded = [sem("st_loaded0"), sem("st_loaded1")]
        parts_stored, m_stored = sem("parts_stored"), [sem("m_storedA"), sem("m_storedB")]
        m_loaded = [sem("m_loadedA"), sem("m_loadedB")]

        def groups(half):
            first = half * HEADS // 2
            return [(j, first + h, n) for j, n in ((0, 4), (1, 2), (2, 1), (3, 1)) for h in range(0, HEADS // 2, n)]

        NG = len(groups(0))
        M_SLOTS = {3: (0, 0, 7), 4: (0, 7, 14), 5: (0, 14, NG), 6: (1, 0, 7), 7: (1, 7, 14), 8: (1, 14, NG)}
        BLOCKS = [[(0, 0, 0)], [(0, 1, 0), (0, 3, 384)], [(1, 0, 0)], [(1, 1, 0), (1, 3, 384)], [(0, 2, 0), (1, 2, 256)]]
        PLACE = {(h, i): (u, col) for u, bank in enumerate(BLOCKS) for h, i, col in bank}
        EARLY = {1: ["q"], 2: ["q_swap"], 3: ["k"], 4: ["k_swap"], 5: ["G1"], 6: ["MA"], 7: ["G2"]}
        LATE = {3: ["G0"], 4: ["V"]}
        TAIL = ["G3", "MB", "F", "O"]

        def uses(more_p, more_m):
            order = [x for slot in range(1, 9) for x in EARLY.get(slot, []) + LATE.get(slot, [])] + TAIL
            kept = [x for x in order if (more_p or x[0] not in "qk") and (more_m or x not in ("V", "MA", "MB"))]
            return {x: n for n, x in enumerate(kept)}

        class Turn:
            def __init__(self, t, p, base, more_p=True, more_m=True):
                self.t, self.p, self.base, self.more_p, self.more_m = t, p, base, more_p, more_m
                self.use = uses(more_p, more_m)

        def turns(eng, body):
            with eng.Fori(0, 3) as i:
                for p in range(2):
                    body(Turn(2 * i + p, p, BEFORE + EACH * (2 * i + p)))
            at = BEFORE + EACH * 6
            last = Turn(6, 0, at, more_p=False)
            body(last)
            body(Turn(7, 1, at + len(last.use), more_p=False, more_m=False))

        def pe_use(pe, name, n, t2, p1):
            if n is not None:
                pe.wait_ge(mb_used, n)
            if name[0] in "qk":
                last = nc.tensor.matmul(mb[:, :], w("w" + name), hT[:, ds(t2 * T, T)], start=True, stop=True)
            elif name == "V":
                for i in range(QT):
                    last = nc.tensor.matmul(mb[:, i * P:(i + 1) * P], HB[:, i * P:(i + 1) * P], w("wv"), start=True, stop=True)
            elif name[0] == "G":
                for j in range(QT):
                    last = nc.tensor.transpose(mb[:, j * P:(j + 1) * P], OT[int(name[1]) % 2][:, j * P:(j + 1) * P], ident)
            elif name[0] == "M":
                rows = mb[:, 0:T // 2].bitcast(BF16)
                for j in range(QT):
                    last = nc.tensor.transpose(rows[0:24, j * P:(j + 1) * P], NMB[:, j, :, :].rearrange("p s h -> p (s h)"), identb[:, :])
            elif name == "F":
                for j in range(QT):
                    last = nc.tensor.transpose(mb[:, j * P:(j + 1) * P], OTK[:, j, :], ident)
            else:
                last = nc.tensor.matmul(mb[:, :], w("wo"), OF[:, :], start=True, stop=True)
            last.then_inc(mb_ready, 1)

        def pe_scores(pe, t, p, k):
            for u, bank in enumerate(BLOCKS):
                n = UNITS_T * t + 5 * k + u
                if not isinstance(n, int) or n >= 4:
                    pe.wait_ge(E_done, n - 3)
                for h, i, col in bank:
                    wide, at = T - i * P, (2 * k + h) * T
                    out = psS[(5 * k + u) % 4][:, col:col + wide]
                    nc.tensor.matmul(out, kst[p][:, at + i * P:at + (i + 1) * P], qst[p][:, at + i * P:at + T], start=True, stop=False)
                    last = nc.tensor.matmul(out[:, 0:P], identb[:, :], mkq[:, :], start=False, stop=True)
                last.then_inc(S_ready, 1)

        def pe_maxima(pe, n0, p, half, a, b):
            for g, (j, h0, nh) in enumerate(groups(half)[a:b]):
                n = n0 + g
                if not isinstance(n, int) or n >= 2:
                    pe.wait_ge(M_used, n - 1)
                wide = (j + 1) * P
                for x in range(nh):
                    at = (h0 + x) * T
                    out = psM[(half * NG + a + g) % 2][:, x * wide:(x + 1) * wide]
                    nc.tensor.matmul(out, qst[p][0:72, at + j * P:at + (j + 1) * P], kst[p][0:72, at:at + wide], start=True, stop=False)
                    last = nc.tensor.matmul(out[:, j * P:wide], identb[:, :], mqk[:, :], start=False, stop=True)
                last.then_inc(M_ready, 1)

        def pe_values(pe, t, p, k):
            pe.wait_ge(E_done, UNITS_T * t + 5 * k + 5)
            if k == 0:
                pe.wait_ge(mb_used, 9 if isinstance(t, int) and t == 0 else v_used(t))
            if k % 2 == 0:
                g = 4 * t + k // 2
                if not isinstance(g, int) or g >= 1:
                    pe.wait_ge(O_copied, g)
            for i in range(QT):
                for h in range(2):
                    u, col = PLACE[(h, i)]
                    c = (2 * k + h) % 4
                    last = nc.tensor.matmul(psO[32 * c:32 * c + 32, i * P:T], VA[p][:, i, 2 * k + h, :],
                                            PT[k % 2][u][:, col:col + T - i * P], start=i == 0, stop=i == QT - 1)
            last.then_inc(PV_done, 1)

        V_AT = uses(True, True)["V"]
        v_used = lambda t: BEFORE + EACH * (t - 1) + V_AT + 1 if isinstance(t, int) else EACH * t + (BEFORE - EACH + V_AT + 1)

        def pe_turn(pe, c):
            for slot in range(1, 9):
                if slot < PAIRS:
                    if slot == 4:
                        pe.wait_ge(m_loaded[1], 16 * c.t + 16)
                    pe_scores(pe, c.t, c.p, slot)
                elif c.more_m:
                    pe.wait_ge(m_loaded[0], 16 * c.t + 32)
                    pe_scores(pe, c.t + 1, 1 - c.p, 0)
                for name in EARLY.get(slot, []):
                    pe_turn_use(pe, c, name)
                if slot in M_SLOTS and c.more_m:
                    half, a, b = M_SLOTS[slot]
                    if slot == 3:
                        pe.wait_ge(st_loaded[1 - c.p], st_count(c.t + 1, 1 - c.p))
                    pe_maxima(pe, 2 * NG * (c.t + 1) + half * NG + a, 1 - c.p, half, a, b)
                for name in LATE.get(slot, []):
                    pe_turn_use(pe, c, name)
                pe_values(pe, c.t, c.p, slot - 1)
            for name in TAIL:
                pe_turn_use(pe, c, name)

        LOADS = 18 * 16
        def st_count(t, p):
            if isinstance(t, int):
                return LOADS * (t // 2 + 1)
            return LOADS // 2 * t + (LOADS if p == 0 else LOADS // 2)

        def pe_turn_use(pe, c, name):
            if name not in c.use:
                return
            if name[0] == "G":
                pe.wait_ge(O_copied, 4 * c.t + int(name[1]) + 1)
            if name == "V":
                pe.wait_ge(hb_ready, c.t + 2)
            if name in ("MA", "MB"):
                pe.wait_ge(m_step, 10 * (c.t + 1) + (5 if name == "MA" else 10))
            pe_use(pe, name, c.base + c.use[name], c.t + 2, 1 - c.p)

        def act_exps(act, t, p, k):
            for u in range(5):
                n = UNITS_T * t + 5 * k + u
                act.wait_ge(S_ready, n + 1)
                if u == 0:
                    pair = PAIRS * t + k
                    if not isinstance(pair, int) or pair >= 2:
                        act.wait_ge(PV_done, pair - 1)
                nc.scalar.activation(PT[k % 2][u][:, :], psS[(5 * k + u) % 4][:, :], ACT.Exp, scale=DK ** -0.5).then_inc(E_done, 1)

        def act_part(act, b, pb, step):
            x = step // 2
            act.wait_ge(rope_step, 6 * b + 3 * x + 1 + step % 2)
            if step == 0:
                if not isinstance(b, int) or b >= 2:
                    act.wait_ge(parts_stored, 32 * b - 32)
            nc.scalar.copy(parts[x][pb][:, step % 2, :], (QR if step % 2 == 0 else R)[:, :]).then_inc(part_step, 1)

        def act_turn(act, c):
            for slot in range(1, 9):
                if slot < PAIRS:
                    act_exps(act, c.t, c.p, slot)
                elif c.more_m:
                    act_exps(act, c.t + 1, 1 - c.p, 0)
                if slot == 2 and c.more_m:
                    act.wait_ge(mb_ready, 9 if isinstance(c.t, int) and c.t == 0 else v_used(c.t))
                    nc.scalar.copy(HB[:, :], hT[:, ds((c.t + 1) * T, T)]).then_inc(hb_ready, 1)
                if slot in (3, 4, 5, 6) and c.more_p:
                    act_part(act, c.t + 2, c.p, slot - 3)
                if slot % 2 == 0:
                    g = 4 * c.t + slot // 2 - 1
                    act.wait_ge(PV_done, PAIRS * c.t + slot)
                    if slot <= 4:
                        act.wait_ge(mb_ready, turn_base_before(c, slot // 2 + 1))
                    else:
                        act.wait_ge(mb_ready, c.base + c.use[f"G{slot // 2 - 3}"] + 1)
                    nc.scalar.copy(OT[(slot // 2 - 1) % 2][:, :], psO[:, :]).then_inc(O_copied, 1)

        def turn_base_before(c, g):
            if isinstance(c.t, int) and c.t == 7:
                prev = uses(False, True)
                return c.base - len(prev) + prev[f"G{g}"] + 1
            prev = uses(True, True)
            return c.base - EACH + prev[f"G{g}"] + 1

        def dve_maxima(dve, n0, t1, half, a, b):
            for g, (j, h0, nh) in enumerate(groups(half)[a:b]):
                dve.wait_ge(M_ready, n0 + g + 1)
                if a + g == 0 and (not isinstance(t1, int) or t1 > 0):
                    dve.wait_ge(m_step, 10 * t1 - 9 + 5 * half)
                src = psM[(half * NG + a + g) % 2][:, 0:nh * (j + 1) * P].rearrange("p (h k) -> p h k", h=nh)
                nc.vector.tensor_reduce(MX[:, j, h0:h0 + nh], src, AX.X, ALU.max).then_inc(M_used, 1)
            if b == NG:
                hs = slice(half * 8, half * 8 + 8)
                at = 10 * t1 + 5 * half
                v = nc.vector
                dve.wait_ge(M_used, 2 * NG * t1 + (half + 1) * NG)
                v.tensor_scalar(NR[:, :, :], MX[:, :, hs], -1.0, None, ALU.mult).then_inc(m_step, 1)
                dve.wait_ge(m_step, at + 1)
                v.tensor_copy(NMB[:, :, 0, :], NR[:, :, :]).then_inc(m_step, 1)
                dve.wait_ge(m_step, at + 2)
                v.tensor_tensor(NR[:, :, :], NR[:, :, :], NMB[:, :, 0, :], ALU.subtract).then_inc(m_step, 1)
                dve.wait_ge(m_step, at + 3)
                v.tensor_copy(NMB[:, :, 1, :], NR[:, :, :]).then_inc(m_step, 1)
                dve.wait_ge(m_step, at + 4)
                v.tensor_tensor(NMB[:, :, 2, :], NR[:, :, :], NMB[:, :, 1, :], ALU.subtract).then_inc(m_step, 1)

        def dve_use(dve, name, n, t, t2, p1):
            dve.wait_ge(mb_ready, n + 1)
            v = nc.vector
            if name[0] in "qk":
                swap = name.endswith("swap")
                x = 0 if name[0] == "q" else 1
                count = 6 * t2 + 3 * x - 2
                if x or not isinstance(t2, int) or t2 > 0:
                    dve.wait_ge(rope_step, count)
                v.tensor_tensor((TB if swap else TA)[:, :], mb[:, :], w("sin" if swap else "cos"), ALU.mult).then_inc(mb_used, 1)
            elif name == "V":
                v.tensor_copy(VA[p1][:, :, :, 0:DK], mb[:, :].rearrange("p (i h r) -> p i h r", i=QT, r=DK)).then_inc(mb_used, 1)
            elif name[0] == "G":
                g = int(name[1])
                o = mb[:, :].rearrange("p (j c r) -> p j c r", j=QT, c=4)
                v.reciprocal(rec[:, :, :], o[:, :, :, DK]).then_inc(x_done, 1)
                dve.wait_ge(x_done, 5 * t + g + 1)
                v.tensor_tensor(OTK[:, :, 32 * g:32 * g + 32].rearrange("p j (c r) -> p j c r", c=4), o[:, :, :, 0:DK],
                                rec[:, :, :].unsqueeze(3).to_broadcast([P, QT, 4, DK]), ALU.mult).then_inc(mb_used, 1)
            elif name[0] == "M":
                half = "AB".index(name[1])
                rows = mb[:, 0:T // 2].bitcast(BF16)
                if not isinstance(t, int) or t >= 0:
                    dve.wait_ge(m_loaded[half], 16 * t + 16)
                v.tensor_copy(MTS[half][:, :], rows[0:24, :]).then_inc(mb_used, 1)
            elif name == "F":
                v.tensor_copy(OF[:, :], mb[:, :]).then_inc(mb_used, 1)
            else:
                x = xT[:, ds(t * T, T)]
                v.scalar_tensor_tensor(x, mb[:, :], gate(t), x, ALU.mult, ALU.add).then_inc(mb_used, 1)

        def dve_turn(dve, c):
            def use(name):
                if name in c.use:
                    dve_use(dve, name, c.base + c.use[name], c.t, c.t + 2, 1 - c.p)
            for slot in range(1, 9):
                for name in EARLY.get(slot, []):
                    use(name)
                if slot in M_SLOTS and c.more_m:
                    half, a, b = M_SLOTS[slot]
                    dve_maxima(dve, 2 * NG * (c.t + 1) + half * NG + a, c.t + 1, half, a, b)
                for name in LATE.get(slot, []):
                    use(name)
            for name in TAIL:
                use(name)
                if name == "G3":
                    dve.sem_inc(x_done, 1)

        def pool_rope(pool, b, pb, x, used, used_prev):
            q, at = parts[x][pb], 6 * b + 3 * x
            pool.wait_ge(mb_used, used)
            if x or not isinstance(b, int) or b > 0:
                pool.wait_ge(part_step, 4 * b + 2 * x)
            nc.gpsimd.tensor_tensor(QR[:, :], TA[:, :], TB[:, :], ALU.add).then_inc(rope_step, 1)
            pool.wait_ge(part_step, 4 * b + 2 * x + 1)
            nc.gpsimd.tensor_tensor(R[:, :], QR[:, :], q[:, 0, :], ALU.subtract).then_inc(rope_step, 1)
            pool.wait_ge(part_step, 4 * b + 2 * x + 2)
            nc.gpsimd.tensor_tensor(q[:, 2, :], R[:, :], q[:, 1, :], ALU.subtract).then_inc(rope_step, 1)

        def store_parts(sp, b, pb):
            sp.wait_ge(rope_step, 6 * b + 6)
            sp.wait_ge(part_step, 4 * b + 4)
            for x in range(2):
                sp.dma_start(scratch[2 * pb + x].rearrange("s p t -> p s t"), parts[x][pb][:, :, :]).then_inc(parts_stored, 16)

        def load_stack(sp, b, pb):
            sp.wait_ge(parts_stored, 32 * b + 32)
            for a in range(3):
                for c in range(3):
                    row = 24 * a + 8 * c
                    for x, (st, part) in enumerate(((qst, a), (kst, c))):
                        sp.dma_start(st[pb][row:row + 8, :].rearrange("j (h t) -> j h t", h=HEADS),
                                     scratch[2 * pb + x, part].rearrange("(h j) t -> j h t", j=DK)).then_inc(st_loaded[pb], 16)

        def send_maxima(sp, b, half, used, pb):
            sp.wait_ge(mb_used, used)
            sp.dma_start(m_scratch[half], MTS[half][:, :]).then_inc(m_stored[half], 16)
            sp.wait_ge(m_stored[half], 16 * b + 16)
            sp.dma_start(qst[pb][MROW:MROW + 3, half * 8 * T:(half + 1) * 8 * T],
                         m_scratch[half].rearrange("(s h) t -> s (h t)", s=3)).then_inc(m_loaded[half], 16)

        PRO = ["q", "q_swap", "k", "k_swap"]
        with nc.Block() as block:
            @block.sync
            def _(sp):
                sp.dma_start(W3[:, :], pack3).then_inc(loaded, 16)
                sp.wait_ge(ones_ready, 1)
                for i in range(2):
                    for n in range(0, HEADS * T, 2 * T):
                        sp.dma_start(kst[i][MROW:KR, n:n + 2 * T], ones3[:, :]).then_inc(ones_loaded, 16)
                store_parts(sp, 0, 0)
                load_stack(sp, 0, 0)
                store_parts(sp, 1, 1)
                send_maxima(sp, 0, 0, 10, 0)
                send_maxima(sp, 0, 1, 11, 0)

                def body(c):
                    if c.more_m:
                        sp.wait_ge(S_ready, UNITS_T * c.t + 5)
                        load_stack(sp, c.t + 1, 1 - c.p)
                        send_maxima(sp, c.t + 1, 0, c.base + c.use["MA"] + 1, 1 - c.p)
                        if c.more_p:
                            store_parts(sp, c.t + 2, c.p)
                        send_maxima(sp, c.t + 1, 1, c.base + c.use["MB"] + 1, 1 - c.p)
                turns(sp, body)

            @block.tensor
            def _(pe):
                pe.wait_ge(loaded, 16)
                pe.wait_ge(act_init, 2)
                for n, (b, name) in enumerate([(b, name) for b in range(2) for name in PRO]):
                    pe_use(pe, name, n or None, b, 0)
                pe.wait_ge(hb_ready, 1)
                pe_use(pe, "V", 8, 0, 0)
                pe.wait_ge(st_loaded[0], LOADS)
                pe_maxima(pe, 0, 0, 0, 0, NG)
                pe.wait_ge(m_step, 5)
                pe_use(pe, "MA", 9, 0, 0)
                pe_maxima(pe, NG, 0, 1, 0, NG)
                pe.wait_ge(m_step, 10)
                pe_use(pe, "MB", 10, 0, 0)
                pe.wait_ge(m_loaded[0], 16)
                pe.wait_ge(ones_loaded, 16 * HEADS)
                pe_scores(pe, 0, 0, 0)
                turns(pe, lambda c: pe_turn(pe, c))

            @block.scalar
            def _(act):
                act.wait_ge(loaded, 16)
                nc.scalar.copy(mqk[:, :], w("mask_qk")).then_inc(act_init, 1)
                nc.scalar.copy(mkq[:, :], w("mask_kq")).then_inc(act_init, 1)
                nc.scalar.copy(HB[:, :], hT[:, 0:T]).then_inc(hb_ready, 1)
                for b in range(2):
                    for step in range(4):
                        act_part(act, b, b, step)
                act_exps(act, 0, 0, 0)
                turns(act, lambda c: act_turn(act, c))

            @block.vector
            def _(dve):
                nc.vector.memset(ones3[:, :], 1.0).then_inc(ones_ready, 1)
                for n, (b, name) in enumerate([(b, name) for b in range(2) for name in PRO]):
                    dve_use(dve, name, n, -1, b, 0)
                dve.wait_ge(pool_init, 3)
                dve_use(dve, "V", 8, -1, 0, 0)
                dve_maxima(dve, 0, 0, 0, 0, NG)
                dve_use(dve, "MA", 9, -1, 0, 0)
                dve_maxima(dve, NG, 0, 1, 0, NG)
                dve_use(dve, "MB", 10, -1, 0, 0)
                turns(dve, lambda c: dve_turn(dve, c))

            @block.gpsimd
            def _(pool):
                for i in range(2):
                    nc.gpsimd.memset(VA[i][:, :, :, :], 0.0).then_inc(pool_init, 1)
                pool.wait_ge(pool_init, 2)
                for i in range(2):
                    last = nc.gpsimd.memset(VA[i][:, :, :, DK], 1.0)
                last.then_inc(pool_init, 1)
                for b in range(2):
                    for x in range(2):
                        pool_rope(pool, b, b, x, 4 * b + 2 * x + 2, None)

                def body(c):
                    if c.more_p:
                        for x, name in enumerate(("q_swap", "k_swap")):
                            pool_rope(pool, c.t + 2, c.p, x, c.base + c.use[name] + 1, None)
                turns(pool, body)


def group_route_stage(nc, W4, pack4, hT, identb, spread, cT):
    w = lambda name: W4[:, OFF4[name][0]:OFF4[name][1]]
    with ExitStack() as ctx:
        sb = lambda name, shape, dt=F32: ctx.enter_context(nc.sbuf_tensor("g_" + name, shape, dt))
        sem = lambda name: ctx.enter_context(nc.semaphore("g_" + name))
        full = lambda name: sb(name, [P, NT, E1])
        scores, sc, masked, key, oh, chosen = (full(n) for n in ("scores", "sc", "masked", "key", "oh", "chosen"))
        pair = sb("pair", [P, NT, GROUPS, 6])
        gs, grank = sb("gs", [P, NT, GROUPS]), sb("grank", [P, NT, GROUPS])
        gt, ge = sb("gt", [P, NT, GROUPS, GROUPS]), sb("ge", [P, NT, GROUPS, GROUPS])
        best, m = sb("best", [P, NT]), sb("m", [P, NT])
        cparts = sb("cparts", [P, NT, 3, E1], BF16)
        psL = ctx.enter_context(nc.psum_tensor("g_psL", [P, NT, E1], F32))
        cps = [ctx.enter_context(nc.psum_tensor(f"g_cps{i}", [48, T], BF16)) for i in range(2)]
        loaded, logits_ready, scores_ready, step, cps_ready, cT_ready, spread_ready = (
            sem(n) for n in ("loaded", "logits_ready", "scores_ready", "step", "cps_ready", "cT_ready", "spread_ready"))
        experts = lambda t: t[:, :].unsqueeze(2).to_broadcast([P, NT, E1])
        STEPS = 51
        with nc.Block() as block:
            @block.sync
            def _(sp):
                sp.dma_start(W4[:, :], pack4).then_inc(loaded, 16)

            @block.tensor
            def _(pe):
                pe.wait_ge(loaded, 16)
                for t in range(NT):
                    last = nc.tensor.matmul(psL[:, t, :], hT[:, t * P:(t + 1) * P], w("router"), start=True, stop=True)
                last.then_inc(logits_ready, 1)
                pe.wait_ge(step, STEPS)
                for i in range(NT // 4):
                    if i >= 2:
                        pe.wait_ge(cT_ready, i - 1)
                    for k in range(4):
                        last = nc.tensor.transpose(cps[i % 2][:, k * P:(k + 1) * P],
                                                   cparts[:, 4 * i + k, :, :].rearrange("p s e -> p (s e)"), identb[:, :])
                    last.then_inc(cps_ready, 1)

            @block.scalar
            def _(act):
                act.wait_ge(loaded, 16)
                nc.scalar.copy(spread[:, :], w("spread")[0:48, :]).then_inc(spread_ready, 1)
                act.wait_ge(logits_ready, 1)
                nc.scalar.activation(scores[:, :, :], psL[:, :, :], ACT.Sigmoid).then_inc(scores_ready, 1)
                for i in range(NT // 4):
                    act.wait_ge(cps_ready, i + 1)
                    nc.scalar.copy(cT[:, i * T:(i + 1) * T], cps[i % 2][:, :]).then_inc(cT_ready, 1)

            @block.vector
            def _(dve):
                done = [0]

                def then(ins):
                    done[0] += 1
                    ins.then_inc(step, 1)
                    dve.wait_ge(step, done[0])

                v = nc.vector
                dve.wait_ge(loaded, 16)
                dve.wait_ge(scores_ready, 1)
                then(v.tensor_tensor(sc[:, :, :], scores[:, :, :], w("e_bias").unsqueeze(1).to_broadcast([P, NT, E1]), ALU.add))
                g4 = sc[:, :, :].rearrange("p t (g e) -> p t g e", g=GROUPS)
                g22 = sc[:, :, :].rearrange("p t (g a b) -> p t g a b", g=GROUPS, a=2)
                for at, x, y in ((0, g4[:, :, :, 0], g4[:, :, :, 1]), (1, g4[:, :, :, 2], g4[:, :, :, 3]),
                                 (2, g4[:, :, :, 0], g4[:, :, :, 2]), (3, g4[:, :, :, 1], g4[:, :, :, 3]),
                                 (4, g4[:, :, :, 0], g4[:, :, :, 3]), (5, g4[:, :, :, 1], g4[:, :, :, 2])):
                    done[0] += 1
                    v.tensor_tensor(pair[:, :, :, at], x, y, ALU.add).then_inc(step, 1)
                dve.wait_ge(step, done[0])
                then(v.tensor_reduce(gs[:, :, :], pair[:, :, :, :], AX.X, ALU.max))
                shape = [P, NT, GROUPS, GROUPS]
                own = gs[:, :, :].unsqueeze(3).to_broadcast(shape)
                other = gs[:, :, :].unsqueeze(2).to_broadcast(shape)
                lower = w("before").rearrange("p (g h) -> p g h", g=GROUPS)
                then(v.tensor_tensor(gt[:, :, :, :], other, own, ALU.is_gt))
                then(v.tensor_tensor(ge[:, :, :, :], other, own, ALU.is_equal))
                then(v.tensor_tensor(ge[:, :, :, :], ge[:, :, :, :], lower.unsqueeze(1).to_broadcast(shape), ALU.mult))
                then(v.tensor_tensor(gt[:, :, :, :], gt[:, :, :, :], ge[:, :, :, :], ALU.add))
                then(v.tensor_reduce(grank[:, :, :], gt[:, :, :, :], AX.X, ALU.add))
                then(v.tensor_scalar(grank[:, :, :], grank[:, :, :], TOP_GROUPS - 0.5, None, ALU.is_lt))
                then(v.tensor_tensor(masked[:, :, :].rearrange("p t (g e) -> p t g e", g=GROUPS), g4,
                                     grank[:, :, :].unsqueeze(3).to_broadcast([P, NT, GROUPS, E1 // GROUPS]), ALU.mult))
                for k in range(TOP_K):
                    then(v.tensor_reduce(best[:, :], masked[:, :, :], AX.X, ALU.max))
                    then(v.tensor_tensor(key[:, :, :], masked[:, :, :], experts(best), ALU.is_ge))
                    then(v.tensor_tensor(key[:, :, :], key[:, :, :], w("ramp16").unsqueeze(1).to_broadcast([P, NT, E1]), ALU.mult))
                    then(v.tensor_reduce(m[:, :], key[:, :, :], AX.X, ALU.max))
                    if k == 0:
                        then(v.tensor_tensor(chosen[:, :, :], key[:, :, :], experts(m), ALU.is_equal))
                        then(v.scalar_tensor_tensor(masked[:, :, :], chosen[:, :, :], -3e38, masked[:, :, :], ALU.mult, ALU.add))
                    else:
                        then(v.tensor_tensor(oh[:, :, :], key[:, :, :], experts(m), ALU.is_equal))
                        then(v.tensor_tensor(chosen[:, :, :], chosen[:, :, :], oh[:, :, :], ALU.add))
                        if k < TOP_K - 1:
                            then(v.scalar_tensor_tensor(masked[:, :, :], oh[:, :, :], -3e38, masked[:, :, :], ALU.mult, ALU.add))
                then(v.tensor_tensor(chosen[:, :, :], chosen[:, :, :], scores[:, :, :], ALU.mult))
                then(v.tensor_reduce(m[:, :], chosen[:, :, :], AX.X, ALU.add))
                then(v.tensor_scalar(m[:, :], m[:, :], 1e-20, None, ALU.add))
                then(v.reciprocal(m[:, :], m[:, :]))
                then(v.tensor_tensor(chosen[:, :, :], chosen[:, :, :], experts(m), ALU.mult))
                then(v.tensor_scalar(chosen[:, :, :], chosen[:, :, :], ROUTED_SCALE, None, ALU.mult))
                then(v.tensor_copy(cparts[:, :, 0, :], chosen[:, :, :]))
                then(v.tensor_tensor(chosen[:, :, :], chosen[:, :, :], cparts[:, :, 0, :], ALU.subtract))
                then(v.tensor_copy(cparts[:, :, 1, :], chosen[:, :, :]))
                then(v.tensor_tensor(cparts[:, :, 2, :], chosen[:, :, :], cparts[:, :, 1, :], ALU.subtract))


def group_experts_stage(nc, W4, hT, spread, cT, xT, gate):
    w = lambda name: W4[:, OFF4[name][0]:OFF4[name][1]]
    with ExitStack() as ctx:
        sb = lambda name, n: [ctx.enter_context(nc.sbuf_tensor(f"f_{name}{i}", [P, T], F32)) for i in range(n)]
        ps = lambda name, n: [ctx.enter_context(nc.psum_tensor(f"f_{name}{i}", [P, T], F32)) for i in range(n)]
        sem = lambda name: ctx.enter_context(nc.semaphore("f_" + name))
        SG, HU, HC = sb("SG", 2), sb("HU", 2), sb("HC", 3)
        psG, psU, psC, psY = ps("psG", 2), ps("psU", 2), ps("psC", 2), ps("psY", 2)
        G_ready, U_ready, C_ready, D_done, SG_ready, HU_ready, HC_ready, x_done = (
            sem(n) for n in ("G_ready", "U_ready", "C_ready", "D_done", "SG_ready", "HU_ready", "HC_ready", "x_done"))
        LAG = 2
        with nc.Block() as block:
            @block.tensor
            def _(pe):
                pe.sem_inc(D_done, 3)
                with pe.Fori(0, B // 2) as i:
                    for q in range(2):
                        b = 2 * i + q
                        h = hT[:, ds(b * T, T)]
                        for c in range(FC + LAG):
                            if c < FC:
                                n, r = FC * b + c, (FC * q + c) % 2
                                pe.wait_ge(SG_ready, n + 1)
                                nc.tensor.matmul(psG[r][:, :], w("gate_w")[:, c * P:(c + 1) * P], h, start=True, stop=True).then_inc(G_ready, 1)
                                if c < RC:
                                    pe.wait_ge(HC_ready, FC * b + c + 1)
                                pe.wait_ge(HU_ready, n + 1)
                                nc.tensor.matmul(psU[r][:, :], w("up_w")[:, c * P:(c + 1) * P], h, start=True, stop=True).then_inc(U_ready, 1)
                            if c < RC:
                                nc.tensor.matmul(psC[c % 2][:, :], spread[:, c * P:(c + 1) * P], cT[:, ds(b * T, T)], start=True, stop=True).then_inc(C_ready, 1)
                            d = c - LAG
                            if d >= 0:
                                if d == 0:
                                    pe.wait_ge(x_done, b + 1)
                                pe.wait_ge(HC_ready, FC * b + d + 3)
                                nc.tensor.matmul(psY[q][:, :], w("down_w")[:, d * P:(d + 1) * P], HC[(FC * q + d) % 3][:, :],
                                                 start=d == 0, stop=d == FC - 1).then_inc(D_done, 1)

            @block.scalar
            def _(act):
                act.sem_inc(SG_ready, 2)
                with act.Fori(0, B // 2) as i:
                    for q in range(2):
                        for c in range(FC):
                            n, r = FC * (2 * i + q) + c, (FC * q + c) % 2
                            act.wait_ge(G_ready, n + 1)
                            act.wait_ge(HU_ready, n + 1)
                            nc.scalar.activation(SG[r][:, :], psG[r][:, :], ACT.Silu).then_inc(SG_ready, 1)

            @block.vector
            def _(dve):
                dve.sem_inc(HU_ready, 2)
                dve.sem_inc(HC_ready, 2)
                dve.sem_inc(x_done, 2)
                with dve.Fori(0, B // 2) as i:
                    for q in range(2):
                        b = 2 * i + q
                        for c in range(FC):
                            n, r = FC * b + c, (FC * q + c) % 2
                            dve.wait_ge(SG_ready, n + 3)
                            dve.wait_ge(U_ready, n + 1)
                            dve.wait_ge(HC_ready, n + 2)
                            nc.vector.tensor_tensor(HU[r][:, :], SG[r][:, :], psU[r][:, :], ALU.mult).then_inc(HU_ready, 1)
                            dve.wait_ge(HU_ready, n + 3)
                            dve.wait_ge(D_done, n + 1)
                            if c < RC:
                                dve.wait_ge(C_ready, RC * b + c + 1)
                                nc.vector.tensor_tensor(HC[(FC * q + c) % 3][:, :], HU[r][:, :], psC[c % 2][:, :], ALU.mult).then_inc(HC_ready, 1)
                            else:
                                nc.vector.tensor_copy(HC[(FC * q + c) % 3][:, :], HU[r][:, :]).then_inc(HC_ready, 1)
                        dve.wait_ge(D_done, FC * b + FC + 3)
                        x = xT[:, ds(b * T, T)]
                        nc.vector.scalar_tensor_tensor(x, psY[q][:, :], gate(b), x, ALU.mult, ALU.add).then_inc(x_done, 1)


def output_stage(nc, W, xT, out):
    w = lambda name: W[:, OFF1[name][0]:OFF1[name][1]]
    with ExitStack() as ctx:
        ps = [ctx.enter_context(nc.psum_tensor(f"out_ps{i}", [P, 4 * P], F32)) for i in range(2)]
        tok = ctx.enter_context(nc.sbuf_tensor("out_tok", [P, NT, P], F32))
        sem = lambda name: ctx.enter_context(nc.semaphore(name))
        out_ps_ready, tok_ready, stored = sem("out_ps_ready"), sem("tok_ready"), sem("stored")
        o = out.rearrange("(n p) d -> p n d", p=P)
        with nc.Block() as block:
            @block.tensor
            def _(pe):
                for i in range(NT // 4):
                    if i >= 2:
                        pe.wait_ge(tok_ready, i - 1)
                    for k in range(4):
                        t = 4 * i + k
                        last = nc.tensor.transpose(ps[i % 2][:, k * P:(k + 1) * P], xT[:, t * P:(t + 1) * P], w("ident"))
                    last.then_inc(out_ps_ready, 1)

            @block.vector
            def _(dve):
                for i in range(NT // 4):
                    dve.wait_ge(out_ps_ready, i + 1)
                    nc.vector.tensor_copy(tok[:, 4 * i:4 * i + 4, :], ps[i % 2][:, :].rearrange("p (k d) -> p k d", k=4)).then_inc(tok_ready, 1)

            @block.sync
            def _(sp):
                for i in range(NT // 4):
                    sp.wait_ge(tok_ready, i + 1)
                    sp.dma_start(o[:, 4 * i:4 * i + 4, :], tok[:, 4 * i:4 * i + 4, :]).then_inc(stored, 16)
                sp.wait_ge(stored, 16 * (NT // 4))


def program(nc, ins, out):
    with ExitStack() as ctx:
        sb = lambda name, shape, dt=F32: ctx.enter_context(nc.sbuf_tensor(name, shape, dt))
        W = sb("W", [P, WIDTH1])
        xT = sb("xT", [P, N])
        mod = sb("mod", [P, 2, 6, B])
        modv = lambda layer, j: (lambda b: mod[:, layer, j, :][:, ds(b, 1)])
        identb = sb("identb", [P, P], BF16)
        with ExitStack() as mamba:
            msb = lambda name, shape, dt=F32: mamba.enter_context(nc.sbuf_tensor(name, shape, dt))
            convW = msb("convW", [P, KC, NCH * P])
            negA = msb("negA", [P, NCH * NS])
            sel = msb("sel", [96, 32, P], BF16)
            XP = msb("XP", [P, (UNITS + 1) * XW])
            setup_stage(nc, ins["x"], ins["slots"], ins["pack1"], W, xT, mod, convW, negA, sel, identb)
            with nc.sbuf_tensor("hT0", [P, N], F32) as hT:
                layernorm_stage(nc, "ln0", W, xT, hT, modv(0, 1), modv(0, 0))
                mamba_inputs_stage(nc, W, hT, XP)
            mamba_stage(nc, W, XP, convW, negA, sel)
            mamba_outputs_stage(nc, W, XP, xT, modv(0, 2))
        slots, results = ins["slots"], ins["results"]
        with ExitStack() as moe:
            msb = lambda name, shape, dt=F32: moe.enter_context(nc.sbuf_tensor(name, shape, dt))
            W2, cw, gather_at = msb("W2", [P, WIDTH2]), msb("cw", [P, NT]), msb("gather_at", [P, NT], U32)
            with nc.sbuf_tensor("hT1", [P, N], F32) as hT:
                layernorm_stage(nc, "ln1", W, xT, hT, modv(0, 4), modv(0, 3))
                route_stage(nc, W, W2, ins["pack2"], hT, slots, cw, gather_at)
            experts_stage(nc, W, W2, slots, results, ins["w1"], ins["b1"], ins["w2"])
            combine_stage(nc, W, results, cw, gather_at, xT, modv(0, 5))
        with nc.sbuf_tensor("hT2", [P, N], F32) as hT:
            layernorm_stage(nc, "ln2", W, xT, hT, modv(1, 1), modv(1, 0))
            attention_stage(nc, W, ins["pack3"], ins["scratch"], ins["m_scratch"], hT, xT, identb, modv(1, 2))
        with ExitStack() as ffn:
            fsb = lambda name, shape, dt=F32: ffn.enter_context(nc.sbuf_tensor(name, shape, dt))
            W4, hT = fsb("W4", [P, WIDTH4]), fsb("hT3", [P, N])
            spread, cT = fsb("spread", [48, RC * P], BF16), fsb("cT", [48, N], BF16)
            layernorm_stage(nc, "ln3", W, xT, hT, modv(1, 4), modv(1, 3))
            group_route_stage(nc, W4, ins["pack4"], hT, identb, spread, cT)
            group_experts_stage(nc, W4, hT, spread, cT, xT, modv(1, 5))
        output_stage(nc, W, xT, out)


def kernel(**inputs):
    import numpy as np
    import concourse.bacc as bacc
    from concourse.bass_utils import run_bass_kernel_spmd

    a = {k: np.asarray(v) for k, v in inputs.items()}
    f = np.float32
    halves = lambda m: np.ascontiguousarray(m.reshape(2, P, -1).transpose(1, 0, 2).reshape(P, -1))
    eye = np.eye(P, dtype=f)
    part = {}
    part["ident"], part["center"] = eye, eye - f(1 / P)
    part["mean"], part["eps"] = np.full((P, P), 1 / P, f), np.full((P, 1), EPS, f)
    part["pick"] = (np.arange(P)[:, None] % 32 == np.arange(32)[None, :]).astype(f)
    for n in range(2):
        part[f"c{n}"], part[f"wmod{n}"] = a[f"L{n}_c"].T, a[f"L{n}_wmod"]
    m = {k[8:]: v for k, v in a.items() if k.startswith("L0_attn_")}
    part["w_in"], part["b_in"] = m["w_in"].T, halves(m["b_in"])
    part["conv_b"], part["m_in"] = halves(m["conv_b"]), m["m_in_w"].T
    part["conv_w"] = np.broadcast_to(m["conv_w"][:, 0, :].T.reshape(1, -1), (P, KC * NCH * P))
    xp = m["xproj_w"]
    part["xproj"] = halves(np.concatenate([xp[RANK:]] * 3 + [xp[:RANK]], 0).T)
    dtw = np.zeros((P, NCH * P), f)
    dtw[96:96 + RANK] = m["dt_w"].T
    part["dt_w"], part["dt_b"] = dtw, halves(m["dt_b"])
    part["a_log"], part["d_skip"] = halves(m["A_log"]), halves(m["Dp"])
    part["m_out"], part["w_out"], part["b_out"] = halves(m["m_out_w"].T), m["w_out"].T, m["b_out"][:, None]
    m0 = {k[7:]: v for k, v in a.items() if k.startswith("L0_ffn_")}
    part["wg"] = m0["wg"]
    part["ramp"] = np.broadcast_to(np.arange(E0, 0, -1, dtype=f), (P, E0))
    part["not_first"] = np.broadcast_to(np.tile(np.arange(NT) > 0, E0).astype(f), (P, E0 * NT))
    part["overflow"] = (SLOT_TILES * P + np.arange(N).reshape(NT, P).T).astype(f)
    part["tri"], part["ones"] = np.triu(np.ones((P, P), f)), np.ones((P, P), f)
    part["b2"] = np.broadcast_to(m0["b2"].reshape(1, -1), (P, E0 * P))
    wqkv = a["L1_attn_W_qkv"]
    swap = np.arange(P) ^ 1
    for n, name in enumerate("qkv"):
        part["w" + name] = wqkv[n * P:(n + 1) * P].T
        part[f"w{name}_swap"] = wqkv[n * P:(n + 1) * P][swap].T
    part["wo"] = a["L1_attn_W_o"].T
    freq = f(10000.0) ** (-np.arange(0, DK, 2, dtype=f) / f(DK))
    angle = (np.arange(T, dtype=f)[None, :] * freq[:, None]).astype(f)[np.arange(P) % DK // 2]
    part["cos"] = np.cos(angle)
    part["sin"] = np.sin(angle) * np.where(np.arange(P) % 2, 1, -1).astype(f)[:, None]
    late = np.arange(P)[None, :] > np.arange(P)[:, None]
    part["mask_qk"] = np.where(late, f(-1e30), f(0))
    part["mask_kq"] = np.ascontiguousarray(part["mask_qk"].T)
    m = {k[7:]: v for k, v in a.items() if k.startswith("L1_ffn_")}
    part["router"] = m["router_weight"].T
    part["e_bias"] = np.broadcast_to(m["e_bias"], (P, E1))
    part["ramp16"] = np.broadcast_to(np.arange(E1, 0, -1, dtype=f), (P, E1))
    part["before"] = np.broadcast_to(np.tril(np.ones((GROUPS, GROUPS), f), -1).reshape(-1), (P, GROUPS * GROUPS))
    part["spread"] = (np.arange(P)[:, None] % E1 == np.arange(RC * P)[None, :] // I1).astype(f)
    part["gate_w"] = np.concatenate([m["gate_w"].reshape(E1 * I1, P), m["sh_gate_w"]], 0).T
    part["up_w"] = np.concatenate([m["up_w"].reshape(E1 * I1, P), m["sh_up_w"]], 0).T
    down = np.concatenate([m["down_w"].transpose(0, 2, 1).reshape(E1 * I1, P), m["sh_down_w"].T], 0)
    part["down_w"] = down.reshape(FC, P, P).transpose(1, 0, 2).reshape(P, FC * P)
    arrays = {"pack4": np.concatenate([part[k] for k in PACK4], 1), "pack3": np.concatenate([part[k] for k in PACK3], 1),
              "w1": m0["W1"].reshape(E0 * P, F0), "w2": m0["W2"].reshape(E0 * F0, P),
              "b1": m0["b1"].reshape(E0, F0 // P, P).transpose(0, 2, 1).reshape(E0 * P, -1),
              "pack2": np.concatenate([part[k] for k in PACK2], 1),
              "x": a["L0_attn_x"].reshape(N, P),
              "pack1": np.concatenate([part[k] for k in PACK1], 1)}
    arrays = {k: np.ascontiguousarray(v) for k, v in arrays.items()}

    nc = bacc.Bacc("TRN2", target_bir_lowering=False, num_devices=1)
    ins = {k: nc.dram_tensor(f"in_{k}", v.shape, mybir.dt.from_np(v.dtype), kind="ExternalInput").ap() for k, v in arrays.items()}
    ins["slots"] = nc.dram_tensor("slots", (SLOT_TILES * P + N, P), F32).ap()
    ins["scratch"] = nc.dram_tensor("scratch", (4, 3, P, T), BF16).ap()
    ins["m_scratch"] = nc.dram_tensor("m_scratch", (2, 24, T), BF16).ap()
    ins["results"] = nc.dram_tensor("results", (SLOTS, P), F32).ap()
    out = nc.dram_tensor("out", (N, P), F32, kind="ExternalOutput").ap()
    program(nc, ins, out)
    r = run_bass_kernel_spmd(nc, [{f"in_{k}": v for k, v in arrays.items()}], core_ids=[0])
    return r.results[0]["out"].reshape(B, T, P)
```

```python
from contextlib import ExitStack

import concourse.bass as bass
from concourse import mybir

F32 = mybir.dt.float32
BF16 = mybir.dt.bfloat16
U32 = mybir.dt.uint32
ALU = mybir.AluOpType
ACT = mybir.ActivationFunctionType
AX = mybir.AxisListType
ds = bass.ds

P = 128
B = 8
T = 512
N = B * T
NT = N // P
NCH = 2
NS = 16
KC = 4
PAD = KC - 1
EARLY = 2
GT = 8
RANK = 8
UNITS = 2 * B
XW = T + PAD
EPS = 1e-5

PACK1 = dict(ident=P, center=P, mean=P, eps=1, pick=32, c0=B, c1=B, wmod0=6 * P, wmod1=6 * P,
             w_in=2 * P, b_in=2, conv_b=NCH, m_in=2 * NCH * P, conv_w=KC * NCH * P, xproj=NCH * 104,
             dt_w=NCH * P, dt_b=NCH, a_log=NCH * NS, d_skip=NCH, m_out=NCH * P, w_out=P, b_out=1)


def offsets(widths):
    at, out = 0, {}
    for name, w in widths.items():
        out[name] = (at, at + w)
        at += w
    return out, at


OFF1, WIDTH1 = offsets(PACK1)

E0, F0 = 8, 512
CAP = int(N / E0 * 1.25) + 1
SLOTS = E0 * CAP
SLOT_TILES = -(-SLOTS // P)
ROWS = 112
RT = -(-CAP // ROWS)
HALF = -(-CAP // 2)
PACK2 = dict(wg=E0, ramp=E0, not_first=E0 * NT, overflow=NT, tri=P, ones=P, b2=E0 * P)
OFF2, WIDTH2 = offsets(PACK2)

HEADS, DK = 16, 8
QT = T // P
PACK3 = dict(wq=P, wq_swap=P, wk=P, wk_swap=P, wv=P, wo=P, cos=T, sin=T, mask_qk=P, mask_kq=P)
OFF3, WIDTH3 = offsets(PACK3)

E1, I1 = 16, 64
GROUPS, TOP_GROUPS, TOP_K = 4, 2, 4
RC = E1 * I1 // P
FC = RC + 1
ROUTED_SCALE = 2.5
PACK4 = dict(router=E1, e_bias=E1, ramp16=E1, before=GROUPS * GROUPS, spread=RC * P, gate_w=FC * P, up_w=FC * P, down_w=FC * P)
OFF4, WIDTH4 = offsets(PACK4)


def setup_stage(nc, x, pack1, W, xT, mod, negA, identb):
    w = lambda name: W[:, OFF1[name][0]:OFF1[name][1]]
    with ExitStack() as ctx:
        sb = lambda name, shape, dt=F32: ctx.enter_context(nc.sbuf_tensor(name, shape, dt))
        sem = lambda name: ctx.enter_context(nc.semaphore(name))
        xtok = sb("xtok", [P, NT, P])
        silu_c = sb("silu_c", [P, 2 * B])
        gsign = sb("gsign", [P, 2, 2, B])
        gabs = sb("gabs", [P, 2, 2, B])
        xps = [ctx.enter_context(nc.psum_tensor(f"xps{i}", [P, 4 * P], F32)) for i in range(2)]
        mps = ctx.enter_context(nc.psum_tensor("mps", [P, 2 * 6 * B], F32))
        ident_loaded, w_loaded = sem("ident_loaded"), sem("w_loaded")
        x_loaded = [sem(f"x_loaded{i}") for i in range(4)]
        xps_ready, xT_ready, silu_ready = sem("xps_ready"), sem("xT_ready"), sem("silu_ready")
        mps_ready, mod_step, prepared = sem("mps_ready"), sem("mod_step"), sem("prepared")
        with nc.Block() as block:
            @block.sync
            def _(sp):
                sp.dma_start(W[:, 0:P], pack1[:, 0:P]).then_inc(ident_loaded, 16)
                for i in range(4):
                    part = slice(i * NT // 4, (i + 1) * NT // 4)
                    sp.dma_start(xtok[:, part, :], x.rearrange("(n p) d -> p n d", p=P)[:, part, :]).then_inc(x_loaded[i], 16)
                sp.dma_start(W[:, P:], pack1[:, P:]).then_inc(w_loaded, 16)

            @block.tensor
            def _(pe):
                pe.wait_ge(ident_loaded, 16)
                for i in range(NT // 4):
                    pe.wait_ge(x_loaded[i // 2], 16)
                    if i >= 2:
                        pe.wait_ge(xT_ready, i - 1)
                    for k in range(4):
                        last = nc.tensor.transpose(xps[i % 2][:, k * P:(k + 1) * P], xtok[:, 4 * i + k, :], w("ident"))
                    last.then_inc(xps_ready, 1)
                pe.wait_ge(w_loaded, 16)
                pe.wait_ge(silu_ready, 1)
                for layer in range(2):
                    wm = w(f"wmod{layer}")
                    for j in range(6):
                        col = (layer * 6 + j) * B
                        last = nc.tensor.matmul(mps[:, col:col + B], wm[:, j * P:(j + 1) * P],
                                                silu_c[:, layer * B:(layer + 1) * B], start=True, stop=True)
                last.then_inc(mps_ready, 1)

            @block.scalar
            def _(act):
                act.wait_ge(w_loaded, 16)
                nc.scalar.activation(silu_c[:, :], W[:, OFF1["c0"][0]:OFF1["c1"][1]], ACT.Silu).then_inc(silu_ready, 1)
                nc.scalar.activation(negA[:, :], w("a_log"), ACT.Exp).then_inc(prepared, 1)
                act.wait_ge(prepared, 1)
                nc.scalar.mul(negA[:, :], negA[:, :], -1.0).then_inc(prepared, 1)
                act.wait_ge(ident_loaded, 16)
                nc.scalar.copy(identb[:, :], w("ident")).then_inc(prepared, 1)

            @block.vector
            def _(dve):
                for i in range(NT // 4):
                    dve.wait_ge(xps_ready, i + 1)
                    nc.vector.tensor_copy(xT[:, i * 4 * P:(i + 1) * 4 * P], xps[i % 2][:, :]).then_inc(xT_ready, 1)
                dve.wait_ge(mps_ready, 1)
                nc.vector.tensor_copy(mod[:, :, :, :], mps[:, :].rearrange("p (l j b) -> p l j b", l=2, j=6)).then_inc(mod_step, 1)
                dve.wait_ge(mod_step, 1)
                scales = mod[:, :, :, :].rearrange("p l (h j) b -> p l h j b", h=2)
                for layer in range(2):
                    nc.vector.tensor_scalar(scales[:, layer, :, 1, :], scales[:, layer, :, 1, :], 1.0, None, ALU.add).then_inc(mod_step, 1)
                    gate = scales[:, layer, :, 2, :]
                    nc.vector.tensor_scalar(gsign[:, layer], gate, 0.0, 2.0, ALU.is_ge, ALU.mult).then_inc(mod_step, 1)
                    nc.vector.scalar_tensor_tensor(gabs[:, layer], gate, -1.0, gate, ALU.mult, ALU.max).then_inc(mod_step, 1)
                    dve.wait_ge(mod_step, 5 * layer + 4)
                    nc.vector.tensor_scalar(gabs[:, layer], gabs[:, layer], 0.25, None, ALU.max).then_inc(mod_step, 1)
                    dve.wait_ge(mod_step, 5 * layer + 5)
                    nc.vector.scalar_tensor_tensor(gate, gsign[:, layer], -1.0, gabs[:, layer], ALU.add, ALU.mult).then_inc(mod_step, 1)


def zero_slots(nc, ctx, slots):
    zeros = ctx.enter_context(nc.sbuf_tensor("zeros", [P, SLOT_TILES * P], F32))
    cleared, zeroed = ctx.enter_context(nc.semaphore("cleared")), ctx.enter_context(nc.semaphore("zeroed"))

    def program(pool):
        nc.gpsimd.memset(zeros[:, :], 0.0).then_inc(cleared, 1)
        pool.wait_ge(cleared, 1)
        pool.dma_start(slots[0:SLOT_TILES * P, :].rearrange("(p n) d -> p (n d)", p=P), zeros[:, :]).then_inc(zeroed, 16)
        pool.wait_ge(zeroed, 16)
    return program


def layernorm_stage(nc, tag, W, xT, hT, scale, shift, prefetch=None, before=None, aside=None):
    center = W[:, OFF1["center"][0]:OFF1["center"][1]]
    mean = W[:, OFF1["mean"][0]:OFF1["mean"][0] + 1]
    eps = W[:, OFF1["eps"][0]:OFF1["eps"][1]]
    ident = W[:, OFF1["ident"][0]:OFF1["ident"][1]]
    with ExitStack() as ctx:
        sem = lambda name: ctx.enter_context(nc.semaphore(f"{tag}_{name}"))
        sb = lambda name, w: ctx.enter_context(nc.sbuf_tensor(f"{tag}_{name}", [P, w], F32))
        ps = lambda name, w: [ctx.enter_context(nc.psum_tensor(f"{tag}_{name}{i}", [P, w], F32)) for i in range(2)]
        sq = [sb(f"sq{i}", T) for i in range(2)]
        sd, rs = sb("sd", NT), sb("rs", NT)
        xc, rb, var = ps("xc", T), ps("rb", T), ps("var", 4)
        xc_ready, sq_ready, copied, var_ready, sd_ready = (
            sem("xc_ready"), sem("sq_ready"), sem("copied"), sem("var_ready"), sem("sd_ready"))
        rs_ready, rb_ready, scaled = sem("rs_ready"), sem("rb_ready"), sem("scaled")
        fetched = sem("fetched") if prefetch else None
        tile = lambda t, b: t[:, b * T:(b + 1) * T]
        four = lambda t, b: t[:, 4 * b:4 * b + 4]
        with nc.Block() as block:
            if prefetch:
                @block.sync
                def _(sp):
                    sp.dma_start(prefetch[0][:, :], prefetch[1]).then_inc(fetched, 16)
                    sp.wait_ge(fetched, 16)

            @block.tensor
            def _(pe):
                for n in range(B + 3):
                    if before and n < B:
                        before.pe(pe, n)
                    b = n - 1
                    if 0 <= b < B:
                        if before:
                            pe.wait_ge(before.x_ready, b + 1)
                        if b >= 2:
                            pe.wait_ge(copied, b - 1)
                        nc.tensor.matmul(xc[b % 2][:, :], center, tile(xT, b), start=True, stop=True).then_inc(xc_ready, 1)
                    b = n - 2
                    if 0 <= b < B:
                        pe.wait_ge(sq_ready, b + 1)
                        if b >= 2:
                            pe.wait_ge(sd_ready, b - 1)
                        for k in range(4):
                            last = nc.tensor.matmul(var[b % 2][:, k:k + 1], sq[b % 2][:, k * P:(k + 1) * P], mean, start=True, stop=True)
                        last.then_inc(var_ready, 1)
                    b = n - 3
                    if 0 <= b < B:
                        pe.wait_ge(rs_ready, b + 1)
                        if b >= 2:
                            pe.wait_ge(scaled, b - 1)
                        for k in range(4):
                            t = 4 * b + k
                            last = nc.tensor.matmul(rb[b % 2][:, k * P:(k + 1) * P], rs[:, t:t + 1].to_broadcast([P, P]), ident,
                                                    start=True, stop=True)
                        last.then_inc(rb_ready, 1)

            @block.scalar
            def _(act):
                for n in range(B + 4):
                    if before and n < B:
                        before.act(act, n)
                    b = n - 1
                    if 0 <= b < B:
                        act.wait_ge(copied, b + 1)
                        if b >= 2:
                            act.wait_ge(var_ready, b - 1)
                        nc.scalar.activation(sq[b % 2][:, :], tile(hT, b), ACT.Square).then_inc(sq_ready, 1)
                    b = n - 2
                    if 0 <= b < B:
                        act.wait_ge(var_ready, b + 1)
                        nc.scalar.activation(four(sd, b), var[b % 2][:, :], ACT.Sqrt, bias=eps).then_inc(sd_ready, 1)
                    b = n - 4
                    if 0 <= b < B:
                        act.wait_ge(scaled, b + 1)
                        nc.scalar.activation(tile(hT, b), tile(hT, b), ACT.Identity, bias=shift(b))

            @block.vector
            def _(dve):
                for n in range(B + 3):
                    if before and n < B:
                        before.dve(dve, n)
                    b = n - 1
                    if 0 <= b < B:
                        dve.wait_ge(xc_ready, b + 1)
                        nc.vector.tensor_copy(tile(hT, b), xc[b % 2][:, :]).then_inc(copied, 1)
                    b = n - 2
                    if 0 <= b < B:
                        dve.wait_ge(sd_ready, b + 1)
                        nc.vector.reciprocal(four(rs, b), four(sd, b)).then_inc(rs_ready, 1)
                    b = n - 3
                    if 0 <= b < B:
                        dve.wait_ge(rb_ready, b + 1)
                        dve.wait_ge(copied, b + 1)
                        dve.wait_ge(sq_ready, b + 1)
                        nc.vector.scalar_tensor_tensor(tile(hT, b), tile(hT, b), scale(b), rb[b % 2][:, :], ALU.mult, ALU.mult).then_inc(scaled, 1)

            if before or aside:
                @block.gpsimd
                def _(pool):
                    (before.pool if before else aside)(pool)


def mamba_inputs_stage(nc, W, hT, XP, convW, sel):
    w = lambda name: W[:, OFF1[name][0]:OFF1[name][1]]
    with ExitStack() as ctx:
        ps = [ctx.enter_context(nc.psum_tensor(f"xp_ps{i}", [P, T], F32)) for i in range(4)]
        sem = lambda name: ctx.enter_context(nc.semaphore(name))
        xp_ps_ready, xp_done, pool_done = sem("xp_ps_ready"), sem("xp_done"), sem("pool_done")
        with nc.Block() as block:
            @block.tensor
            def _(pe):
                with pe.Fori(0, B // 2) as i:
                    for k in range(4):
                        pe.wait_ge(xp_done, 4 * i + k + 1)
                        nc.tensor.matmul(ps[k][:, :], w("w_in")[:, (k % 2) * P:(k % 2 + 1) * P],
                                         hT[:, ds((2 * i + k // 2) * T, T)], start=True, stop=True).then_inc(xp_ps_ready, 1)

            @block.scalar
            def _(act):
                act.sem_inc(xp_done, 4)
                with act.Fori(0, B // 2) as i:
                    for k in range(4):
                        act.wait_ge(xp_ps_ready, 4 * i + k + 1)
                        src = ps[k][:, :] if k % 2 == 0 else ps[k][:, ::-1]
                        nc.scalar.activation(XP[:, ds((4 * i + k + 1) * XW + PAD, T)], src, ACT.Identity,
                                             bias=w("b_in")[:, k % 2:k % 2 + 1]).then_inc(xp_done, 1)

            @block.gpsimd
            def _(pool):
                nc.gpsimd.memset(XP[:, :].rearrange("p (u t) -> p u t", t=XW)[:, :, 0:PAD], 0.0).then_inc(pool_done, 1)
                for k in range(KC):
                    nc.gpsimd.tensor_tensor(convW[:, k, :], W[:, OFF1["m_in"][0]:OFF1["m_in"][0] + NCH * P],
                                            w("conv_w")[:, k * NCH * P:(k + 1) * NCH * P], ALU.mult).then_inc(pool_done, 1)
                nc.gpsimd.tensor_copy(sel[:, :, :], w("pick")[0:96, :].unsqueeze(2).to_broadcast([96, 32, P])).then_inc(pool_done, 1)


def mamba_stage(nc, W, XP, convW, negA, sel):
    w = lambda name: W[:, OFF1[name][0]:OFF1[name][1]]
    with ExitStack() as ctx:
        sb = lambda name, shape, dt=F32: ctx.enter_context(nc.sbuf_tensor(name, shape, dt))
        ps = lambda name: ctx.enter_context(nc.psum_tensor(name, [P, T], F32))
        sem = lambda name: ctx.enter_context(nc.semaphore(name))
        pre = sb("pre", [P, 4 * T])
        UZ = [sb(f"UZ{i}", [P, 4 * T]) for i in range(2)]
        xd = sb("xd", [P, T])
        ST = [sb(f"ST{i}", [96, T], BF16) for i in range(2)]
        r1 = sb("r1", [96, T])
        m1 = sb("m1", [96, T], BF16)
        xdt = sb("xdt", [P, NCH * T])
        ab = sb("ab", [P, NCH * T])
        DT = [sb(f"DT{i}", [P, NCH * T]) for i in range(2)]
        DU = [sb(f"DU{i}", [P, NCH * T]) for i in range(2)]
        CS = [sb(f"CS{i}", [P, T]) for i in range(4)]
        DA = [sb(f"DA{i}", [P, NCH * T]) for i in range(4)]
        DB = [sb(f"DB{i}", [P, NCH * T]) for i in range(2)]
        H = [sb(f"H{i}", [P, T]) for i in range(8)]
        PR = [sb(f"PR{i}", [P, T]) for i in range(8)]
        YZ = sb("YZ", [P, NCH * T])
        psB = [ps("psB0"), ps("psB1")]
        psC = [ps("psC0"), ps("psC1")]
        psY = [ps("psY0"), ps("psY1")]
        banks = [ps("pp0"), ps("pp1")]
        B_ready, C_ready, Y_done, pp_ready = sem("B_ready"), sem("C_ready"), sem("Y_done"), sem("pp_ready")
        pp_copied, silu_done, softplus_step, cs_ready, dA_ready = (
            sem("pp_copied"), sem("silu_done"), sem("softplus_step"), sem("cs_ready"), sem("dA_ready"))
        mult_done, scan_done, dt_ready, du_ready, fin_step, fin_done = (
            sem("mult_done"), sem("scan_done"), sem("dt_ready"), sem("du_ready"), sem("fin_step"), sem("fin_done"))
        prod_ready, rest_ready, split_step = sem("prod_ready"), sem("rest_ready"), sem("split_step")
        chunk = lambda t, c: t[:, c * T:(c + 1) * T]

        ORDER = (1, 2, 0, 3, 4, 5, 6, 7)
        place = lambda u, k: 0 if isinstance(u, int) and u == UNITS - 1 else ORDER.index(k)
        used = lambda u, k: 8 * u + 7 + place(u, k)
        bank = lambda u, k: banks[(k - 1 if u is None else 7 + place(u, k)) % 2]
        STEPS = {3: (1, 2), 4: (0,), 5: (3,), 6: (4,), 9: (5,), 11: (6,), 13: (7,)}

        def pe_step(pe, k, u, v, pv):
            pp = bank(u, k)
            if u is not None or k > 2:
                pe.wait_ge(pp_copied, (used(u, k) if u is not None else k - 1) - 1)
            if k == 0:
                pe.wait_ge(fin_done, u + 1)
                for c in range(NCH):
                    last = nc.tensor.matmul(pp[:, :], w("m_out")[:, c * P:(c + 1) * P], chunk(YZ, c), start=c == 0, stop=c == NCH - 1)
            elif k in (1, 2):
                for tap in range(KC):
                    last = nc.tensor.matmul(pp[:, :], convW[:, tap, (k - 1) * P:k * P], XP[:, ds((v + 1) * XW + tap, T)],
                                            start=tap == 0, stop=tap == KC - 1)
            elif k in (3, 4):
                last = nc.tensor.matmul(pp[:, :], w("m_in")[:, (k - 1) * P:k * P], XP[:, ds((v + 1) * XW + PAD, T)], start=True, stop=True)
            elif k == 5:
                pe.wait_ge(silu_done, v + 1)
                for c in range(NCH):
                    last = nc.tensor.matmul(pp[0:104, :], w("xproj")[:, c * 104:(c + 1) * 104], chunk(UZ[pv], c), start=c == 0, stop=c == NCH - 1)
            else:
                if k == 6:
                    pe.wait_ge(pp_copied, used(u, 5) + 1 if u is not None else 5)
                last = nc.tensor.matmul(pp[:, :], w("dt_w")[96:104, (k - 6) * P:(k - 5) * P], xd[96:104, :], start=True, stop=True)
            last.then_inc(pp_ready, 1)

        def pe_spread(pe, g, s, p, first):
            if not first or s >= 2:
                pe.wait_ge(mult_done, g - 1)
            nc.tensor.matmul(psB[s % 2][:, :], sel[:, s, :], ST[p][:, :], start=True, stop=True).then_inc(B_ready, 1)
            if not first or s >= 2:
                pe.wait_ge(cs_ready, g - 1)
            nc.tensor.matmul(psC[s % 2][:, :], sel[:, NS + s, :], ST[p][:, :], start=True, stop=True).then_inc(C_ready, 1)

        def pe_turn(pe, u, p, more):
            for j in range(3, NS + 3):
                if j < NS:
                    pe_spread(pe, 16 * u + j, j, p, False)
                elif more:
                    if j == NS:
                        pe.wait_ge(split_step, 3 * u + 6)
                    pe_spread(pe, 16 * u + j, j - NS, 1 - p, False)
                for k in STEPS.get(j, ()):
                    if more or k == 0:
                        pe_step(pe, k, u, u + 1, 1 - p)
                for c in range(NCH):
                    n = 2 * (j - 3) + c
                    pe.wait_ge(prod_ready, 32 * u + n + 9)
                    if j == 3:
                        pe.wait_ge(fin_step, 2 * u + c + 1)
                    nc.tensor.matmul(psY[c][:, :], w("ident"), PR[n % 8][:, :],
                                     start=j == 3, stop=j == NS + 2).then_inc(Y_done, 1)

        def act_step(act, k, u, v, pv):
            pp = bank(u, k)
            act.wait_ge(pp_ready, used(u, k) + 1 if u is not None else k)
            if k == 0:
                nc.scalar.copy(XP[:, ds(u * XW + PAD, T)], pp[:, ::-1] if pv else pp[:, :]).then_inc(pp_copied, 1)
            elif k <= 4:
                if u is not None:
                    act.wait_ge(silu_done, v)
                if k <= 2:
                    nc.scalar.activation(chunk(pre, k - 1), pp[:, :], ACT.Identity, bias=w("conv_b")[:, k - 1:k]).then_inc(pp_copied, 1)
                else:
                    nc.scalar.activation(chunk(pre, k - 1), pp[:, :], ACT.Identity).then_inc(pp_copied, 1)
            elif k == 5:
                if u is not None:
                    act.wait_ge(split_step, 3 * v)
                nc.scalar.copy(ST[pv][:, :], pp[0:96, :])
                nc.scalar.copy(xd[0:104, :], pp[0:104, :]).then_inc(pp_copied, 1)
            else:
                if u is not None:
                    act.wait_ge(dt_ready, v)
                nc.scalar.activation(chunk(xdt, k - 6), pp[:, :], ACT.Identity, bias=w("dt_b")[:, k - 6:k - 5]).then_inc(pp_copied, 1)
            if k == 4:
                act.wait_ge(pp_copied, used(u, 4) + 1 if u is not None else 4)
                if u is not None:
                    act.wait_ge(fin_done, u + 1)
                nc.scalar.activation(UZ[pv][:, :], pre[:, :], ACT.Silu).then_inc(silu_done, 1)
            if k == 7:
                act.wait_ge(pp_copied, used(u, 7) + 1 if u is not None else 7)
                nc.scalar.activation(ab[:, :], xdt[:, :], ACT.Abs).then_inc(softplus_step, 1)
                act.wait_ge(softplus_step, 3 * v + 1)
                nc.scalar.activation(ab[:, :], ab[:, :], ACT.Exp, scale=-1.0).then_inc(softplus_step, 1)
                act.wait_ge(softplus_step, 3 * v + 2)
                nc.scalar.activation(ab[:, :], ab[:, :], ACT.Ln, bias=1.0).then_inc(softplus_step, 1)

        def act_turn(act, u, p, more):
            for j in range(3, NS + 3):
                for k in STEPS.get(j - 1, ()):
                    if more or k == 0:
                        act_step(act, k, u, u + 1, 1 - p)
                if j < NS or more:
                    act_c(act, 16 * u + j, j % NS, False)
                if j + 1 < NS:
                    act_da(act, 16 * u + j + 1, j + 1, p, False)
                elif more:
                    if j + 1 == NS:
                        act.wait_ge(dt_ready, u + 2)
                    act_da(act, 16 * u + j + 1, j + 1 - NS, 1 - p, False)

        def act_c(act, g, s, first):
            act.wait_ge(C_ready, g + 1)
            if not first:
                act.wait_ge(prod_ready, 2 * g + 2)
            nc.scalar.copy(CS[s % 4][:, :], psC[s % 2][:, :]).then_inc(cs_ready, 1)

        def act_da(act, g, s, p, first):
            for c in range(NCH):
                if not first:
                    act.wait_ge(scan_done, 2 * g + c - 7)
                nc.scalar.activation(chunk(DA[s % 4], c), chunk(DT[p], c), ACT.Exp, scale=negA[:, c * NS + s:c * NS + s + 1]).then_inc(dA_ready, 1)

        def dve_state(dve, g, s, p, first):
            dve.wait_ge(B_ready, g + 1)
            if not first or s >= 2:
                dve.wait_ge(scan_done, 2 * g - 2)
            nc.vector.tensor_tensor(DB[s % 2][:, :].rearrange("p (c t) -> p c t", c=NCH),
                                    DU[p][:, :].rearrange("p (c t) -> p c t", c=NCH),
                                    psB[s % 2][:, :].unsqueeze(1).to_broadcast([P, NCH, T]), ALU.mult).then_inc(mult_done, 1)
            for c in range(NCH):
                dve.wait_ge(dA_ready, 2 * g + c + 1)
                if c == 0:
                    dve.wait_ge(mult_done, g + 1)
                dve.wait_ge(prod_ready, 2 * g + c + 1)
                nc.vector.tensor_tensor_scan(H[(2 * s + c) % 8][:, :], chunk(DA[s % 4], c), chunk(DB[s % 2], c), 0.0,
                                             ALU.mult, ALU.add).then_inc(scan_done, 1)

        def dve_dt(dve, v, pv):
            dve.wait_ge(softplus_step, 3 * v + 3)
            nc.vector.scalar_tensor_tensor(DT[pv][:, :], xdt[:, :], 0.0, ab[:, :], ALU.max, ALU.add).then_inc(dt_ready, 1)
            dve.wait_ge(dt_ready, v + 1)
            nc.vector.tensor_tensor(DU[pv][:, :], DT[pv][:, :], UZ[pv][:, 0:NCH * T], ALU.mult).then_inc(du_ready, 1)

        def dve_turn(dve, u, p, more):
            for j in range(3, NS + 3):
                if j < NS:
                    dve_state(dve, 16 * u + j, j, p, False)
                elif more:
                    if j == NS:
                        dve.wait_ge(du_ready, u + 2)
                    dve_state(dve, 16 * u + j, j - NS, 1 - p, False)
                if j == 13 and more:
                    dve_split(dve, u + 1, 1 - p)
                if j == 14 and more:
                    dve_dt(dve, u + 1, 1 - p)
            dve.wait_ge(Y_done, 32 * u + 40)
            dve.wait_ge(pp_ready, used(u, 0) + 1)
            for c in range(NCH):
                nc.vector.scalar_tensor_tensor(chunk(YZ, c), chunk(UZ[p], c), w("d_skip")[:, c:c + 1], psY[c][:, :],
                                               ALU.mult, ALU.add).then_inc(fin_step, 1)
            dve.wait_ge(fin_step, 2 * u + 4)
            nc.vector.tensor_tensor(YZ[:, :], YZ[:, :], UZ[p][:, NCH * T:], ALU.mult).then_inc(fin_done, 1)

        def pool_state(pool, g, s):
            for c in range(NCH):
                n = 2 * g + c
                pool.wait_ge(scan_done, n + 1)
                if c == 0:
                    pool.wait_ge(cs_ready, g + 1)
                pool.wait_ge(Y_done, n + 1)
                nc.gpsimd.tensor_tensor(PR[(2 * s + c) % 8][:, :], H[(2 * s + c) % 8][:, :], CS[s % 4][:, :], ALU.mult).then_inc(prod_ready, 1)

        def pool_split_rest(pool, pv, copied):
            pool.wait_ge(pp_copied, copied)
            nc.gpsimd.tensor_tensor(r1[:, :], xd[0:96, :], ST[pv][:, :], ALU.subtract).then_inc(rest_ready, 1)

        def dve_split(dve, v, pv):
            dve.wait_ge(rest_ready, v + 1)
            nc.vector.tensor_copy(m1[:, :], r1[:, :]).then_inc(split_step, 1)
            dve.wait_ge(split_step, 3 * v + 1)
            nc.vector.tensor_copy(ST[pv][32:64, :], m1[32:64, :]).then_inc(split_step, 1)
            nc.vector.tensor_tensor(ST[pv][64:96, :], r1[64:96, :], m1[64:96, :], ALU.subtract).then_inc(split_step, 1)

        def pool_turn(pool, u, p, more):
            for j in range(3, NS + 3):
                if j < NS:
                    pool_state(pool, 16 * u + j, j)
                elif more:
                    pool_state(pool, 16 * u + j, j - NS)
                if j == 11 and more:
                    pool_split_rest(pool, 1 - p, used(u, 5) + 1)

        with nc.Block() as block:
            @block.tensor
            def _(pe):
                pe.sem_inc(Y_done, 8)
                for k in range(1, 8):
                    pe_step(pe, k, None, 0, 0)
                pe.wait_ge(split_step, 3)
                for s in range(3):
                    pe_spread(pe, s, s, 0, True)
                with pe.Fori(0, B - 1) as i:
                    for p in range(2):
                        pe_turn(pe, 2 * i + p, p, True)
                pe_turn(pe, UNITS - 2, 0, True)
                pe_turn(pe, UNITS - 1, 1, False)
                pe.wait_ge(pp_copied, used(UNITS - 1, 0))
                pe.wait_ge(fin_done, UNITS + 1)
                for c in range(NCH):
                    last = nc.tensor.matmul(banks[0][:, :], w("m_out")[:, c * P:(c + 1) * P], chunk(YZ, c), start=c == 0, stop=c == NCH - 1)
                last.then_inc(pp_ready, 1)

            @block.scalar
            def _(act):
                for k in range(1, 8):
                    act_step(act, k, None, 0, 0)
                act.wait_ge(dt_ready, 1)
                for s in range(4):
                    act_da(act, s, s, 0, True)
                    if s < 3:
                        act_c(act, s, s, True)
                with act.Fori(0, B - 1) as i:
                    for p in range(2):
                        act_turn(act, 2 * i + p, p, True)
                act_turn(act, UNITS - 2, 0, True)
                act_turn(act, UNITS - 1, 1, False)
                act.wait_ge(pp_ready, used(UNITS - 1, 0) + 2)
                nc.scalar.copy(XP[:, UNITS * XW + PAD:UNITS * XW + PAD + T], banks[0][:, ::-1]).then_inc(pp_copied, 1)

            @block.vector
            def _(dve):
                dve.sem_inc(fin_step, 2)
                nc.vector.memset(YZ[:, :], 0.0).then_inc(fin_done, 1)
                dve_split(dve, 0, 0)
                dve_dt(dve, 0, 0)
                dve.wait_ge(du_ready, 1)
                for s in range(3):
                    dve_state(dve, s, s, 0, True)
                with dve.Fori(0, B - 1) as i:
                    for p in range(2):
                        dve_turn(dve, 2 * i + p, p, True)
                dve_turn(dve, UNITS - 2, 0, True)
                dve_turn(dve, UNITS - 1, 1, False)

            @block.gpsimd
            def _(pool):
                pool.sem_inc(prod_ready, 8)
                pool_split_rest(pool, 0, 5)
                for s in range(3):
                    pool_state(pool, s, s)
                with pool.Fori(0, B - 1) as i:
                    for p in range(2):
                        pool_turn(pool, 2 * i + p, p, True)
                pool_turn(pool, UNITS - 2, 0, True)
                pool_turn(pool, UNITS - 1, 1, False)


class MambaOutputs:
    def __init__(self, nc, ctx, W, XP, xT, gate):
        self.nc, self.W, self.XP, self.xT, self.gate = nc, W, XP, xT, gate
        self.ps = [ctx.enter_context(nc.psum_tensor(f"wo_ps{i}", [P, T], F32)) for i in range(2)]
        self.gated = [ctx.enter_context(nc.sbuf_tensor(f"wo_gated{i}", [P, T], F32)) for i in range(2)]
        sem = lambda name: ctx.enter_context(nc.semaphore(name))
        self.wo_ready, self.gated_ready, self.x_ready = sem("wo_ready"), sem("gated_ready"), sem("wo_x_ready")

    def pe(self, pe, b):
        w_out = self.W[:, OFF1["w_out"][0]:OFF1["w_out"][1]]
        if b >= 2:
            pe.wait_ge(self.gated_ready, b - 1)
        for k in range(2):
            at = (2 * b + 1 + k) * XW + PAD
            last = self.nc.tensor.matmul(self.ps[b % 2][:, :], w_out, self.XP[:, at:at + T], start=k == 0, stop=k == 1)
        last.then_inc(self.wo_ready, 1)

    def act(self, act, b):
        pass

    def dve(self, dve, b):
        dve.wait_ge(self.wo_ready, b + 1)
        if b >= 2:
            dve.wait_ge(self.x_ready, b - 1)
        self.nc.vector.tensor_scalar(self.gated[b % 2][:, :], self.ps[b % 2][:, :], self.W[:, OFF1["b_out"][0]:OFF1["b_out"][1]],
                                     self.gate(b), ALU.add, ALU.mult).then_inc(self.gated_ready, 1)

    def pool(self, pool):
        for b in range(B):
            pool.wait_ge(self.gated_ready, b + 1)
            x = self.xT[:, b * T:(b + 1) * T]
            self.nc.gpsimd.tensor_tensor(x, x, self.gated[b % 2][:, :], ALU.add).then_inc(self.x_ready, 1)


def route_stage(nc, W, W2, hT, slots, cw, gather_at):
    w = lambda name: W2[:, OFF2[name][0]:OFF2[name][1]]
    G = NT // GT
    with ExitStack() as ctx:
        sb = lambda name, shape, dt=F32: ctx.enter_context(nc.sbuf_tensor(name, shape, dt))
        sem = lambda name: ctx.enter_context(nc.semaphore(name))
        htok = sb("htok", [P, NT, P])
        scatter_at = sb("scatter_at", [P, NT], U32)
        two = lambda name, shape: [sb(f"{name}{i}", shape) for i in range(2)]
        lm, ex, sc, key, oh = (two(name, [P, GT, E0]) for name in ("lm", "ex", "scs", "key", "oh"))
        mx, sm, top, m8 = (two(name, [P, GT]) for name in ("mx", "sm", "top", "m8"))
        pos = sb("pos", [P, GT, E0])
        tot, incl, base = sb("tot", [P, E0, GT]), sb("incl", [P, E0, GT]), sb("base", [P, E0])
        rank, ok, slot, send = (sb(name, [P, GT]) for name in ("rank", "ok", "slot", "send"))
        ps = lambda name, shape: [ctx.enter_context(nc.psum_tensor(f"{name}{i}", shape, F32)) for i in range(2)]
        psL, psPN, tps = ps("psL", [P, GT, E0]), ps("psPN", [P, 2, GT * E0]), ps("tps", [P, 4, P])
        logits_ready, tps_ready, htok_ready = sem("logits_ready"), sem("tps_ready"), sem("htok_ready")
        lm_ready, ex_ready, oh_ready, count_ready, step, counted, scatter_ready, scattered = (
            sem("lm_ready"), sem("ex_ready"), sem("oh_ready"), sem("count_ready"), sem("route_step"), sem("counted"),
            sem("scatter_ready"), sem("scattered"))
        by_expert = lambda t: t[:, :].unsqueeze(2).to_broadcast([P, GT, E0])
        with nc.Block() as block:
            @block.tensor
            def _(pe):
                for n in range(G + 1):
                    if n < G:
                        if n >= 2:
                            pe.wait_ge(lm_ready, n - 1)
                        for k in range(GT):
                            t = GT * n + k
                            last = nc.tensor.matmul(psL[n % 2][:, k, :], hT[:, t * P:(t + 1) * P], w("wg"), start=True, stop=True)
                        last.then_inc(logits_ready, 1)
                    if n >= 1:
                        q = n - 1
                        pe.wait_ge(oh_ready, q + 1)
                        if q >= 2:
                            pe.wait_ge(counted, q - 1)
                        flat = oh[q % 2][:, :, :].rearrange("p t e -> p (t e)")
                        nc.tensor.matmul(psPN[q % 2][:, 0, :], w("tri"), flat, start=True, stop=True)
                        nc.tensor.matmul(psPN[q % 2][:, 1, :], w("ones"), flat, start=True, stop=True).then_inc(count_ready, 1)
                    if n < G:
                        for i in range(n * GT // 4, (n + 1) * GT // 4):
                            if i >= 2:
                                pe.wait_ge(htok_ready, i - 1)
                            for k in range(4):
                                t = 4 * i + k
                                last = nc.tensor.transpose(tps[i % 2][:, k, :], hT[:, t * P:(t + 1) * P], W[:, 0:P])
                            last.then_inc(tps_ready, 1)

            @block.scalar
            def _(act):
                for q in range(G):
                    act.wait_ge(lm_ready, q + 1)
                    nc.scalar.activation(ex[q % 2][:, :, :], lm[q % 2][:, :, :], ACT.Exp).then_inc(ex_ready, 1)
                    for i in range(q * GT // 4, (q + 1) * GT // 4):
                        act.wait_ge(tps_ready, i + 1)
                        nc.scalar.copy(htok[:, 4 * i:4 * i + 4, :], tps[i % 2][:, :, :]).then_inc(htok_ready, 1)

            @block.vector
            def _(dve):
                done = [0]
                v = nc.vector

                def then(ins):
                    done[0] += 1
                    ins.then_inc(step, 1)
                    dve.wait_ge(step, done[0])

                def choose(q):
                    p = q % 2
                    dve.wait_ge(logits_ready, q + 1)
                    then(v.tensor_reduce(mx[p][:, :], psL[p][:, :, :], AX.X, ALU.max))
                    v.tensor_tensor(lm[p][:, :, :], psL[p][:, :, :], by_expert(mx[p]), ALU.subtract).then_inc(lm_ready, 1)
                    dve.wait_ge(ex_ready, q + 1)
                    then(v.tensor_reduce(sm[p][:, :], ex[p][:, :, :], AX.X, ALU.add))
                    then(v.reciprocal(sm[p][:, :], sm[p][:, :]))
                    then(v.tensor_tensor(sc[p][:, :, :], ex[p][:, :, :], by_expert(sm[p]), ALU.mult))
                    then(v.tensor_reduce(top[p][:, :], sc[p][:, :, :], AX.X, ALU.max))
                    then(v.tensor_tensor(key[p][:, :, :], sc[p][:, :, :], by_expert(top[p]), ALU.is_ge))
                    then(v.tensor_tensor(key[p][:, :, :], key[p][:, :, :], w("ramp").unsqueeze(1).to_broadcast([P, GT, E0]), ALU.mult))
                    then(v.tensor_reduce(m8[p][:, :], key[p][:, :, :], AX.X, ALU.max))
                    v.tensor_tensor(oh[p][:, :, :], key[p][:, :, :], by_expert(m8[p]), ALU.is_equal).then_inc(oh_ready, 1)

                def place(q):
                    p, tiles = q % 2, slice(GT * q, GT * q + GT)
                    flat = lambda t: t[:, :, :].rearrange("p e t -> p (e t)")
                    dve.wait_ge(count_ready, q + 1)
                    dve.wait_ge(oh_ready, q + 1)
                    then(v.tensor_copy(tot[:, :, :], psPN[p][:, 1, :].rearrange("p (t e) -> p e t", e=E0)))
                    then(v.tensor_tensor_scan(flat(incl), w("not_first")[:, 0:E0 * GT], flat(tot), 0.0, ALU.mult, ALU.add))
                    then(v.tensor_tensor(tot[:, :, :], incl[:, :, :], tot[:, :, :], ALU.subtract))
                    then(v.tensor_tensor(tot[:, :, :], tot[:, :, :], base[:, :].unsqueeze(2).to_broadcast([P, E0, GT]), ALU.add))
                    v.tensor_tensor(pos[:, :, :], psPN[p][:, 0, :].rearrange("p (t e) -> p t e", e=E0),
                                    tot[:, :, :].rearrange("p e t -> p t e"), ALU.add).then_inc(counted, 1)
                    then(v.tensor_tensor(base[:, :], base[:, :], incl[:, :, GT - 1], ALU.add))
                    dve.wait_ge(counted, q + 1)
                    then(v.tensor_tensor(pos[:, :, :], pos[:, :, :], oh[p][:, :, :], ALU.mult))
                    then(v.tensor_reduce(rank[:, :], pos[:, :, :], AX.X, ALU.add))
                    then(v.tensor_scalar(ok[:, :], rank[:, :], float(CAP), None, ALU.is_le))
                    then(v.tensor_scalar(slot[:, :], m8[p][:, :], float(-CAP), float(E0 * CAP - 1), ALU.mult, ALU.add))
                    then(v.tensor_tensor(slot[:, :], slot[:, :], rank[:, :], ALU.add))
                    then(v.tensor_tensor(send[:, :], slot[:, :], w("overflow")[:, tiles], ALU.subtract))
                    then(v.tensor_tensor(send[:, :], send[:, :], ok[:, :], ALU.mult))
                    then(v.tensor_tensor(send[:, :], send[:, :], w("overflow")[:, tiles], ALU.add))
                    v.tensor_copy(scatter_at[:, tiles], send[:, :]).then_inc(scatter_ready, 1)
                    then(v.tensor_tensor(cw[:, tiles], top[p][:, :], ok[:, :], ALU.mult))
                    then(v.tensor_scalar(slot[:, :], slot[:, :], float(SLOTS - 1), None, ALU.min))
                    then(v.tensor_copy(gather_at[:, tiles], slot[:, :]))

                then(v.memset(base[:, :], 0.0))
                for n in range(G + 1):
                    if n < G:
                        choose(n)
                    if n >= 1:
                        place(n - 1)

            @block.gpsimd
            def _(pool):
                for q in range(G):
                    pool.wait_ge(htok_ready, (q + 1) * GT // 4)
                    pool.wait_ge(scatter_ready, q + 1)
                    for t in range(GT * q, GT * q + GT):
                        nc.gpsimd.indirect_dma_start(slots, bass.IndirectOffsetOnAxis(ap=scatter_at[:, t:t + 1], axis=0),
                                                     htok[:, t, :], None).then_inc(scattered, 16)
                pool.wait_ge(scattered, 16 * NT)


def experts_stage(nc, W, W2, slots, results, w1, b1, w2):
    w = lambda name: W2[:, OFF2[name][0]:OFF2[name][1]]
    NF = F0 // P
    parts = [(0, HALF), (HALF, CAP - HALF)]
    with ExitStack() as ctx:
        sb = lambda name, shape, dt=F32: ctx.enter_context(nc.sbuf_tensor(name, shape, dt))
        sem = lambda name: ctx.enter_context(nc.semaphore(name))
        stok = sb("stok", [P, SLOT_TILES, P])
        sT = sb("sT", [P, SLOT_TILES * P])
        W1R = [sb(f"W1R{i}", [P, F0]) for i in range(2)]
        B1R = [sb(f"B1R{i}", [P, NF]) for i in range(2)]
        W2R = [sb(f"W2R{i}", [P, NF, P]) for i in range(2)]
        hs = [sb(f"hs{i}", [P, NF, CAP]) for i in range(2)]
        yt = sb("yt", [P, E0 * RT * P])
        tps = [ctx.enter_context(nc.psum_tensor(f"stp{i}", [P, 4, P], F32)) for i in range(2)]
        psH = [ctx.enter_context(nc.psum_tensor(f"psH{i}", [P, HALF], F32)) for i in range(4)]
        psO = [ctx.enter_context(nc.psum_tensor(f"psO{i}", [P, P], F32)) for i in range(2)]
        s_loaded = [sem(f"s_loaded{i}") for i in range(4)]
        w_loaded = [sem(f"ew_loaded{i}") for i in range(2)]
        tps_ready, sT_ready, H_ready, hs_ready, O_ready, yt_ready = (
            sem("stp_ready"), sem("sT_ready"), sem("H_ready"), sem("hs_ready"), sem("O_ready"), sem("yt_ready"))
        stored = sem("y_stored")
        groups = [range(i, min(i + 4, SLOT_TILES)) for i in range(0, SLOT_TILES, 4)]
        cuts = [0, 12, 24, 36, SLOT_TILES]
        src = slots[0:SLOT_TILES * P, :].rearrange("(n p) d -> p n d", p=P)
        with nc.Block() as block:
            @block.sync
            def _(sp):
                for i in range(4):
                    sp.dma_start(stok[:, cuts[i]:cuts[i + 1], :], src[:, cuts[i]:cuts[i + 1], :]).then_inc(s_loaded[i], 16)
                with sp.Fori(0, E0 // 2) as i:
                    for q in range(2):
                        e = 2 * i + q
                        sp.wait_ge(O_ready, RT * e + RT)
                        sp.dma_start(W1R[q][:, :], w1[ds(e * P, P), :]).then_inc(w_loaded[q], 16)
                        sp.dma_start(B1R[q][:, :], b1[ds(e * P, P), :]).then_inc(w_loaded[q], 16)
                        sp.dma_start(W2R[q][:, :, :], w2[ds(e * F0, F0), :].rearrange("(c p) d -> p c d", p=P)).then_inc(w_loaded[q], 16)

            @block.tensor
            def _(pe):
                pe.sem_inc(O_ready, 2 * RT)
                pe.sem_inc(H_ready, 8)
                for g, tiles in enumerate(groups):
                    if tiles[0] in cuts:
                        pe.wait_ge(s_loaded[cuts.index(tiles[0])], 16)
                    if g >= 2:
                        pe.wait_ge(sT_ready, g - 1)
                    for k, t in enumerate(tiles):
                        if t in cuts:
                            pe.wait_ge(s_loaded[cuts.index(t)], 16)
                        last = nc.tensor.transpose(tps[g % 2][:, k, :], stok[:, t, :], W[:, 0:P])
                    last.then_inc(tps_ready, 1)
                pe.wait_ge(sT_ready, len(groups))
                with pe.Fori(0, E0 // 2) as i:
                    for q in range(2):
                        pe.wait_ge(w_loaded[q], 48 * i + 48)
                        for n, (at, wide) in enumerate(parts):
                            for f in range(NF):
                                k = 16 * i + 8 * q + 4 * n + f
                                pe.wait_ge(hs_ready, k + 1)
                                nc.tensor.matmul(psH[f][:, 0:wide], W1R[q][:, f * P:(f + 1) * P],
                                                 sT[:, ds((2 * i + q) * CAP + at, wide)], start=True, stop=True).then_inc(H_ready, 1)
                    for q in range(2):
                        pe.wait_ge(hs_ready, 16 * i + 8 * q + 12)
                        for r in range(RT):
                            rows = min(ROWS, CAP - r * ROWS)
                            pe.wait_ge(yt_ready, RT * (2 * i + q) + r + 1)
                            for f in range(NF):
                                last = nc.tensor.matmul(psO[r % 2][0:rows, :], hs[q][:, f, r * ROWS:r * ROWS + rows],
                                                        W2R[q][:, f, :], start=f == 0, stop=f == NF - 1)
                            last.then_inc(O_ready, 1)

            @block.scalar
            def _(act):
                act.sem_inc(hs_ready, 4)
                with act.Fori(0, E0 // 2) as i:
                    for q in range(2):
                        act.wait_ge(O_ready, RT * (2 * i + q) + RT)
                        for n, (at, wide) in enumerate(parts):
                            for f in range(NF):
                                act.wait_ge(H_ready, 16 * i + 8 * q + 4 * n + f + 9)
                                nc.scalar.activation(hs[q][:, f, at:at + wide], psH[f][:, 0:wide], ACT.Gelu,
                                                     bias=B1R[q][:, f:f + 1]).then_inc(hs_ready, 1)

            @block.vector
            def _(dve):
                for g, tiles in enumerate(groups):
                    dve.wait_ge(tps_ready, g + 1)
                    nc.vector.tensor_copy(sT[:, tiles[0] * P:(tiles[-1] + 1) * P],
                                          tps[g % 2][:, 0:len(tiles), :].rearrange("p k t -> p (k t)")).then_inc(sT_ready, 1)
                dve.sem_inc(yt_ready, 2)
                with dve.Fori(0, E0 // 2) as i:
                    for q in range(2):
                        for r in range(RT):
                            rows = min(ROWS, CAP - r * ROWS)
                            dve.wait_ge(O_ready, RT * (2 * i + q) + r + 1 + 2 * RT)
                            nc.vector.tensor_tensor(yt[0:rows, ds(((2 * i + q) * RT + r) * P, P)], psO[r % 2][0:rows, :],
                                                    w("b2")[0:rows, ds((2 * i + q) * P, P)], ALU.add).then_inc(yt_ready, 1)

            @block.gpsimd
            def _(pool):
                with pool.Fori(0, E0 // 2) as i:
                    for q in range(2):
                        pool.wait_ge(yt_ready, RT * (2 * i + q + 1) + 2)
                        full = (RT - 1) * ROWS
                        pool.dma_start(results[ds((2 * i + q) * CAP, full), :].rearrange("(r p) d -> p r d", p=ROWS),
                                       yt[0:ROWS, ds((2 * i + q) * RT * P, (RT - 1) * P)].rearrange("p (r d) -> p r d", d=P)).then_inc(stored, 16)
                        pool.dma_start(results[ds((2 * i + q) * CAP + full, CAP - full), :],
                                       yt[0:CAP - full, ds(((2 * i + q) * RT + RT - 1) * P, P)]).then_inc(stored, 16)
                pool.wait_ge(stored, 32 * E0)


class Combine:
    def __init__(self, nc, ctx, W, results, cw, gather_at, xT, gate):
        self.nc, self.W, self.results, self.cw, self.gather_at, self.xT, self.gate = nc, W, results, cw, gather_at, xT, gate
        sb = lambda name: ctx.enter_context(nc.sbuf_tensor(name, [P, NT, P], F32))
        sem = lambda name: ctx.enter_context(nc.semaphore(name))
        self.gtok, self.weighted = sb("gtok"), sb("weighted")
        self.ps = [ctx.enter_context(nc.psum_tensor(f"gps{i}", [P, T], F32)) for i in range(2)]
        self.gathered = [sem(f"gathered{i}") for i in range(B)]
        self.weighted_ready, self.ps_ready, self.x_ready = sem("weighted_ready"), sem("gps_ready"), sem("g_x_ready")

    def pool(self, pool):
        for t in range(NT):
            self.nc.gpsimd.indirect_dma_start(self.gtok[:, t, :], None, self.results,
                                              bass.IndirectOffsetOnAxis(ap=self.gather_at[:, t:t + 1], axis=0)
                                              ).then_inc(self.gathered[t // 4], 16)

    def act(self, act, b):
        act.wait_ge(self.gathered[b], 64)
        for t in range(4 * b, 4 * b + 4):
            self.nc.scalar.activation(self.weighted[:, t, :], self.gtok[:, t, :], ACT.Copy,
                                      scale=self.cw[:, t:t + 1]).then_inc(self.weighted_ready, 1)

    def pe(self, pe, b):
        pe.wait_ge(self.weighted_ready, 4 * b + 4)
        if b >= 2:
            pe.wait_ge(self.x_ready, b - 1)
        for k in range(4):
            last = self.nc.tensor.transpose(self.ps[b % 2][:, k * P:(k + 1) * P], self.weighted[:, 4 * b + k, :], self.W[:, 0:P])
        last.then_inc(self.ps_ready, 1)

    def dve(self, dve, b):
        dve.wait_ge(self.ps_ready, b + 1)
        x = self.xT[:, b * T:(b + 1) * T]
        self.nc.vector.scalar_tensor_tensor(x, self.ps[b % 2][:, :], self.gate(b), x, ALU.mult, ALU.add).then_inc(self.x_ready, 1)


def attention_stage(nc, W, W3, tiles, scratch_q, scratch_k, m_scratch, hT, xT, identb, gate):
    w = lambda name: W3[:, OFF3[name][0]:OFF3[name][1]]
    ident = W[:, 0:P]
    MROW = 72
    KR = MROW + 3
    PAIRS = HEADS // 2
    UNITS_T = 5 * PAIRS
    BEFORE, EACH = 11, 13
    with ExitStack() as ctx:
        sb = lambda name, shape, dt=F32: ctx.enter_context(nc.sbuf_tensor("a_" + name, shape, dt))
        ps = lambda name: ctx.enter_context(nc.psum_tensor("a_" + name, [P, T], F32))
        sem = lambda name: ctx.enter_context(nc.semaphore("a_" + name))
        mqk, mkq = sb("mqk", [P, P], BF16), sb("mkq", [P, P], BF16)
        qst = [sb(f"qst{i}", [KR, HEADS * T], BF16) for i in range(2)]
        kst = [sb(f"kst{i}", [KR, HEADS * T], BF16) for i in range(2)]
        parts = [sb(f"parts{x}", [P, 3, T], BF16) for x in "qk"]
        TA, TB, QR, R, HB = (tiles[:, i * T:(i + 1) * T] for i in range(5))
        VA = [sb(f"VA{i}", [P, QT, HEADS, 32]) for i in range(2)]
        PT = [[sb(f"PT{i}{u}", [P, T]) for u in range(5)] for i in range(4)]
        OT = [sb(f"OT{i}", [P, T]) for i in range(2)]
        OTK, OF = sb("OTK", [P, QT, P]), sb("OF", [P, T])
        rec = sb("rec", [P, QT, 4])
        MX, NR = sb("MX", [P, QT, HEADS]), sb("NR", [P, QT, HEADS // 2])
        NMB = sb("NMB", [P, QT, 3, HEADS // 2], BF16)
        MTS = [sb(f"MTS{i}", [24, T], BF16) for i in range(2)]
        psM = [ps("psM0"), ps("psM1")]
        psS = [ps(f"psS{i}") for i in range(4)]
        psO, mb = ps("psO"), ps("mb")
        mb_ready, S_ready, M_ready, PV_done = sem("mb_ready"), sem("S_ready"), sem("M_ready"), sem("PV_done")
        mb_used, M_used, m_step, x_done = sem("mb_used"), sem("M_used"), sem("m_step"), sem("x_done")
        E_done, O_copied, part_step, hb_ready, act_init = sem("E_done"), sem("O_copied"), sem("part_step"), sem("hb_ready"), sem("act_init")
        rope_step, pool_init = sem("rope_step"), sem("pool_init")
        ones_ready, ones_loaded = sem("ones_ready"), sem("ones_loaded")
        ones3 = sb("ones3", [3, T], BF16)
        st_loaded = [sem("st_loaded0"), sem("st_loaded1")]
        parts_stored, m_stored = sem("parts_stored"), [sem("m_storedA"), sem("m_storedB")]
        m_loaded = [sem("m_loadedA"), sem("m_loadedB")]

        def groups(half):
            first = half * HEADS // 2
            return [(j, first + h, n) for j, n in ((0, 4), (1, 2), (2, 1), (3, 1)) for h in range(0, HEADS // 2, n)]

        NG = len(groups(0))
        M_SLOTS = {2: (0, 0, 6), 3: (0, 6, 12), 4: (0, 12, 17), 5: (0, 17, NG), 6: (1, 0, 8), 7: (1, 8, 15), 8: (1, 15, NG)}
        BLOCKS = [[(0, 0, 0)], [(0, 1, 0), (0, 3, 384)], [(1, 0, 0)], [(1, 1, 0), (1, 3, 384)], [(0, 2, 0), (1, 2, 256)]]
        PLACE = {(h, i): (u, col) for u, bank in enumerate(BLOCKS) for h, i, col in bank}
        EARLY = {2: ["q"], 3: ["q_swap"], 4: ["k"], 5: ["k_swap", "G1"], 7: ["G2"], 9: ["MB", "G3"]}
        LATE = {3: ["G0"], 4: ["V"], 6: ["MA"]}
        TAIL = ["F", "O"]
        PART_SLOTS = {4: 0, 5: 1, 6: 2, 7: 3}
        SLOTS_T = range(2, PAIRS + 2)

        def uses(more_p, more_m):
            order = [x for slot in SLOTS_T for x in EARLY.get(slot, []) + LATE.get(slot, [])] + TAIL
            kept = [x for x in order if (more_p or x[0] not in "qk") and (more_m or x not in ("V", "MA", "MB"))]
            return {x: n for n, x in enumerate(kept)}

        def slot_items(c, slot):
            early = [x for x in EARLY.get(slot, []) if x in c.use]
            half, a, b = M_SLOTS[slot] if slot in M_SLOTS and c.more_m else (0, 0, 0)
            maxima = [(half, g) for g in range(a, b)]
            items = []
            while early or maxima:
                items += early[:1] + maxima[:2]
                early, maxima = early[1:], maxima[2:]
            return items + [x for x in LATE.get(slot, []) if x in c.use]

        class Turn:
            def __init__(self, t, p, base, more_p=True, more_m=True):
                self.t, self.p, self.base, self.more_p, self.more_m = t, p, base, more_p, more_m
                self.use = uses(more_p, more_m)

        def turns(eng, body):
            with eng.Fori(0, 3) as i:
                for p in range(2):
                    body(Turn(2 * i + p, p, BEFORE + EACH * (2 * i + p)))
            at = BEFORE + EACH * 6
            last = Turn(6, 0, at, more_p=False)
            body(last)
            body(Turn(7, 1, at + len(last.use), more_p=False, more_m=False))

        def pe_use(pe, name, n, t2, p1):
            if n is not None:
                pe.wait_ge(mb_used, n)
            if name[0] in "qk":
                last = nc.tensor.matmul(mb[:, :], w("w" + name), hT[:, ds(t2 * T, T)], start=True, stop=True)
            elif name == "V":
                for i in range(QT):
                    last = nc.tensor.matmul(mb[:, i * P:(i + 1) * P], HB[:, i * P:(i + 1) * P], w("wv"), start=True, stop=True)
            elif name[0] == "G":
                for j in range(QT):
                    last = nc.tensor.transpose(mb[:, j * P:(j + 1) * P], OT[int(name[1]) % 2][:, j * P:(j + 1) * P], ident)
            elif name[0] == "M":
                rows = mb[:, 0:T // 2].bitcast(BF16)
                for j in range(QT):
                    last = nc.tensor.transpose(rows[0:24, j * P:(j + 1) * P], NMB[:, j, :, :].rearrange("p s h -> p (s h)"), identb[:, :])
            elif name == "F":
                for j in range(QT):
                    last = nc.tensor.transpose(mb[:, j * P:(j + 1) * P], OTK[:, j, :], ident)
            else:
                last = nc.tensor.matmul(mb[:, :], w("wo"), OF[:, :], start=True, stop=True)
            last.then_inc(mb_ready, 1)

        def pe_scores(pe, t, p, k, u):
            n = UNITS_T * t + 5 * k + u
            if not isinstance(n, int) or n >= 4:
                pe.wait_ge(E_done, n - 3)
            for h, i, col in BLOCKS[u]:
                wide, at = T - i * P, (2 * k + h) * T
                out = psS[(5 * k + u) % 4][:, col:col + wide]
                nc.tensor.matmul(out, kst[p][:, at + i * P:at + (i + 1) * P], qst[p][:, at + i * P:at + T], start=True, stop=False)
                last = nc.tensor.matmul(out[:, 0:P], identb[:, :], mkq[:, :], start=False, stop=True)
            last.then_inc(S_ready, 1)

        def pe_maxima(pe, n0, p, half, a, b):
            for g, (j, h0, nh) in enumerate(groups(half)[a:b]):
                n = n0 + g
                if not isinstance(n, int) or n >= 2:
                    pe.wait_ge(M_used, n - 1)
                wide = (j + 1) * P
                for x in range(nh):
                    at = (h0 + x) * T
                    out = psM[(half * NG + a + g) % 2][:, x * wide:(x + 1) * wide]
                    nc.tensor.matmul(out, qst[p][0:72, at + j * P:at + (j + 1) * P], kst[p][0:72, at:at + wide], start=True, stop=False)
                    last = nc.tensor.matmul(out[:, j * P:wide], identb[:, :], mqk[:, :], start=False, stop=True)
                last.then_inc(M_ready, 1)

        def pe_values(pe, t, p, g, i):
            if i == 0:
                pe.wait_ge(E_done, UNITS_T * t + 10 * g + 10)
                if g == 0:
                    pe.wait_ge(mb_used, 9 if isinstance(t, int) and t == 0 else v_used(t))
                n = 4 * t + g
                if not isinstance(n, int) or n >= 1:
                    pe.wait_ge(O_copied, n + 1)
            for c in range(4):
                u, col = PLACE[(c % 2, i)]
                last = nc.tensor.matmul(psO[32 * c:32 * c + 32, i * P:T], VA[p][:, i, 4 * g + c, :],
                                        PT[(2 * g + c // 2) % 4][u][:, col:col + T - i * P], start=i == 0, stop=i == QT - 1)
            if i == QT - 1:
                last.then_inc(PV_done, 1)

        V_AT = uses(True, True)["V"]
        v_used = lambda t: BEFORE + EACH * (t - 1) + V_AT + 1 if isinstance(t, int) else EACH * t + (BEFORE - EACH + V_AT + 1)

        def pe_turn(pe, c):
            for slot in SLOTS_T:
                fill = []
                if slot < PAIRS:
                    fill += [("S", c.t, c.p, slot, u) for u in range(5)]
                elif c.more_m:
                    fill += [("S", c.t + 1, 1 - c.p, slot - PAIRS, u) for u in range(5)]
                if slot % 2 == 0:
                    fill += [("V", c.t, c.p, slot // 2 - 1, i) for i in range(QT)]
                items = slot_items(c, slot)
                if slot == 4:
                    pe.wait_ge(m_loaded[1], 16 * c.t + 16)
                if slot == PAIRS and c.more_m:
                    pe.wait_ge(m_loaded[0], 16 * c.t + 32)
                late = 7 if slot == 2 else 0
                for n in range(max(len(fill), len(items) + late)):
                    if n < len(fill):
                        (pe_scores if fill[n][0] == "S" else pe_values)(pe, *fill[n][1:])
                    if late and n == late and c.more_m:
                        pe.wait_ge(st_loaded[1 - c.p], st_count(c.t + 1, 1 - c.p))
                    if late <= n < len(items) + late:
                        if isinstance(items[n - late], str):
                            pe_turn_use(pe, c, items[n - late])
                        else:
                            half, g = items[n - late]
                            pe_maxima(pe, 2 * NG * (c.t + 1) + half * NG + g, 1 - c.p, half, g, g + 1)
            for name in TAIL:
                pe_turn_use(pe, c, name)

        LOADS = 4 * 16
        def st_count(t, p):
            if isinstance(t, int):
                return LOADS * (t // 2 + 1)
            return LOADS // 2 * t + (LOADS if p == 0 else LOADS // 2)

        def pe_turn_use(pe, c, name):
            if name not in c.use:
                return
            if name[0] == "G":
                pe.wait_ge(O_copied, 4 * c.t + int(name[1]) + 2)
            if name == "V":
                pe.wait_ge(hb_ready, c.t + 2)
            if name in ("MA", "MB"):
                pe.wait_ge(m_step, 10 * (c.t + 1) + (5 if name == "MA" else 10))
            pe_use(pe, name, c.base + c.use[name], c.t + 2, 1 - c.p)

        def act_exps(act, t, k):
            for u in range(5):
                n = UNITS_T * t + 5 * k + u
                act.wait_ge(S_ready, n + 1)
                if u == 0:
                    pair = PAIRS * t + k
                    if not isinstance(pair, int) or pair >= 4:
                        act.wait_ge(PV_done, 4 * t + k // 2)
                nc.scalar.activation(PT[k % 4][u][:, :], psS[(5 * k + u) % 4][:, :], ACT.Exp, scale=DK ** -0.5).then_inc(E_done, 1)

        def act_part(act, b, step):
            x = step // 2
            act.wait_ge(rope_step, 6 * b + 3 * x + 1 + step % 2)
            if step == 0:
                if not isinstance(b, int) or b >= 1:
                    act.wait_ge(parts_stored, 64 * b)
            nc.scalar.copy(parts[x][:, step % 2, :], (QR if step % 2 == 0 else R)[:, :]).then_inc(part_step, 1)

        def act_turn(act, c):
            for slot in SLOTS_T:
                if slot < PAIRS:
                    act_exps(act, c.t, slot)
                elif c.more_m:
                    act_exps(act, c.t + 1, slot - PAIRS)
                if slot == 2 and c.more_m:
                    act.wait_ge(mb_ready, 9 if isinstance(c.t, int) and c.t == 0 else v_used(c.t))
                    nc.scalar.copy(HB[:, :], hT[:, ds((c.t + 1) * T, T)]).then_inc(hb_ready, 1)
                if slot in PART_SLOTS and c.more_p:
                    act_part(act, c.t + 2, PART_SLOTS[slot])
                if slot % 2 == 0:
                    g = 4 * c.t + slot // 2 - 1
                    act.wait_ge(PV_done, g + 2)
                    if slot <= 4:
                        act.wait_ge(mb_ready, turn_base_before(c, slot // 2 + 1))
                    else:
                        act.wait_ge(mb_ready, c.base + c.use[f"G{slot // 2 - 3}"] + 1)
                    nc.scalar.copy(OT[(slot // 2 - 1) % 2][:, :], psO[:, :]).then_inc(O_copied, 1)

        def turn_base_before(c, g):
            if isinstance(c.t, int) and c.t == 7:
                prev = uses(False, True)
                return c.base - len(prev) + prev[f"G{g}"] + 1
            prev = uses(True, True)
            return c.base - EACH + prev[f"G{g}"] + 1

        def dve_maxima(dve, n0, t1, half, a, b):
            for g, (j, h0, nh) in enumerate(groups(half)[a:b]):
                dve.wait_ge(M_ready, n0 + g + 1)
                if a + g == 0 and (not isinstance(t1, int) or t1 > 0):
                    dve.wait_ge(m_step, 10 * t1 - 9 + 5 * half)
                src = psM[(half * NG + a + g) % 2][:, 0:nh * (j + 1) * P].rearrange("p (h k) -> p h k", h=nh)
                nc.vector.tensor_reduce(MX[:, j, h0:h0 + nh], src, AX.X, ALU.max).then_inc(M_used, 1)
            if b == NG:
                hs = slice(half * 8, half * 8 + 8)
                at = 10 * t1 + 5 * half
                v = nc.vector
                dve.wait_ge(M_used, 2 * NG * t1 + (half + 1) * NG)
                v.tensor_scalar(NR[:, :, :], MX[:, :, hs], -1.0, None, ALU.mult).then_inc(m_step, 1)
                dve.wait_ge(m_step, at + 1)
                v.tensor_copy(NMB[:, :, 0, :], NR[:, :, :]).then_inc(m_step, 1)
                dve.wait_ge(m_step, at + 2)
                v.tensor_tensor(NR[:, :, :], NR[:, :, :], NMB[:, :, 0, :], ALU.subtract).then_inc(m_step, 1)
                dve.wait_ge(m_step, at + 3)
                v.tensor_copy(NMB[:, :, 1, :], NR[:, :, :]).then_inc(m_step, 1)
                dve.wait_ge(m_step, at + 4)
                v.tensor_tensor(NMB[:, :, 2, :], NR[:, :, :], NMB[:, :, 1, :], ALU.subtract).then_inc(m_step, 1)

        def dve_use(dve, name, n, t, t2, p1):
            dve.wait_ge(mb_ready, n + 1)
            v = nc.vector
            if name[0] in "qk":
                swap = name.endswith("swap")
                x = 0 if name[0] == "q" else 1
                count = 6 * t2 + 3 * x - 2
                if x or not isinstance(t2, int) or t2 > 0:
                    dve.wait_ge(rope_step, count)
                v.tensor_tensor((TB if swap else TA)[:, :], mb[:, :], w("sin" if swap else "cos"), ALU.mult).then_inc(mb_used, 1)
            elif name == "V":
                v.tensor_copy(VA[p1][:, :, :, 0:DK], mb[:, :].rearrange("p (i h r) -> p i h r", i=QT, r=DK)).then_inc(mb_used, 1)
            elif name[0] == "G":
                g = int(name[1])
                o = mb[:, :].rearrange("p (j c r) -> p j c r", j=QT, c=4)
                v.reciprocal(rec[:, :, :], o[:, :, :, DK]).then_inc(x_done, 1)
                dve.wait_ge(x_done, 4 * t + g + 1)
                v.tensor_tensor(OTK[:, :, 32 * g:32 * g + 32].rearrange("p j (c r) -> p j c r", c=4), o[:, :, :, 0:DK],
                                rec[:, :, :].unsqueeze(3).to_broadcast([P, QT, 4, DK]), ALU.mult).then_inc(mb_used, 1)
            elif name[0] == "M":
                half = "AB".index(name[1])
                rows = mb[:, 0:T // 2].bitcast(BF16)
                if not isinstance(t, int) or t >= 0:
                    dve.wait_ge(m_loaded[half], 16 * t + 16)
                v.tensor_copy(MTS[half][:, :], rows[0:24, :]).then_inc(mb_used, 1)
            elif name == "F":
                v.tensor_copy(OF[:, :], mb[:, :]).then_inc(mb_used, 1)
            else:
                x = xT[:, ds(t * T, T)]
                v.scalar_tensor_tensor(x, mb[:, :], gate(t), x, ALU.mult, ALU.add).then_inc(mb_used, 1)

        def dve_turn(dve, c):
            def use(name):
                dve_use(dve, name, c.base + c.use[name], c.t, c.t + 2, 1 - c.p)
            for slot in SLOTS_T:
                for item in slot_items(c, slot):
                    if isinstance(item, str):
                        use(item)
                    else:
                        half, g = item
                        dve_maxima(dve, 2 * NG * (c.t + 1) + half * NG + g, c.t + 1, half, g, g + 1)
            for name in TAIL:
                use(name)

        def pool_rope(pool, b, x, used):
            q = parts[x]
            pool.wait_ge(mb_used, used)
            if x or not isinstance(b, int) or b > 0:
                pool.wait_ge(part_step, 4 * b + 2 * x)
            nc.gpsimd.tensor_tensor(QR[:, :], TA[:, :], TB[:, :], ALU.add).then_inc(rope_step, 1)
            pool.wait_ge(part_step, 4 * b + 2 * x + 1)
            nc.gpsimd.tensor_tensor(R[:, :], QR[:, :], q[:, 0, :], ALU.subtract).then_inc(rope_step, 1)
            pool.wait_ge(part_step, 4 * b + 2 * x + 2)
            nc.gpsimd.tensor_tensor(q[:, 2, :], R[:, :], q[:, 1, :], ALU.subtract).then_inc(rope_step, 1)

        def store_parts(sp, b, pb):
            sp.wait_ge(rope_step, 6 * b + 6)
            sp.wait_ge(part_step, 4 * b + 4)
            for c in range(3):
                sp.dma_start(scratch_q[pb, :, c].rearrange("a p t -> p a t"), parts[0][:, :, :]).then_inc(parts_stored, 16)
            sp.dma_start(scratch_k[pb].rearrange("c p t -> p c t"), parts[1][:, :, :]).then_inc(parts_stored, 16)

        def load_stack(sp, b, pb):
            sp.wait_ge(parts_stored, 64 * b + 64)
            sp.dma_start(qst[pb][0:MROW, :], scratch_q[pb].rearrange("a c (j h) t -> (a c j) (h t)", h=HEADS)).then_inc(st_loaded[pb], 16)
            for a in range(3):
                sp.dma_start(kst[pb][24 * a:24 * a + 24, :],
                             scratch_k[pb].rearrange("c (j h) t -> (c j) (h t)", h=HEADS)).then_inc(st_loaded[pb], 16)

        def send_maxima(sp, b, half, used, pb):
            sp.wait_ge(mb_used, used)
            rows = m_scratch[ds(48 * b + 24 * half, 24), :]
            sp.dma_start(rows, MTS[half][:, :]).then_inc(m_stored[half], 16)
            sp.wait_ge(m_stored[half], 16 * b + 16)
            sp.dma_start(qst[pb][MROW:MROW + 3, half * 8 * T:(half + 1) * 8 * T],
                           rows.rearrange("(s h) t -> s (h t)", s=3)).then_inc(m_loaded[half], 16)

        PRO = ["q", "q_swap", "k", "k_swap"]
        with nc.Block() as block:
            @block.sync
            def _(sp):
                sp.wait_ge(ones_ready, 1)
                for i in range(2):
                    sp.dma_start(kst[i][MROW:KR, :].rearrange("s (h t) -> s h t", h=HEADS),
                                 ones3[:, :].unsqueeze(1).to_broadcast([3, HEADS, T])).then_inc(ones_loaded, 16)
                store_parts(sp, 0, 0)
                load_stack(sp, 0, 0)
                store_parts(sp, 1, 1)
                load_stack(sp, 1, 1)
                send_maxima(sp, 0, 0, 10, 0)
                send_maxima(sp, 0, 1, 11, 0)

                def body(c):
                    if c.more_m:
                        send_maxima(sp, c.t + 1, 0, c.base + c.use["MA"] + 1, 1 - c.p)
                        if c.more_p:
                            store_parts(sp, c.t + 2, c.p)
                            sp.wait_ge(S_ready, UNITS_T * c.t + UNITS_T + 1)
                            load_stack(sp, c.t + 2, c.p)
                        send_maxima(sp, c.t + 1, 1, c.base + c.use["MB"] + 1, 1 - c.p)
                turns(sp, body)

            @block.tensor
            def _(pe):
                pe.wait_ge(act_init, 2)
                for n, (b, name) in enumerate([(b, name) for b in range(2) for name in PRO]):
                    pe_use(pe, name, n or None, b, 0)
                pe.wait_ge(hb_ready, 1)
                pe_use(pe, "V", 8, 0, 0)
                pe.sem_inc(PV_done, 1)
                pe.wait_ge(st_loaded[0], LOADS)
                pe_maxima(pe, 0, 0, 0, 0, NG)
                pe.wait_ge(m_step, 5)
                pe_use(pe, "MA", 9, 0, 0)
                pe_maxima(pe, NG, 0, 1, 0, NG)
                pe.wait_ge(m_step, 10)
                pe_use(pe, "MB", 10, 0, 0)
                pe.wait_ge(m_loaded[0], 16)
                pe.wait_ge(ones_loaded, 32)
                for k in range(2):
                    for u in range(5):
                        pe_scores(pe, 0, 0, k, u)
                turns(pe, lambda c: pe_turn(pe, c))

            @block.scalar
            def _(act):
                nc.scalar.copy(mqk[:, :], w("mask_qk")).then_inc(act_init, 1)
                nc.scalar.copy(mkq[:, :], w("mask_kq")).then_inc(act_init, 1)
                nc.scalar.copy(HB[:, :], hT[:, 0:T]).then_inc(hb_ready, 1)
                for b in range(2):
                    for step in range(4):
                        act_part(act, b, step)
                act.sem_inc(O_copied, 1)
                for k in range(2):
                    act_exps(act, 0, k)
                turns(act, lambda c: act_turn(act, c))

            @block.vector
            def _(dve):
                nc.vector.memset(ones3[:, :], 1.0).then_inc(ones_ready, 1)
                for n, (b, name) in enumerate([(b, name) for b in range(2) for name in PRO]):
                    dve_use(dve, name, n, -1, b, 0)
                dve.wait_ge(pool_init, 3)
                dve_use(dve, "V", 8, -1, 0, 0)
                dve_maxima(dve, 0, 0, 0, 0, NG)
                dve_use(dve, "MA", 9, -1, 0, 0)
                dve_maxima(dve, NG, 0, 1, 0, NG)
                dve_use(dve, "MB", 10, -1, 0, 0)
                turns(dve, lambda c: dve_turn(dve, c))

            @block.gpsimd
            def _(pool):
                for i in range(2):
                    nc.gpsimd.memset(VA[i][:, :, :, :], 0.0).then_inc(pool_init, 1)
                pool.wait_ge(pool_init, 2)
                for i in range(2):
                    last = nc.gpsimd.memset(VA[i][:, :, :, DK], 1.0)
                last.then_inc(pool_init, 1)
                for b in range(2):
                    for x in range(2):
                        pool_rope(pool, b, x, 4 * b + 2 * x + 2)
                def body(c):
                    if c.more_p:
                        for x, name in enumerate(("q_swap", "k_swap")):
                            pool_rope(pool, c.t + 2, x, c.base + c.use[name] + 1)
                turns(pool, body)


def group_route_stage(nc, W4, hT, identb, spread, cT, HE):
    w = lambda name: W4[:, OFF4[name][0]:OFF4[name][1]]
    with ExitStack() as ctx:
        sb = lambda name, shape, dt=F32: ctx.enter_context(nc.sbuf_tensor("g_" + name, shape, dt))
        sem = lambda name: ctx.enter_context(nc.semaphore("g_" + name))
        full = lambda name: sb(name, [P, NT, E1])
        scores, sc, masked, key, oh, chosen = (full(n) for n in ("scores", "sc", "masked", "key", "oh", "chosen"))
        pair = sb("pair", [P, NT, GROUPS, 6])
        gs, grank = sb("gs", [P, NT, GROUPS]), sb("grank", [P, NT, GROUPS])
        gt, ge = sb("gt", [P, NT, GROUPS, GROUPS]), sb("ge", [P, NT, GROUPS, GROUPS])
        best, m = sb("best", [P, NT]), sb("m", [P, NT])
        cparts = sb("cparts", [P, NT, 3, E1], BF16)
        psL = ctx.enter_context(nc.psum_tensor("g_psL", [P, NT, E1], F32))
        cps = [ctx.enter_context(nc.psum_tensor(f"g_cps{i}", [48, T], BF16)) for i in range(2)]
        logits_ready, scores_ready, step, cps_ready, cT_ready, spread_ready = (
            sem(n) for n in ("logits_ready", "scores_ready", "step", "cps_ready", "cT_ready", "spread_ready"))
        two = lambda make, name: [ctx.enter_context(make(f"g_{name}{i}", [P, T], F32)) for i in range(2)]
        psG, psU, SG, UC = two(nc.psum_tensor, "psG"), two(nc.psum_tensor, "psU"), two(nc.sbuf_tensor, "SG"), two(nc.sbuf_tensor, "UC")
        G_ready, U_ready, SG_ready, UC_ready, HE_ready = (sem(n) for n in ("G_ready", "U_ready", "SG_ready", "UC_ready", "HE_ready"))
        experts = lambda t: t[:, :].unsqueeze(2).to_broadcast([P, NT, E1])
        STEPS = 51
        with nc.Block() as block:
            @block.tensor
            def _(pe):
                for t in range(NT):
                    last = nc.tensor.matmul(psL[:, t, :], hT[:, t * P:(t + 1) * P], w("router"), start=True, stop=True)
                last.then_inc(logits_ready, 1)
                for m in range(EARLY * FC):
                    b, c = divmod(m, FC)
                    for ps, name, ready, used in ((psG, "gate_w", G_ready, SG_ready), (psU, "up_w", U_ready, UC_ready)):
                        if m >= 2:
                            pe.wait_ge(used, m - 1)
                        nc.tensor.matmul(ps[m % 2][:, :], w(name)[:, c * P:(c + 1) * P], hT[:, b * T:(b + 1) * T],
                                         start=True, stop=True).then_inc(ready, 1)
                pe.wait_ge(step, STEPS)
                for i in range(NT // 4):
                    if i >= 2:
                        pe.wait_ge(cT_ready, i - 1)
                    for k in range(4):
                        last = nc.tensor.transpose(cps[i % 2][:, k * P:(k + 1) * P],
                                                   cparts[:, 4 * i + k, :, :].rearrange("p s e -> p (s e)"), identb[:, :])
                    last.then_inc(cps_ready, 1)

            @block.scalar
            def _(act):
                nc.scalar.copy(spread[:, :], w("spread")[0:48, :]).then_inc(spread_ready, 1)
                act.wait_ge(logits_ready, 1)
                nc.scalar.activation(scores[:, :, :], psL[:, :, :], ACT.Sigmoid).then_inc(scores_ready, 1)
                for m in range(EARLY * FC):
                    act.wait_ge(G_ready, m + 1)
                    if m >= 2:
                        act.wait_ge(HE_ready, m - 1)
                    nc.scalar.activation(SG[m % 2][:, :], psG[m % 2][:, :], ACT.Silu).then_inc(SG_ready, 1)
                    act.wait_ge(U_ready, m + 1)
                    nc.scalar.copy(UC[m % 2][:, :], psU[m % 2][:, :]).then_inc(UC_ready, 1)
                for i in range(NT // 4):
                    act.wait_ge(cps_ready, i + 1)
                    nc.scalar.copy(cT[:, i * T:(i + 1) * T], cps[i % 2][:, :]).then_inc(cT_ready, 1)

            @block.vector
            def _(dve):
                done = [0]

                def then(ins):
                    done[0] += 1
                    ins.then_inc(step, 1)
                    dve.wait_ge(step, done[0])

                v = nc.vector
                dve.wait_ge(scores_ready, 1)
                then(v.tensor_tensor(sc[:, :, :], scores[:, :, :], w("e_bias").unsqueeze(1).to_broadcast([P, NT, E1]), ALU.add))
                g4 = sc[:, :, :].rearrange("p t (g e) -> p t g e", g=GROUPS)
                for at, x, y in ((0, g4[:, :, :, 0], g4[:, :, :, 1]), (1, g4[:, :, :, 2], g4[:, :, :, 3]),
                                 (2, g4[:, :, :, 0], g4[:, :, :, 2]), (3, g4[:, :, :, 1], g4[:, :, :, 3]),
                                 (4, g4[:, :, :, 0], g4[:, :, :, 3]), (5, g4[:, :, :, 1], g4[:, :, :, 2])):
                    done[0] += 1
                    v.tensor_tensor(pair[:, :, :, at], x, y, ALU.add).then_inc(step, 1)
                dve.wait_ge(step, done[0])
                then(v.tensor_reduce(gs[:, :, :], pair[:, :, :, :], AX.X, ALU.max))
                shape = [P, NT, GROUPS, GROUPS]
                own = gs[:, :, :].unsqueeze(3).to_broadcast(shape)
                other = gs[:, :, :].unsqueeze(2).to_broadcast(shape)
                lower = w("before").rearrange("p (g h) -> p g h", g=GROUPS)
                then(v.tensor_tensor(gt[:, :, :, :], other, own, ALU.is_gt))
                then(v.tensor_tensor(ge[:, :, :, :], other, own, ALU.is_equal))
                then(v.tensor_tensor(ge[:, :, :, :], ge[:, :, :, :], lower.unsqueeze(1).to_broadcast(shape), ALU.mult))
                then(v.tensor_tensor(gt[:, :, :, :], gt[:, :, :, :], ge[:, :, :, :], ALU.add))
                then(v.tensor_reduce(grank[:, :, :], gt[:, :, :, :], AX.X, ALU.add))
                then(v.tensor_scalar(grank[:, :, :], grank[:, :, :], TOP_GROUPS - 0.5, None, ALU.is_lt))
                then(v.tensor_tensor(masked[:, :, :].rearrange("p t (g e) -> p t g e", g=GROUPS), g4,
                                     grank[:, :, :].unsqueeze(3).to_broadcast([P, NT, GROUPS, E1 // GROUPS]), ALU.mult))
                for k in range(TOP_K):
                    then(v.tensor_reduce(best[:, :], masked[:, :, :], AX.X, ALU.max))
                    then(v.tensor_tensor(key[:, :, :], masked[:, :, :], experts(best), ALU.is_ge))
                    then(v.tensor_tensor(key[:, :, :], key[:, :, :], w("ramp16").unsqueeze(1).to_broadcast([P, NT, E1]), ALU.mult))
                    then(v.tensor_reduce(m[:, :], key[:, :, :], AX.X, ALU.max))
                    if k == 0:
                        then(v.tensor_tensor(chosen[:, :, :], key[:, :, :], experts(m), ALU.is_equal))
                        then(v.scalar_tensor_tensor(masked[:, :, :], chosen[:, :, :], -3e38, masked[:, :, :], ALU.mult, ALU.add))
                    else:
                        then(v.tensor_tensor(oh[:, :, :], key[:, :, :], experts(m), ALU.is_equal))
                        then(v.tensor_tensor(chosen[:, :, :], chosen[:, :, :], oh[:, :, :], ALU.add))
                        if k < TOP_K - 1:
                            then(v.scalar_tensor_tensor(masked[:, :, :], oh[:, :, :], -3e38, masked[:, :, :], ALU.mult, ALU.add))
                then(v.tensor_tensor(chosen[:, :, :], chosen[:, :, :], scores[:, :, :], ALU.mult))
                then(v.tensor_reduce(m[:, :], chosen[:, :, :], AX.X, ALU.add))
                then(v.tensor_scalar(m[:, :], m[:, :], 1e-20, None, ALU.add))
                then(v.reciprocal(m[:, :], m[:, :]))
                then(v.tensor_tensor(chosen[:, :, :], chosen[:, :, :], experts(m), ALU.mult))
                then(v.tensor_scalar(chosen[:, :, :], chosen[:, :, :], ROUTED_SCALE, None, ALU.mult))
                then(v.tensor_copy(cparts[:, :, 0, :], chosen[:, :, :]))
                then(v.tensor_tensor(chosen[:, :, :], chosen[:, :, :], cparts[:, :, 0, :], ALU.subtract))
                then(v.tensor_copy(cparts[:, :, 1, :], chosen[:, :, :]))
                then(v.tensor_tensor(cparts[:, :, 2, :], chosen[:, :, :], cparts[:, :, 1, :], ALU.subtract))

            @block.gpsimd
            def _(pool):
                for m in range(EARLY * FC):
                    pool.wait_ge(SG_ready, m + 1)
                    pool.wait_ge(UC_ready, m + 1)
                    nc.gpsimd.tensor_tensor(HE[:, m * T:(m + 1) * T], SG[m % 2][:, :], UC[m % 2][:, :], ALU.mult).then_inc(HE_ready, 1)


def group_experts_stage(nc, W4, hT, spread, cT, HE, xT, gate):
    w = lambda name: W4[:, OFF4[name][0]:OFF4[name][1]]
    with ExitStack() as ctx:
        sb = lambda name, n: [ctx.enter_context(nc.sbuf_tensor(f"f_{name}{i}", [P, T], F32)) for i in range(n)]
        ps = lambda name, n: [ctx.enter_context(nc.psum_tensor(f"f_{name}{i}", [P, T], F32)) for i in range(n)]
        sem = lambda name: ctx.enter_context(nc.semaphore("f_" + name))
        SG, HU, HC = sb("SG", 2), sb("HU", 2), sb("HC", 3)
        psG, psU, psC, psY = ps("psG", 2), ps("psU", 2), ps("psC", 2), ps("psY", 2)
        G_ready, U_ready, C_ready, D_done, SG_ready, HU_ready, HC_ready, x_done = (
            sem(n) for n in ("G_ready", "U_ready", "C_ready", "D_done", "SG_ready", "HU_ready", "HC_ready", "x_done"))
        LAG = 2

        def turns(eng, body):
            for b in range(EARLY):
                body(b, b, True)
            with eng.Fori(0, (B - EARLY) // 2) as i:
                for q in range(2):
                    body(2 * i + EARLY + q, q, False)

        with nc.Block() as block:
            @block.tensor
            def _(pe):
                pe.sem_inc(D_done, 3)
                pe.sem_inc(G_ready, EARLY * FC)
                pe.sem_inc(U_ready, EARLY * FC)

                def body(b, q, early):
                    h = hT[:, ds(b * T, T)]
                    for c in range(FC + LAG):
                        if c < FC and not early:
                            n, r = FC * b + c, (FC * q + c) % 2
                            pe.wait_ge(SG_ready, n + 1)
                            nc.tensor.matmul(psG[r][:, :], w("gate_w")[:, c * P:(c + 1) * P], h, start=True, stop=True).then_inc(G_ready, 1)
                        if c < RC:
                            pe.wait_ge(HC_ready, FC * b + c + 1)
                        if c < FC and not early:
                            pe.wait_ge(HU_ready, n + 1)
                            nc.tensor.matmul(psU[r][:, :], w("up_w")[:, c * P:(c + 1) * P], h, start=True, stop=True).then_inc(U_ready, 1)
                        if c < RC:
                            nc.tensor.matmul(psC[c % 2][:, :], spread[:, c * P:(c + 1) * P], cT[:, ds(b * T, T)], start=True, stop=True).then_inc(C_ready, 1)
                        d = c - LAG
                        if d >= 0:
                            if d == 0:
                                pe.wait_ge(x_done, b + 1)
                            pe.wait_ge(HC_ready, FC * b + d + 3)
                            nc.tensor.matmul(psY[q][:, :], w("down_w")[:, d * P:(d + 1) * P], HC[(FC * q + d) % 3][:, :],
                                             start=d == 0, stop=d == FC - 1).then_inc(D_done, 1)
                turns(pe, body)

            @block.scalar
            def _(act):
                act.sem_inc(SG_ready, 2 + EARLY * FC)

                def body(b, q, early):
                    for c in range(FC if not early else 0):
                        n, r = FC * b + c, (FC * q + c) % 2
                        act.wait_ge(G_ready, n + 1)
                        act.wait_ge(HU_ready, n + 1)
                        nc.scalar.activation(SG[r][:, :], psG[r][:, :], ACT.Silu).then_inc(SG_ready, 1)
                turns(act, body)

            @block.vector
            def _(dve):
                dve.sem_inc(HU_ready, 2 + EARLY * FC)
                dve.sem_inc(HC_ready, 2)
                dve.sem_inc(x_done, 2)

                def body(b, q, early):
                    for c in range(FC):
                        n, r = FC * b + c, (FC * q + c) % 2
                        if early:
                            hu = HE[:, n * T:(n + 1) * T]
                        else:
                            hu = HU[r][:, :]
                            dve.wait_ge(SG_ready, n + 3)
                            dve.wait_ge(U_ready, n + 1)
                            dve.wait_ge(HC_ready, n + 2)
                            nc.vector.tensor_tensor(hu, SG[r][:, :], psU[r][:, :], ALU.mult).then_inc(HU_ready, 1)
                            dve.wait_ge(HU_ready, n + 3)
                        dve.wait_ge(D_done, n + 1)
                        if c < RC:
                            dve.wait_ge(C_ready, RC * b + c + 1)
                            nc.vector.tensor_tensor(HC[(FC * q + c) % 3][:, :], hu, psC[c % 2][:, :], ALU.mult).then_inc(HC_ready, 1)
                        else:
                            nc.vector.tensor_copy(HC[(FC * q + c) % 3][:, :], hu).then_inc(HC_ready, 1)
                    dve.wait_ge(D_done, FC * b + FC + 3)
                    x = xT[:, ds(b * T, T)]
                    nc.vector.scalar_tensor_tensor(x, psY[q][:, :], gate(b), x, ALU.mult, ALU.add).then_inc(x_done, 1)
                turns(dve, body)


def output_stage(nc, W, xT, out):
    w = lambda name: W[:, OFF1[name][0]:OFF1[name][1]]
    with ExitStack() as ctx:
        ps = [ctx.enter_context(nc.psum_tensor(f"out_ps{i}", [P, 4 * P], F32)) for i in range(4)]
        tok = ctx.enter_context(nc.sbuf_tensor("out_tok", [P, NT, P], F32))
        sem = lambda name: ctx.enter_context(nc.semaphore(name))
        out_ps_ready, stored = sem("out_ps_ready"), sem("stored")
        tok_ready = [sem("tok_ready_dve"), sem("tok_ready_act")]
        o = out.rearrange("(n p) d -> p n d", p=P)
        with nc.Block() as block:
            @block.tensor
            def _(pe):
                for i in range(NT // 4):
                    if i >= 4:
                        pe.wait_ge(tok_ready[i % 2], i // 2 - 1)
                    for k in range(4):
                        t = 4 * i + k
                        last = nc.tensor.transpose(ps[i % 4][:, k * P:(k + 1) * P], xT[:, t * P:(t + 1) * P], w("ident"))
                    last.then_inc(out_ps_ready, 1)

            @block.vector
            def _(dve):
                for i in range(0, NT // 4, 2):
                    dve.wait_ge(out_ps_ready, i + 1)
                    nc.vector.tensor_copy(tok[:, 4 * i:4 * i + 4, :], ps[i % 4][:, :].rearrange("p (k d) -> p k d", k=4)).then_inc(tok_ready[0], 1)

            @block.scalar
            def _(act):
                for i in range(1, NT // 4, 2):
                    act.wait_ge(out_ps_ready, i + 1)
                    nc.scalar.copy(tok[:, 4 * i:4 * i + 4, :], ps[i % 4][:, :].rearrange("p (k d) -> p k d", k=4)).then_inc(tok_ready[1], 1)

            @block.sync
            def _(sp):
                for i in range(NT // 4):
                    sp.wait_ge(tok_ready[i % 2], i // 2 + 1)
                    sp.dma_start(o[:, 4 * i:4 * i + 4, :], tok[:, 4 * i:4 * i + 4, :]).then_inc(stored, 16)
                sp.wait_ge(stored, 16 * (NT // 4))


def program(nc, ins, out):
    with ExitStack() as ctx:
        sb = lambda name, shape, dt=F32: ctx.enter_context(nc.sbuf_tensor(name, shape, dt))
        W = sb("W", [P, WIDTH1])
        xT = sb("xT", [P, N])
        mod = sb("mod", [P, 2, 6, B])
        modv = lambda layer, j: (lambda b: mod[:, layer, j, :][:, ds(b, 1)])
        identb = sb("identb", [P, P], BF16)
        slots, results = ins["slots"], ins["results"]
        XP = sb("work", [P, (UNITS + 1) * XW])
        hT, W3, tiles, W4 = XP[:, 0:N], XP[:, N:N + WIDTH3], XP[:, N + WIDTH3:N + WIDTH3 + 5 * T], XP[:, N:N + WIDTH4]
        with ExitStack() as mamba:
            msb = lambda name, shape, dt=F32: mamba.enter_context(nc.sbuf_tensor(name, shape, dt))
            convW = msb("convW", [P, KC, NCH * P])
            negA = msb("negA", [P, NCH * NS])
            sel = msb("sel", [96, 32, P], BF16)
            setup_stage(nc, ins["x"], ins["pack1"], W, xT, mod, negA, identb)
            with nc.sbuf_tensor("hT0", [P, N], F32) as hT0:
                with ExitStack() as zeros:
                    layernorm_stage(nc, "ln0", W, xT, hT0, modv(0, 1), modv(0, 0), aside=zero_slots(nc, zeros, slots))
                mamba_inputs_stage(nc, W, hT0, XP, convW, sel)
            mamba_stage(nc, W, XP, convW, negA, sel)
        with ExitStack() as moe:
            msb = lambda name, shape, dt=F32: moe.enter_context(nc.sbuf_tensor(name, shape, dt))
            W2, cw, gather_at = msb("W2", [P, WIDTH2]), msb("cw", [P, NT]), msb("gather_at", [P, NT], U32)
            with ExitStack() as outputs:
                layernorm_stage(nc, "ln1", W, xT, hT, modv(0, 4), modv(0, 3), (W2, ins["pack2"]),
                                MambaOutputs(nc, outputs, W, XP, xT, modv(0, 2)))
            route_stage(nc, W, W2, hT, slots, cw, gather_at)
            experts_stage(nc, W, W2, slots, results, ins["w1"], ins["b1"], ins["w2"])
            with ExitStack() as combine:
                layernorm_stage(nc, "ln2", W, xT, hT, modv(1, 1), modv(1, 0), (W3, ins["pack3"]),
                                Combine(nc, combine, W, results, cw, gather_at, xT, modv(0, 5)))
        attention_stage(nc, W, W3, tiles, ins["scratch_q"], ins["scratch_k"], ins["m_scratch"], hT, xT, identb, modv(1, 2))
        with nc.sbuf_tensor("spread", [48, RC * P], BF16) as spread, nc.sbuf_tensor("cT", [48, N], BF16) as cT:
            layernorm_stage(nc, "ln3", W, xT, hT, modv(1, 4), modv(1, 3), (W4, ins["pack4"]))
            with nc.sbuf_tensor("HE", [P, EARLY * FC * T], F32) as HE:
                group_route_stage(nc, W4, hT, identb, spread, cT, HE)
                group_experts_stage(nc, W4, hT, spread, cT, HE, xT, modv(1, 5))
        output_stage(nc, W, xT, out)


def kernel(**inputs):
    import numpy as np
    import concourse.bacc as bacc
    from concourse.bass_utils import run_bass_kernel_spmd

    a = {k: np.asarray(v) for k, v in inputs.items()}
    f = np.float32
    halves = lambda m: np.ascontiguousarray(m.reshape(2, P, -1).transpose(1, 0, 2).reshape(P, -1))
    eye = np.eye(P, dtype=f)
    part = {}
    part["ident"], part["center"] = eye, eye - f(1 / P)
    part["mean"], part["eps"] = np.full((P, P), 1 / P, f), np.full((P, 1), EPS, f)
    part["pick"] = (np.arange(P)[:, None] % 32 == np.arange(32)[None, :]).astype(f)
    for n in range(2):
        part[f"c{n}"], part[f"wmod{n}"] = a[f"L{n}_c"].T, a[f"L{n}_wmod"]
    m = {k[8:]: v for k, v in a.items() if k.startswith("L0_attn_")}
    part["w_in"], part["b_in"] = m["w_in"].T, halves(m["b_in"])
    part["conv_b"], part["m_in"] = halves(m["conv_b"]), m["m_in_w"].T
    part["conv_w"] = np.broadcast_to(m["conv_w"][:, 0, :].T.reshape(1, -1), (P, KC * NCH * P))
    xp = m["xproj_w"]
    part["xproj"] = halves(np.concatenate([xp[RANK:]] * 3 + [xp[:RANK]], 0).T)
    dtw = np.zeros((P, NCH * P), f)
    dtw[96:96 + RANK] = m["dt_w"].T
    part["dt_w"], part["dt_b"] = dtw, halves(m["dt_b"])
    part["a_log"], part["d_skip"] = halves(m["A_log"]), halves(m["Dp"])
    part["m_out"], part["w_out"], part["b_out"] = halves(m["m_out_w"].T), m["w_out"].T, m["b_out"][:, None]
    m0 = {k[7:]: v for k, v in a.items() if k.startswith("L0_ffn_")}
    part["wg"] = m0["wg"]
    part["ramp"] = np.broadcast_to(np.arange(E0, 0, -1, dtype=f), (P, E0))
    part["not_first"] = np.broadcast_to(np.tile(np.arange(GT) > 0, E0 * NT // GT).astype(f), (P, E0 * NT))
    part["overflow"] = (SLOT_TILES * P + np.arange(N).reshape(NT, P).T).astype(f)
    part["tri"], part["ones"] = np.triu(np.ones((P, P), f)), np.ones((P, P), f)
    part["b2"] = np.broadcast_to(m0["b2"].reshape(1, -1), (P, E0 * P))
    wqkv = a["L1_attn_W_qkv"]
    order = np.arange(P).reshape(HEADS, DK).T.reshape(P)
    for n, name in enumerate("qk"):
        part["w" + name] = wqkv[n * P:(n + 1) * P][order].T
        part[f"w{name}_swap"] = wqkv[n * P:(n + 1) * P][order ^ 1].T
    part["wv"] = wqkv[2 * P:].T
    part["wo"] = a["L1_attn_W_o"].T
    freq = f(10000.0) ** (-np.arange(0, DK, 2, dtype=f) / f(DK))
    angle = (np.arange(T, dtype=f)[None, :] * freq[:, None]).astype(f)[order % DK // 2]
    part["cos"] = np.cos(angle)
    part["sin"] = np.sin(angle) * np.where(order % 2, 1, -1).astype(f)[:, None]
    late = np.arange(P)[None, :] > np.arange(P)[:, None]
    part["mask_qk"] = np.where(late, f(-1e30), f(0))
    part["mask_kq"] = np.ascontiguousarray(part["mask_qk"].T)
    m = {k[7:]: v for k, v in a.items() if k.startswith("L1_ffn_")}
    part["router"] = m["router_weight"].T
    part["e_bias"] = np.broadcast_to(m["e_bias"], (P, E1))
    part["ramp16"] = np.broadcast_to(np.arange(E1, 0, -1, dtype=f), (P, E1))
    part["before"] = np.broadcast_to(np.tril(np.ones((GROUPS, GROUPS), f), -1).reshape(-1), (P, GROUPS * GROUPS))
    part["spread"] = (np.arange(P)[:, None] % E1 == np.arange(RC * P)[None, :] // I1).astype(f)
    part["gate_w"] = np.concatenate([m["gate_w"].reshape(E1 * I1, P), m["sh_gate_w"]], 0).T
    part["up_w"] = np.concatenate([m["up_w"].reshape(E1 * I1, P), m["sh_up_w"]], 0).T
    down = np.concatenate([m["down_w"].transpose(0, 2, 1).reshape(E1 * I1, P), m["sh_down_w"].T], 0)
    part["down_w"] = down.reshape(FC, P, P).transpose(1, 0, 2).reshape(P, FC * P)
    arrays = {"pack4": np.concatenate([part[k] for k in PACK4], 1), "pack3": np.concatenate([part[k] for k in PACK3], 1),
              "w1": m0["W1"].reshape(E0 * P, F0), "w2": m0["W2"].reshape(E0 * F0, P),
              "b1": m0["b1"].reshape(E0, F0 // P, P).transpose(0, 2, 1).reshape(E0 * P, -1),
              "pack2": np.concatenate([part[k] for k in PACK2], 1),
              "x": a["L0_attn_x"].reshape(N, P),
              "pack1": np.concatenate([part[k] for k in PACK1], 1)}
    arrays = {k: np.ascontiguousarray(v) for k, v in arrays.items()}

    nc = bacc.Bacc("TRN2", target_bir_lowering=False, num_devices=1)
    ins = {k: nc.dram_tensor(f"in_{k}", v.shape, mybir.dt.from_np(v.dtype), kind="ExternalInput").ap() for k, v in arrays.items()}
    ins["slots"] = nc.dram_tensor("slots", (SLOT_TILES * P + N, P), F32).ap()
    ins["scratch_q"] = nc.dram_tensor("scratch_q", (2, 3, 3, P, T), BF16).ap()
    ins["scratch_k"] = nc.dram_tensor("scratch_k", (2, 3, P, T), BF16).ap()
    ins["m_scratch"] = nc.dram_tensor("m_scratch", (B * 48, T), BF16).ap()
    ins["results"] = nc.dram_tensor("results", (SLOTS, P), F32).ap()
    out = nc.dram_tensor("out", (N, P), F32, kind="ExternalOutput").ap()
    program(nc, ins, out)
    r = run_bass_kernel_spmd(nc, [{f"in_{k}": v for k, v in arrays.items()}], core_ids=[0])
    return r.results[0]["out"].reshape(B, T, P)
```
